# Optimizing a Trainium2 kernel written in Bass

```python
import numpy as np
import jax
import jax.numpy as jnp

def _softmax(x, axis=-1):
    return jax.nn.softmax(x, axis=axis)

def _gelu(x):
    return jax.nn.gelu(x, approximate=True)

def _silu(x):
    return jax.nn.silu(x)

def _sigmoid(x):
    return jax.nn.sigmoid(x)

def _layernorm(x, axis=-1, eps=1e-05):
    m = jnp.mean(x, axis=axis, keepdims=True)
    v = jnp.var(x, axis=axis, keepdims=True)
    return (x - m) / jnp.sqrt(v + eps)

def _scatter_add(tgt, idx, src, axis=0):
    return tgt.at[idx].add(src)

def _segment_sum(src, seg, n):
    return jax.ops.segment_sum(src, seg, n)
kernel_name = 'mk_flamingo_gated_d2_seqx_r4_73bf01'

def setup_inputs(seed: int=0):
    np.random.seed(seed)
    _w = jnp.asarray

    def _rec_inputs():
        import jax
        import jax.numpy as jnp
        _rk = jax.random.key(seed)
        x = -0.0003929 + 0.9999 * jax.random.normal(jax.random.fold_in(_rk, 1), (16, 128, 1024), jnp.float32)
        _lenS = 128 - jax.random.randint(jax.random.fold_in(_rk, 7), (16,), 0, max(1, 128 // 4) + 1, jnp.int32)
        _lenS2 = 128 - jax.random.randint(jax.random.fold_in(_rk, 8), (16,), 0, max(1, 128 // 4) + 1, jnp.int32)
        _ctx_4096P = jax.random.normal(jax.random.fold_in(_rk, 11), (16, 16, 1024), jnp.float32)
        _ctx_4096c = jax.random.dirichlet(jax.random.fold_in(_rk, 511), 0.3 * jnp.ones((16,), jnp.float32), (16, 128))
        _ctx_4096t = jnp.einsum('bsk,bkd->bsd', _ctx_4096c, _ctx_4096P)
        _ctx_4096t = _ctx_4096t * jax.lax.rsqrt(jnp.mean(jnp.square(_ctx_4096t)) + 1e-12) * 0.953939
        ctx_4096 = 2.81802e-05 + 1.00001 * (_ctx_4096t + 0.3 * jax.random.normal(jax.random.fold_in(_rk, 611), (16, 128, 1024), jnp.float32))
        _g = jax.random.normal(jax.random.fold_in(_rk, 9001), (2, 2), jnp.float32)
        _g = jnp.sign(_g) * jnp.maximum(jnp.abs(_g), 1.0) + (_g == 0) * 1.0
        g_xattn = _g[0]
        g_ffn = _g[1]
        return (x, ctx_4096, g_xattn, g_ffn)
    x, ctx_4096, g_xattn, g_ffn = _rec_inputs()

    def _L0_xattn_setup():
        import jax, jax.numpy as jnp
        import numpy as np
        DIM = 128
        HEADS = 8
        DIM_HEAD = 64
        HIDDEN = HEADS * DIM_HEAD
        SCALE = DIM_HEAD ** (-0.5)
        key = jax.random.key(seed)
        ks = jax.random.split(key, 9)
        b, n = (8, 1024)
        std = 1.0 / np.sqrt(DIM)
        return {'q': jax.random.normal(ks[0], (b, DIM, n), jnp.float32), 'k': jax.random.normal(ks[1], (b, DIM, n), jnp.float32), 'v': jax.random.normal(ks[2], (b, DIM, n), jnp.float32), 'Wq': jax.random.normal(ks[3], (HIDDEN, DIM), jnp.float32) * std, 'Wk': jax.random.normal(ks[4], (HIDDEN, DIM), jnp.float32) * std, 'Wv': jax.random.normal(ks[5], (HIDDEN, DIM), jnp.float32) * std, 'Wo': jax.random.normal(ks[6], (DIM, HIDDEN), jnp.float32) * (1.0 / np.sqrt(HIDDEN)), 'bo': jax.random.normal(ks[7], (DIM,), jnp.float32) * 0.01, 'g': jnp.ones((1, DIM, 1), jnp.float32)}
    _L0_xattn_all = _L0_xattn_setup()
    _L0_xattn_in = {k: v for k, v in _L0_xattn_all.items() if k in ('Wq', 'Wk', 'Wv', 'Wo', 'bo', 'g')}
    del _L0_xattn_all

    def _L0_ffn_setup():
        import jax, jax.numpy as jnp
        import numpy as np
        key = jax.random.key(seed)
        k = jax.random.split(key, 6)
        x = jax.random.normal(k[0], (4, 512, 1024), jnp.float32)
        W = jax.random.normal(k[1], (1024, 1024), jnp.float32) * 0.02
        bias = jax.random.normal(k[2], (1024,), jnp.float32) * 0.02
        A = jax.random.normal(k[3], (16, 16, 1024), jnp.float32) * 0.02
        Bf = jax.random.normal(k[4], (16, 1024, 16), jnp.float32) * 0.02
        coeffs = jax.random.uniform(k[5], (16,), jnp.float32)
        scales = jnp.full((16,), 0.5, jnp.float32)
        return {'x': x, 'W': W, 'bias': bias, 'A': A, 'Bf': Bf, 'coeffs': coeffs, 'scales': scales}
    _L0_ffn_all = _L0_ffn_setup()
    _L0_ffn_in = {k: v for k, v in _L0_ffn_all.items() if k in ('W', 'bias', 'A', 'Bf', 'coeffs', 'scales')}
    del _L0_ffn_all

    def _L1_xattn_setup():
        import jax, jax.numpy as jnp
        import numpy as np
        EPS = 1e-05

        def instance_norm(x):
            mu = jnp.mean(x, axis=-1, keepdims=True)
            var = jnp.mean((x - mu) ** 2, axis=-1, keepdims=True)
            return (x - mu) * jax.lax.rsqrt(var + EPS)
        key = jax.random.key(seed)
        ks = jax.random.split(key, 10)
        bs, qk_dim, v_dim, N, M = (4, 128, 128, 1024, 1024)
        sc_qk = 1.0 / np.sqrt(qk_dim)
        sc_v = 1.0 / np.sqrt(v_dim)
        return {'q': jax.random.normal(ks[0], (bs, qk_dim, N), jnp.float32), 'k': jax.random.normal(ks[1], (bs, qk_dim, M), jnp.float32), 'c': jax.random.normal(ks[2], (bs, v_dim, N), jnp.float32), 's': jax.random.normal(ks[3], (bs, v_dim, M), jnp.float32), 'Wq': jax.random.normal(ks[4], (qk_dim, qk_dim), jnp.float32) * sc_qk, 'bq': jax.random.normal(ks[5], (qk_dim,), jnp.float32) * 0.01, 'Wk': jax.random.normal(ks[6], (qk_dim, qk_dim), jnp.float32) * sc_qk, 'bk': jax.random.normal(ks[7], (qk_dim,), jnp.float32) * 0.01, 'Ws': jax.random.normal(ks[8], (v_dim, v_dim), jnp.float32) * sc_v, 'bs_': jax.random.normal(ks[9], (v_dim,), jnp.float32) * 0.01}
    _L1_xattn_all = _L1_xattn_setup()
    _L1_xattn_in = {k: v for k, v in _L1_xattn_all.items() if k in ('Wq', 'bq', 'Wk', 'bk', 'Ws', 'bs_')}
    del _L1_xattn_all

    def _L1_ffn_setup():
        import jax, jax.numpy as jnp
        import numpy as np
        B_, S, D_IN, D_OUT = (4, 512, 1024, 1024)
        N, RANK, ALPHA = (8, 16, 32)
        SCALE = ALPHA / RANK
        key = jax.random.key(seed)
        kx, ka, kb, kw, kbias = jax.random.split(key, 5)
        x = jax.random.normal(kx, (B_, S, D_IN), dtype=jnp.float32)
        lora_A = jax.random.normal(ka, (N, RANK, D_IN), dtype=jnp.float32) * (1.0 / np.sqrt(D_IN))
        lora_B = jax.random.normal(kb, (N, D_OUT, RANK), dtype=jnp.float32) * (1.0 / np.sqrt(RANK))
        W = jax.random.normal(kw, (D_OUT, D_IN), dtype=jnp.float32) * (1.0 / np.sqrt(D_IN))
        bias = jax.random.normal(kbias, (D_OUT,), dtype=jnp.float32) * 0.01
        lora_weights = jnp.full((N,), 1.0 / N, dtype=jnp.float32)
        return {'x': x, 'lora_A': lora_A, 'lora_B': lora_B, 'W': W, 'bias': bias, 'lora_weights': lora_weights}
    _L1_ffn_all = _L1_ffn_setup()
    _L1_ffn_in = {k: v for k, v in _L1_ffn_all.items() if k in ('lora_A', 'lora_B', 'W', 'bias', 'lora_weights')}
    del _L1_ffn_all
    return {'x': x, 'ctx_4096': ctx_4096, 'g_xattn': g_xattn, 'g_ffn': g_ffn, 'L0_xattn_Wq': _L0_xattn_in['Wq'], 'L0_xattn_Wk': _L0_xattn_in['Wk'], 'L0_xattn_Wv': _L0_xattn_in['Wv'], 'L0_xattn_Wo': _L0_xattn_in['Wo'], 'L0_xattn_bo': _L0_xattn_in['bo'], 'L0_xattn_g': _L0_xattn_in['g'], 'L0_ffn_W': _L0_ffn_in['W'], 'L0_ffn_bias': _L0_ffn_in['bias'], 'L0_ffn_A': _L0_ffn_in['A'], 'L0_ffn_Bf': _L0_ffn_in['Bf'], 'L0_ffn_coeffs': _L0_ffn_in['coeffs'], 'L0_ffn_scales': _L0_ffn_in['scales'], 'L1_xattn_Wq': _L1_xattn_in['Wq'], 'L1_xattn_bq': _L1_xattn_in['bq'], 'L1_xattn_Wk': _L1_xattn_in['Wk'], 'L1_xattn_bk': _L1_xattn_in['bk'], 'L1_xattn_Ws': _L1_xattn_in['Ws'], 'L1_xattn_bs_': _L1_xattn_in['bs_'], 'L1_ffn_lora_A': _L1_ffn_in['lora_A'], 'L1_ffn_lora_B': _L1_ffn_in['lora_B'], 'L1_ffn_W': _L1_ffn_in['W'], 'L1_ffn_bias': _L1_ffn_in['bias'], 'L1_ffn_lora_weights': _L1_ffn_in['lora_weights']}

def reference(x, ctx_4096, g_xattn, g_ffn, L0_xattn_Wq, L0_xattn_Wk, L0_xattn_Wv, L0_xattn_Wo, L0_xattn_bo, L0_xattn_g, L0_ffn_W, L0_ffn_bias, L0_ffn_A, L0_ffn_Bf, L0_ffn_coeffs, L0_ffn_scales, L1_xattn_Wq, L1_xattn_bq, L1_xattn_Wk, L1_xattn_bk, L1_xattn_Ws, L1_xattn_bs_, L1_ffn_lora_A, L1_ffn_lora_B, L1_ffn_W, L1_ffn_bias, L1_ffn_lora_weights):
    import jax
    import jax.numpy as jnp

    def _L0_xattn_ref(q, k, v, Wq, Wk, Wv, Wo, bo, g):
        import jax, jax.numpy as jnp
        import numpy as np
        DIM = 128
        HEADS = 8
        DIM_HEAD = 64
        HIDDEN = HEADS * DIM_HEAD
        SCALE = DIM_HEAD ** (-0.5)
        b = q.shape[0]
        qh = jnp.einsum('bcn,oc->bon', q, Wq).reshape(b, HEADS, DIM_HEAD, -1)
        kh = jnp.einsum('bcn,oc->bon', k, Wk).reshape(b, HEADS, DIM_HEAD, -1)
        vh = jnp.einsum('bcn,oc->bon', v, Wv).reshape(b, HEADS, DIM_HEAD, -1)
        qh = jax.nn.softmax(qh, axis=-2) * SCALE
        kh = jax.nn.softmax(kh, axis=-1)
        context = jnp.einsum('bhdn,bhen->bhde', kh, vh)
        out = jnp.einsum('bhde,bhdn->bhen', context, qh)
        out = out.reshape(b, HIDDEN, -1)
        out = jnp.einsum('bcn,oc->bon', out, Wo) + bo[None, :, None]
        norm = jnp.maximum(jnp.sqrt(jnp.sum(out * out, axis=1, keepdims=True)), 1e-12)
        return out / norm * g * np.sqrt(DIM)

    def _L0_ffn_ref(x, W, bias, A, Bf, coeffs, scales):
        import jax, jax.numpy as jnp
        import numpy as np
        out = jnp.einsum('bsd,od->bso', x, W) + bias
        xa = jnp.einsum('bsd,erd->ebsr', x, A)
        w = coeffs * scales
        upd = jnp.einsum('ebsr,eor,e->bso', xa, Bf, w)
        return out + upd

    def _L1_xattn_ref(q, k, c, s, Wq, bq, Wk, bk, Ws, bs_):
        import jax, jax.numpy as jnp
        import numpy as np
        EPS = 1e-05

        def instance_norm(x):
            mu = jnp.mean(x, axis=-1, keepdims=True)
            var = jnp.mean((x - mu) ** 2, axis=-1, keepdims=True)
            return (x - mu) * jax.lax.rsqrt(var + EPS)
        qp = jnp.einsum('oc,bcn->bon', Wq, instance_norm(q)) + bq[None, :, None]
        kp = jnp.einsum('oc,bcm->bom', Wk, instance_norm(k)) + bk[None, :, None]
        sp = jnp.einsum('oc,bcm->bom', Ws, s) + bs_[None, :, None]
        attn = jax.nn.softmax(jnp.einsum('bcn,bcm->bnm', qp, kp), axis=-1)
        mean = jnp.einsum('bnm,bvm->bvn', attn, sp)
        mean_sq = jnp.einsum('bnm,bvm->bvn', attn, sp * sp)
        std = jnp.sqrt(jax.nn.relu(mean_sq - mean * mean))
        cs = instance_norm(c) * std + mean
        return cs

    def _L1_ffn_ref(x, lora_A, lora_B, W, bias, lora_weights):
        import jax, jax.numpy as jnp
        import numpy as np
        B_, S, D_IN, D_OUT = (4, 512, 1024, 1024)
        N, RANK, ALPHA = (8, 16, 32)
        SCALE = ALPHA / RANK
        h = jnp.einsum('bsd,nrd->nbsr', x, lora_A)
        coef = (SCALE * lora_weights)[:, None, None]
        lora_out = jnp.einsum('nbsr,nor->bso', h, lora_B * coef)
        base = jnp.einsum('bsd,od->bso', x, W) + bias
        return base + lora_out
    x = x + jnp.tanh(g_xattn[0]) * _L0_xattn_ref(_layernorm(x, axis=-1), ctx_4096, ctx_4096, L0_xattn_Wq, L0_xattn_Wk, L0_xattn_Wv, L0_xattn_Wo, L0_xattn_bo, L0_xattn_g)
    x = x + jnp.tanh(g_ffn[0]) * _L0_ffn_ref(_layernorm(x, axis=-1), L0_ffn_W, L0_ffn_bias, L0_ffn_A, L0_ffn_Bf, L0_ffn_coeffs, L0_ffn_scales)
    x = x + jnp.tanh(g_xattn[1]) * _L1_xattn_ref(_layernorm(x, axis=-1), ctx_4096, ctx_4096, ctx_4096, L1_xattn_Wq, L1_xattn_bq, L1_xattn_Wk, L1_xattn_bk, L1_xattn_Ws, L1_xattn_bs_)
    x = x + jnp.tanh(g_ffn[1]) * _L1_ffn_ref(_layernorm(x, axis=-1), L1_ffn_lora_A, L1_ffn_lora_B, L1_ffn_W, L1_ffn_bias, L1_ffn_lora_weights)
    return x

_drawn_inputs = setup_inputs


def setup_inputs(seed=0):
    import zlib

    import numpy as np

    out = dict(_drawn_inputs(seed))
    spreads = {'g_ffn': (-1.0, 0.2),
     'L0_xattn_g': (1.0, 0.2),
     'L0_ffn_scales': (0.5, 0.6),
     'L1_ffn_lora_weights': (0.125, 0.592)}
    factors = {'L0_ffn_bias': 2.977,
     'L1_xattn_bq': 3.428,
     'L1_xattn_bk': 8.0,
     'L1_xattn_bs_': 8.0,
     'L1_ffn_bias': 8.0}
    for name, (base, spread) in spreads.items():
        noise = np.random.default_rng([zlib.crc32(name.encode()), seed]).standard_normal(out[name].shape)
        drawn = base * np.exp(spread * noise) if base else spread * noise
        out[name] = jnp.asarray(drawn.astype(out[name].dtype))
    for name, factor in factors.items():
        out[name] = (out[name] * factor).astype(out[name].dtype)
    return out
```

```python
from contextlib import ExitStack

import concourse.bass as bass
from concourse import mybir

P = 128
ACT = mybir.ActivationFunctionType
ALU = mybir.AluOpType
F32 = mybir.dt.float32
F32R = mybir.dt.float32r
AX_X = mybir.AxisListType.X
LN_EPS = 1e-5
HEADS, DIM_HEAD = 8, 64


def wait(eng, sem, value):
    if not (isinstance(value, int) and value <= 0):
        eng.wait_ge(sem, value)


def three_pass(eng, out, lhs, rhs, first=True, last=True):
    (lh, ll), (rh, rl) = lhs, rhs
    eng.matmul(out, lh, rh, start=first, stop=False)
    eng.matmul(out, lh, rl, start=False, stop=False)
    return eng.matmul(out, ll, rh, start=False, stop=last)


def pair(t, *idx):
    return (t[0][idx], t[1][idx])


def f32(ap):
    return ap.bitcast(F32)


def prepare(nc, ctx, env):
    x, ctx_in, g_xattn, g_ffn = env["x_dram"], env["ctx_dram"], env["g_xattn"], env["g_ffn"]
    NB, N = x.shape[0], x.shape[2]
    X, ident, tg, st, stats = env["X"], env["ident"], env["tg"], env["st"], env["stats"]
    with ExitStack() as c:
        sem = lambda n: c.enter_context(nc.semaphore(n))
        x_loaded = [sem(f"p_x_loaded{i}") for i in range(NB)]
        g_loaded, ident_zero, ident_ready = sem("p_g_loaded"), sem("p_ident_zero"), sem("p_ident_ready")
        gates_done, stats_done, aggr_done = sem("p_gates_done"), sem("p_stats_done"), sem("p_aggr_done")
        var_eps, sqrt_done, chain = sem("p_var_eps"), sem("p_sqrt_done"), sem("p_chain")
        block = c.enter_context(nc.Block())

        @block.sync
        def _(sp):
            sp.dma_start(tg[:, 0:2], g_xattn.unsqueeze(0).broadcast_to([P, 2])).then_inc(g_loaded, 16)
            sp.dma_start(tg[:, 2:4], g_ffn.unsqueeze(0).broadcast_to([P, 2])).then_inc(g_loaded, 16)
            for b in range(NB):
                sp.dma_start(X[:, b, :], x[b]).then_inc(x_loaded[b], 16)

        @block.gpsimd
        def _(pool):
            pool.memset(ident[:], 0.0).then_inc(ident_zero, 1)
            pool.wait_ge(ident_zero, 1)
            pool.affine_select(out=ident[:], in_=ident[:], compare_op=ALU.not_equal, fill=1.0, base=0,
                               pattern=[[-1, P]], channel_multiplier=1).then_inc(ident_ready, 1)

        @block.scalar
        def _(act):
            act.wait_ge(g_loaded, 32)
            act.activation(tg[:, 4:8], tg[:, 0:4], ACT.Tanh).then_inc(gates_done, 1)
            act.wait_ge(var_eps, 1)
            act.activation(st[:, 2, :], st[:, 1, :], ACT.Sqrt).then_inc(sqrt_done, 1)

        @block.vector
        def _(dve):
            for b in range(NB):
                dve.wait_ge(x_loaded[b], 16)
                row_stats(dve, X[:, b, :], stats[:, b, :], env["mv"][:, b, :], stats_done, 2 * b, aggr_done)
            dve.wait_ge(aggr_done, NB)
            scales(dve, env, env["mv"], var_eps, sqrt_done, chain)


def row_stats(dve, row, six, mv, stats_done, before, aggr_done):
    for h in range(2):
        dve.bn_stats(six[:, 6 * h:6 * h + 6], row[:, 512 * h:512 * h + 512]).then_inc(stats_done, 1)
    dve.wait_ge(stats_done, before + 2)
    dve.bn_aggr(mv, six).then_inc(aggr_done, 1)


def updated_stats(dve, env, b, S, mv):
    six, two = env["stats"][:, 0, :], env["pair"][:, 0:2]
    wait(dve, S["x_new"], b + 1)
    dve.memset(env["pair"][:, 2:3], 0.0).then_inc(S["pair_clear"], 1)
    for h in range(2):
        dve.bn_stats(six[:, 6 * h:6 * h + 6], env["X"][:, b, 512 * h:512 * h + 512]).then_inc(S["row_stats"], 1)
    wait(dve, S["row_stats"], 2 * b + 2)
    dve.memset(env["pair"][:, 3:4], 0.0).then_inc(S["pair_clear"], 1)
    dve.bn_aggr(two, six).then_inc(S["row_aggr"], 1)
    wait(dve, S["row_aggr"], b + 1)
    dve.tensor_copy(mv[:, b, :], two).then_inc(S["row_kept"], 1)


def scales(dve, env, mv, var_eps, sqrt_done, chain, at=0):
    st = env["st"]
    dve.tensor_scalar(st[:, 1, :], mv[:, :, 1], LN_EPS, None, ALU.add).then_inc(var_eps, 1)
    dve.wait_ge(sqrt_done, at + 1)
    dve.reciprocal(st[:, 0, :], st[:, 2, :]).then_inc(chain, 1)


def xattn0(nc, ctx, env):
    X, ident, st, mv, tg = env["X"], env["ident"], env["st"], env["mv"], env["tg"]
    work_ps, turn_ps, acc_ps = env["work_ps"], env["turn_ps"], env["acc_ps"]
    NB, N = X.shape[1], X.shape[2]
    NT = N // P
    HID = HEADS * DIM_HEAD
    HT = HID // P
    SCALE = DIM_HEAD ** -0.5
    with ExitStack() as c:
        sb = lambda n, s, d=F32: c.enter_context(nc.sbuf_tensor("a_" + n, s, d))
        two = lambda n, s: (sb(n + "_h", s, F32R), sb(n + "_l", s, F32R))
        sem = lambda n: env["first_sems"].append(nc.alloc_semaphore("a_" + n)) or env["first_sems"][-1]
        wq, wk, bvo = two("wq", [P, HID]), two("wk", [P, HID]), two("bvo", [P, HEADS * P])
        bo_row, gate_g = sb("bo_row", [P, P]), sb("gate_g", [P, 2])

        with ExitStack() as w:
            wsb = lambda n, s, d=F32: w.enter_context(nc.sbuf_tensor("aw_" + n, s, d))
            wsem = lambda n: sem("w_" + n)
            q_raw, k_raw = wsb("q_raw", [P, HT, P]), wsb("k_raw", [P, HT, P])
            v_raw, o_raw, o_turn = wsb("v_raw", [P, HT, P]), wsb("o_raw", [P, HID]), wsb("o_turn", [P, HT, P])
            loaded, turned, head_done = wsem("loaded"), wsem("turned"), wsem("head_done")
            tail_done, o_copied, b_done, g_scaled = wsem("tail_done"), wsem("o_copied"), wsem("b_done"), wsem("g_scaled")
            by_parity = lambda t: t.rearrange("p (j i o) -> p i j o", i=2, o=P)
            b_rows = work_ps[1][:].rearrange("p i (j o) -> p i j o", o=P)
            block = w.enter_context(nc.Block())

            @block.sync
            def _(sp):
                for dst, src in ((q_raw, env["L0_xattn_Wq"]), (k_raw, env["L0_xattn_Wk"]), (v_raw, env["L0_xattn_Wv"])):
                    sp.dma_start(dst[:], src.rearrange("(j p) c -> p j c", p=P)).then_inc(loaded, 16)
                sp.dma_start(o_raw[:], env["L0_xattn_Wo"]).then_inc(loaded, 16)
                sp.dma_start(bo_row[:], env["L0_xattn_bo"].unsqueeze(0).broadcast_to([P, P])).then_inc(loaded, 16)
                sp.dma_start(gate_g[:, 0:1], env["L0_xattn_g"].rearrange("a p b -> p (a b)")).then_inc(loaded, 16)

            @block.tensor
            def _(pe):
                pe.wait_ge(loaded, 96)
                for n, (raw, out) in enumerate(((q_raw, work_ps[0][:, 0]), (k_raw, work_ps[0][:, 1]))):
                    for j in range(HT):
                        mm = pe.transpose(out[:, j * P:(j + 1) * P], raw[:, j, :], ident[:])
                    mm.then_inc(turned, 1)
                for j in range(HT):
                    mm = pe.transpose(turn_ps[:, 0, j * P:(j + 1) * P], o_raw[:, j * P:(j + 1) * P], ident[:])
                mm.then_inc(turned, 1)
                pe.wait_ge(o_copied, 1)
                for h in range(HEADS):
                    lo = DIM_HEAD * (h % 2)
                    rows = slice(lo, lo + DIM_HEAD)
                    mm = pe.matmul(work_ps[1][:, h % 2, (h // 2) * P:(h // 2 + 1) * P], v_raw[rows, h // 2, :],
                                   o_turn[rows, h // 2, :], start=True, stop=True)
                mm.then_inc(b_done, 1)

            @block.scalar
            def _(act):
                for n, w_ in enumerate((wq, wk)):
                    act.wait_ge(turned, n + 1)
                    act.activation(w_[0][:], work_ps[0][:, n], ACT.Copy).then_inc(head_done, 1)
                act.wait_ge(b_done, 1)
                act.activation(by_parity(bvo[0][:]), b_rows, ACT.Copy).then_inc(head_done, 1)

            @block.vector
            def _(dve):
                dve.wait_ge(turned, 3)
                dve.tensor_copy(o_turn[:], turn_ps[:, 0].rearrange("p (j o) -> p j o", o=P)).then_inc(o_copied, 1)
                for n, w_ in enumerate((wq, wk)):
                    dve.wait_ge(head_done, n + 1)
                    dve.tensor_tensor(w_[1][:], work_ps[0][:, n], f32(w_[0][:]), ALU.subtract).then_inc(tail_done, 1)
                dve.wait_ge(head_done, 3)
                dve.tensor_tensor(by_parity(bvo[1][:]), b_rows, by_parity(f32(bvo[0][:])), ALU.subtract).then_inc(tail_done, 1)
                dve.scalar_tensor_tensor(gate_g[:, 1:2], gate_g[:, 0:1], float(P) ** 0.5, tg[:, 4:5],
                                         ALU.mult, ALU.mult).then_inc(g_scaled, 1)

        cx, xn = sb("cx", [P, N]), sb("xn", [P, N])
        ch, xh = two("c", [P, N]), two("x", [P, N])
        ct = two("ct", [P, NT, P])
        ke, qs = sb("ke", [P, 2, N]), sb("qs", [P, 2, 2, HID])
        kt = two("kt", [P, NT, HID])
        gt, mt = two("gt", [P, HID]), two("mt", [P, HT, P])
        mt_f = sb("mt_f", [P, HT, P])
        qt = [two(f"qt{i}", [P, 2, HT, P]) for i in range(2)]
        kmax, ksum, krec = sb("kmax", [P, HT]), sb("ksum", [P, HT]), sb("krec", [P, HT])
        qmax, qsum, qrec = (sb(n, [P, 4, 2, HEADS]) for n in ("qmax", "qsum", "qrec"))
        ot, ot2 = sb("ot", [P, NT, P]), sb("ot2", [P, NT, P])
        ss, nrm, rn = sb("ss", [P, NT]), sb("nrm", [P, NT]), sb("rn", [P, NT])
        c6, c2 = sb("c6", [P, 12]), sb("c2", [P, 2])
        cmv = env["cmv"]
        names = ("ctx_loaded ctx_stats ctx_aggr ctx_kept c_head c_tail xn_done x_head x_tail ctx_turned ct_head ct_tail k_mm k_max "
                 "k_exp k_turned kt_head kt_tail k_rec g_mm g_head g_tail m_mm m_diag m_head m_tail q_mm q_max "
                 "q_sub q_exp q_sum q_rec q_norm q_turned qt_head qt_tail out_mm o_bias o_sq o_ss o_root "
                 "o_floor o_rec o_scaled o_turned x_new row_stats row_aggr row_kept pair_clear")
        S = {n: sem(n) for n in names.split()}
        block = c.enter_context(nc.Block())

        def every_batch(eng, body, tail=None):
            body(0)
            with eng.Fori(1, NB) as b:
                body(b)
            if tail:
                tail(NB)

        @block.sync
        def _(sp):
            def body(b):
                wait(sp, S["ctx_stats"], 2 * b)
                wait(sp, S["ctx_turned"], b)
                wait(sp, S["c_tail"], b)
                sp.dma_start(cx[:], env["ctx_dram"][b]).then_inc(S["ctx_loaded"], 16)
            every_batch(sp, body)

        @block.gpsimd
        def _(pool):
            def body(b):
                wait(pool, S["c_head"], b + 1)
                pool.tensor_tensor(ch[1][:], cx[:], f32(ch[0][:]), ALU.subtract).then_inc(S["c_tail"], 1)
                wait(pool, S["x_head"], b + 1)
                pool.tensor_tensor(xh[1][:], xn[:], f32(xh[0][:]), ALU.subtract).then_inc(S["x_tail"], 1)
                for u in range(4):
                    wait(pool, S["q_rec"], 4 * b + u + 1)
                    q = qs[:, u % 2].rearrange("p t (h d) -> p (t h) d", d=DIM_HEAD)
                    r = qrec[:, u].rearrange("p t h -> p (t h)").unsqueeze(2).broadcast_to([P, 2 * HEADS, DIM_HEAD])
                    pool.tensor_tensor(q, q, r, ALU.mult).then_inc(S["q_norm"], 1)
            every_batch(pool, body)

        @block.tensor
        def _(pe):
            def turn(out, src):
                for i in range(8):
                    mm = pe.transpose(out[:, i // 4, (i % 4) * P:(i % 4 + 1) * P], src(i), ident[:])
                return mm

            def keys(j):
                for n in range(2):
                    mm = three_pass(pe, work_ps[j % 2][:, n], pair(wk, slice(None), slice(j * P, (j + 1) * P)),
                                    pair(ch, slice(None), slice(n * 512, n * 512 + 512)))
                mm.then_inc(S["k_mm"], 1)

            def turn_keys(j):
                turn(turn_ps, lambda i: ke[:, j % 2, i * P:(i + 1) * P]).then_inc(S["k_turned"], 1)

            def queries(u):
                for n in range(2):
                    t = 2 * u + n
                    mm = three_pass(pe, work_ps[u % 2][:, n], pair(xh, slice(None), slice(t * P, (t + 1) * P)),
                                    pair(wq, slice(None), slice(None)))
                mm.then_inc(S["q_mm"], 1)

            def turn_queries(b, u):
                wait(pe, S["q_norm"], 4 * b + u + 1)
                turn(turn_ps, lambda i: qs[:, u % 2, i // 4, (i % 4) * P:(i % 4 + 1) * P]).then_inc(S["q_turned"], 1)

            def out_rows(b, u):
                wait(pe, S["qt_tail"], 4 * b + u + 1)
                for n in range(2):
                    t = 2 * u + n
                    for j in range(HT):
                        mm = three_pass(pe, acc_ps[:, t // 4, (t % 4) * P:(t % 4 + 1) * P],
                                        pair(qt[u % 2], slice(None), n, j), pair(mt, slice(None), j),
                                        first=j == 0, last=j == HT - 1)
                mm.then_inc(S["out_mm"], 1)

            def turn_out(b):
                wait(pe, S["o_scaled"], b)
                turn(turn_ps, lambda i: ot2[:, i, :]).then_inc(S["o_turned"], 1)

            def body(b):
                wait(pe, S["ctx_loaded"], 16 * b + 16)
                wait(pe, S["qt_tail"], 4 * b)
                turn(turn_ps, lambda i: cx[:, i * P:(i + 1) * P]).then_inc(S["ctx_turned"], 1)
                wait(pe, S["c_tail"], b + 1)
                wait(pe, S["q_sub"], 4 * b - 1)
                keys(0)
                wait(pe, S["q_sub"], 4 * b)
                keys(1)
                wait(pe, S["k_exp"], 4 * b + 1)
                wait(pe, S["ct_tail"], b + 1)
                turn_keys(0)
                keys(2)
                wait(pe, S["k_exp"], 4 * b + 2)
                wait(pe, S["kt_tail"], 4 * b + 1)
                turn_keys(1)
                keys(3)
                wait(pe, S["kt_tail"], 4 * b + 2)
                if not (isinstance(b, int) and b == 0):
                    turn_out(b)
                wait(pe, S["k_exp"], 4 * b + 3)
                wait(pe, S["x_tail"], b + 1)
                queries(0)
                wait(pe, S["x_new"], b)
                turn_keys(2)
                wait(pe, S["k_exp"], 4 * b + 4)
                queries(1)
                wait(pe, S["kt_tail"], 4 * b + 3)
                turn_keys(3)
                wait(pe, S["q_sub"], 4 * b + 1)
                queries(2)
                wait(pe, S["kt_tail"], 4 * b + 4)
                wait(pe, S["o_bias"], b)
                for t in range(NT):
                    mm = three_pass(pe, acc_ps[:, 0], pair(ct, slice(None), t), pair(kt, slice(None), t),
                                    first=t == 0, last=t == NT - 1)
                mm.then_inc(S["g_mm"], 1)
                turn_queries(b, 0)
                wait(pe, S["q_sub"], 4 * b + 2)
                queries(3)
                wait(pe, S["g_tail"], b + 1)
                wait(pe, S["qt_tail"], 4 * b + 1)
                for j in range(HT):
                    mm = three_pass(pe, turn_ps[:, j // 2, (j % 2) * 256:(j % 2 + 1) * 256],
                                    pair(gt, slice(None), slice(j * P, (j + 1) * P)),
                                    pair(bvo, slice(None), slice(j * 256, (j + 1) * 256)))
                mm.then_inc(S["m_mm"], 1)
                wait(pe, S["m_diag"], 2 * b + 2)
                turn_queries(b, 1)
                wait(pe, S["m_tail"], b + 1)
                out_rows(b, 0)
                wait(pe, S["qt_tail"], 4 * b + 2)
                turn_queries(b, 2)
                out_rows(b, 1)
                wait(pe, S["qt_tail"], 4 * b + 3)
                turn_queries(b, 3)
                out_rows(b, 2)
                out_rows(b, 3)

            def tail(b):
                turn_out(b)
            every_batch(pe, body, tail)

        @block.scalar
        def _(act):
            def exp_keys(b, j):
                wait(act, S["k_max"], 4 * b + j + 1)
                wait(act, S["k_turned"], 4 * b + j - 1)
                act.activation(ke[:, j % 2, :], work_ps[j % 2][:].rearrange("p a n -> p (a n)"), ACT.Exp,
                               bias=kmax[:, j:j + 1], accum_out=ksum[:, j:j + 1]).then_inc(S["k_exp"], 1)

            def head_keys(b, j):
                wait(act, S["k_turned"], 4 * b + j + 1)
                wait(act, S["g_mm"], b)
                act.activation(kt[0][:, :, j * P:(j + 1) * P], turn_ps[:].rearrange("p a (t o) -> p (a t) o", o=P),
                               ACT.Copy).then_inc(S["kt_head"], 1)

            def exp_queries(b, u):
                wait(act, S["q_sub"], 4 * b + u + 1)
                q = qs[:, u % 2].rearrange("p t n -> p (t n)")
                act.activation(q, q, ACT.Exp).then_inc(S["q_exp"], 1)

            def head_queries(b, u):
                wait(act, S["q_turned"], 4 * b + u + 1)
                wait(act, S["out_mm"], 4 * b + u - 1)
                act.activation(qt[u % 2][0][:].rearrange("p t j n -> p (t j n)"),
                               turn_ps[:].rearrange("p a n -> p (a n)"), ACT.Copy).then_inc(S["qt_head"], 1)

            def out_norm(b):
                wait(act, S["o_ss"], b)
                act.activation(nrm[:], ss[:], ACT.Sqrt).then_inc(S["o_root"], 1)

            def body(b):
                wait(act, S["ctx_loaded"], 16 * b + 16)
                wait(act, S["k_mm"], 4 * b)
                act.activation(ch[0][:], cx[:], ACT.Copy).then_inc(S["c_head"], 1)
                wait(act, S["ctx_turned"], b + 1)
                wait(act, S["g_mm"], b)
                act.activation(ct[0][:].rearrange("p t c -> p (t c)"), turn_ps[:].rearrange("p a n -> p (a n)"),
                               ACT.Copy).then_inc(S["ct_head"], 1)
                if not (isinstance(b, int) and b == 0):
                    out_norm(b)
                wait(act, S["xn_done"], b + 1)
                wait(act, S["q_mm"], 4 * b)
                act.activation(xh[0][:], xn[:], ACT.Copy).then_inc(S["x_head"], 1)
                exp_keys(b, 0)
                exp_keys(b, 1)
                head_keys(b, 0)
                exp_keys(b, 2)
                head_keys(b, 1)
                exp_keys(b, 3)
                head_keys(b, 2)
                exp_queries(b, 0)
                head_keys(b, 3)
                exp_queries(b, 1)
                wait(act, S["g_mm"], b + 1)
                act.activation(gt[0][:], acc_ps[:, 0], ACT.Copy).then_inc(S["g_head"], 1)
                head_queries(b, 0)
                exp_queries(b, 2)
                wait(act, S["m_diag"], 2 * b + 2)
                wait(act, S["out_mm"], 4 * b)
                act.activation(mt[0][:], mt_f[:], ACT.Copy).then_inc(S["m_head"], 1)
                head_queries(b, 1)
                exp_queries(b, 3)
                head_queries(b, 2)
                head_queries(b, 3)

            every_batch(act, body, out_norm)

        @block.vector
        def _(dve):
            def max_keys(b, j):
                wait(dve, S["k_mm"], 4 * b + j + 1)
                wait(dve, S["k_exp"], 4 * b + j - 3)
                dve.tensor_reduce(kmax[:, j:j + 1], work_ps[j % 2][:], mybir.AxisListType.XY, ALU.max,
                                  negate=True).then_inc(S["k_max"], 1)

            def tail_keys(b, j):
                wait(dve, S["kt_head"], 4 * b + j + 1)
                dve.tensor_tensor(kt[1][:, :, j * P:(j + 1) * P], turn_ps[:].rearrange("p a (t o) -> p (a t) o", o=P),
                                  f32(kt[0][:, :, j * P:(j + 1) * P]), ALU.subtract).then_inc(S["kt_tail"], 1)

            def shift_queries(b, u):
                q = work_ps[u % 2][:].rearrange("p t (h d) -> p (t h) d", d=DIM_HEAD)
                wait(dve, S["q_mm"], 4 * b + u + 1)
                dve.tensor_reduce(qmax[:, u], q, AX_X, ALU.max).then_inc(S["q_max"], 1)
                wait(dve, S["q_max"], 4 * b + u + 1)
                wait(dve, S["q_turned"], 4 * b + u - 1)
                dve.tensor_tensor(qs[:, u % 2].rearrange("p t (h d) -> p (t h) d", d=DIM_HEAD), q,
                                  qmax[:, u].rearrange("p t h -> p (t h)").unsqueeze(2)
                                  .broadcast_to([P, 2 * HEADS, DIM_HEAD]), ALU.subtract).then_inc(S["q_sub"], 1)

            def sum_queries(b, u):
                wait(dve, S["q_exp"], 4 * b + u + 1)
                wait(dve, S["q_norm"], 4 * b + u - 3)
                dve.tensor_reduce(qsum[:, u], qs[:, u % 2].rearrange("p t (h d) -> p (t h) d", d=DIM_HEAD), AX_X,
                                  ALU.add).then_inc(S["q_sum"], 1)
                wait(dve, S["q_sum"], 4 * b + u + 1)
                dve.reciprocal(qrec[:, u], qsum[:, u]).then_inc(S["q_rec"], 1)

            def tail_queries(b, u):
                wait(dve, S["qt_head"], 4 * b + u + 1)
                dve.tensor_tensor(qt[u % 2][1][:].rearrange("p t j n -> p (t j n)"),
                                  turn_ps[:].rearrange("p a n -> p (a n)"),
                                  f32(qt[u % 2][0][:]).rearrange("p t j n -> p (t j n)"),
                                  ALU.subtract).then_inc(S["qt_tail"], 1)

            def row_lengths(b):
                wait(dve, S["o_bias"], b)
                wait(dve, S["o_turned"], b - 1)
                dve.tensor_tensor(ot2[:], ot[:], ot[:], ALU.mult).then_inc(S["o_sq"], 1)
                wait(dve, S["o_sq"], b)
                wait(dve, S["o_root"], b - 1)
                dve.tensor_reduce(ss[:], ot2[:], AX_X, ALU.add).then_inc(S["o_ss"], 1)

            def scale_rows(b):
                wait(dve, S["o_root"], b)
                dve.tensor_scalar(nrm[:], nrm[:], 1e-12, None, ALU.max).then_inc(S["o_floor"], 1)
                wait(dve, S["o_floor"], b)
                dve.reciprocal(rn[:], nrm[:]).then_inc(S["o_rec"], 1)
                wait(dve, S["o_rec"], b)
                dve.tensor_tensor(ot2[:], ot[:], rn[:].unsqueeze(2).broadcast_to([P, NT, P]),
                                  ALU.mult).then_inc(S["o_scaled"], 1)

            def update(b):
                wait(dve, S["o_turned"], b)
                wait(dve, S["xn_done"], b)
                at = X[:, b - 1, :]
                dve.scalar_tensor_tensor(at, turn_ps[:].rearrange("p a n -> p (a n)"), gate_g[:, 1:2], at,
                                         ALU.mult, ALU.add).then_inc(S["x_new"], 1)
                updated_stats(dve, env, b - 1, S, env["mv2"])

            def body(b):
                later = not (isinstance(b, int) and b == 0)
                if later:
                    row_lengths(b)
                wait(dve, S["x_tail"], b)
                dve.tensor_scalar(xn[:], X[:, b, :], mv[:, b, 0:1], st[:, 0, bass.ds(b, 1)],
                                  ALU.subtract, ALU.mult).then_inc(S["xn_done"], 1)
                wait(dve, S["ct_head"], b + 1)
                dve.tensor_tensor(ct[1][:].rearrange("p t c -> p (t c)"), turn_ps[:].rearrange("p a n -> p (a n)"),
                                  f32(ct[0][:]).rearrange("p t c -> p (t c)"), ALU.subtract).then_inc(S["ct_tail"], 1)
                max_keys(b, 0)
                if later:
                    scale_rows(b)
                max_keys(b, 1)
                wait(dve, S["ctx_loaded"], 16 * b + 16)
                for h in range(2):
                    dve.bn_stats(c6[:, 6 * h:6 * h + 6], cx[:, 512 * h:512 * h + 512]).then_inc(S["ctx_stats"], 1)
                tail_keys(b, 0)
                wait(dve, S["ctx_stats"], 2 * b + 2)
                max_keys(b, 2)
                dve.bn_aggr(c2[:], c6[:]).then_inc(S["ctx_aggr"], 1)
                tail_keys(b, 1)
                wait(dve, S["ctx_aggr"], b + 1)
                dve.tensor_copy(cmv[:, b, :], c2[:]).then_inc(S["ctx_kept"], 1)
                max_keys(b, 3)
                if later:
                    update(b)
                shift_queries(b, 0)
                tail_keys(b, 2)
                shift_queries(b, 1)
                tail_keys(b, 3)
                sum_queries(b, 0)
                wait(dve, S["k_exp"], 4 * b + 4)
                wait(dve, S["m_diag"], 2 * b)
                dve.reciprocal(krec[:], ksum[:]).then_inc(S["k_rec"], 1)
                sum_queries(b, 1)
                wait(dve, S["g_head"], b + 1)
                dve.tensor_tensor(gt[1][:], acc_ps[:, 0], f32(gt[0][:]), ALU.subtract).then_inc(S["g_tail"], 1)
                tail_queries(b, 0)
                shift_queries(b, 2)
                wait(dve, S["m_mm"], b + 1)
                wait(dve, S["k_rec"], b + 1)
                wait(dve, S["m_tail"], b)
                mps = turn_ps[:].rearrange("p a (j e) -> p (a j) e", e=256)
                for i in range(2):
                    rows = slice(64 * i, 64 * i + 64)
                    dve.scalar_tensor_tensor(mt_f[rows], mps[rows, :, i * P:(i + 1) * P], SCALE,
                                             krec[rows].unsqueeze(2).broadcast_to([64, HT, P]),
                                             ALU.mult, ALU.mult).then_inc(S["m_diag"], 1)
                sum_queries(b, 2)
                wait(dve, S["m_head"], b + 1)
                dve.tensor_tensor(mt[1][:], mt_f[:], f32(mt[0][:]), ALU.subtract).then_inc(S["m_tail"], 1)
                tail_queries(b, 1)
                shift_queries(b, 3)
                tail_queries(b, 2)
                sum_queries(b, 3)
                tail_queries(b, 3)
                wait(dve, S["out_mm"], 4 * b + 4)
                wait(dve, S["o_scaled"], b)
                dve.tensor_tensor(ot[:], acc_ps[:].rearrange("p a (t o) -> p (a t) o", o=P),
                                  bo_row[:].unsqueeze(1).broadcast_to([P, NT, P]), ALU.add).then_inc(S["o_bias"], 1)

            def tail(b):
                row_lengths(b)
                scale_rows(b)
                update(b)
            every_batch(dve, body, tail)


def paired(eng, body, count):
    body(0, 0, True, False)
    with eng.Fori(0, (count - 2) // 2) as i:
        body(2 * i + 1, 1, False, False)
        body(2 * i + 2, 0, False, False)
    body(count - 1, 1, False, True)


def ffn(nc, ctx, env, layer):
    X, ident, tg, work_ps, turn_ps = env["X"], env["ident"], env["tg"], env["work_ps"], env["turn_ps"]
    mv, mv_next = env["mv2"], env["mv"]
    NB, N = X.shape[1], X.shape[2]
    NT = N // P
    gate = tg[:, 6 + layer:7 + layer]
    if layer == 0:
        W, bias, A, B = (env["L0_ffn_" + n] for n in ("W", "bias", "A", "Bf"))
        factors = [env["L0_ffn_coeffs"], env["L0_ffn_scales"]]
    else:
        W, bias, A, B = (env["L1_ffn_" + n] for n in ("W", "bias", "lora_A", "lora_B"))
        factors = [env["L1_ffn_lora_weights"]]
    E, RANK = A.shape[0], A.shape[1]
    LORA_SCALE = 32 / RANK
    KT = E * RANK // P
    st = env["st"]
    with ExitStack() as c:
        sb = lambda n, s, d=F32: c.enter_context(nc.sbuf_tensor(f"f{layer}_" + n, s, d))
        two = lambda n, s: (sb(n + "_h", s, F32R), sb(n + "_l", s, F32R))
        sem = lambda n: c.enter_context(nc.semaphore(f"f{layer}_" + n))
        wt = two("wt", [P, NT, N])
        gbias = sb("gbias", [P, N])

        with ExitStack() as w:
            wsb = lambda n, s, d=F32: w.enter_context(nc.sbuf_tensor(f"fw{layer}_" + n, s, d))
            w_raw, a_raw, b_raw = wsb("w_raw", [P, NT, N]), wsb("a_raw", [P, KT, N]), wsb("b_raw", [P, NT, E, RANK])
            b_turn, fac = wsb("b_turn", [P, KT, N]), wsb("fac", [P, 2, E])
            names = ("w_loaded lora_loaded bias_loaded fac_done b_scaled b_turned b_copied w_mm w_head w_tail "
                     "bias_done var_eps root rstd_done")
            S = {n: w.enter_context(nc.semaphore(f"fw{layer}_" + n)) for n in names.split()}
            block = w.enter_context(nc.Block())

            @block.sync
            def _(sp):
                for n, f in enumerate(factors):
                    sp.dma_start(fac[:, n], f.unsqueeze(0).broadcast_to([P, E])).then_inc(S["lora_loaded"], 16)
                for t in range(NT):
                    sp.dma_start(b_raw[:, t], B[:, t * P:(t + 1) * P, :].rearrange("e p r -> p e r")).then_inc(
                        S["lora_loaded"], 16)
                sp.dma_start(a_raw[:], A.rearrange("e r d -> (e r) d").rearrange("(k p) d -> p k d", p=P)).then_inc(
                    S["lora_loaded"], 16)
                sp.dma_start(w_raw[:], W.rearrange("(t p) d -> p t d", p=P)).then_inc(S["w_loaded"], 16)
                sp.dma_start(gbias[:], bias.unsqueeze(0).broadcast_to([P, N])).then_inc(S["bias_loaded"], 16)

            @block.vector
            def _(dve):
                dve.tensor_scalar(st[:, 1, :], mv[:, :, 1], LN_EPS, None, ALU.add).then_inc(S["var_eps"], 1)
                dve.wait_ge(S["lora_loaded"], 16 * (len(factors) + NT + 1))
                if layer == 0:
                    dve.tensor_tensor(fac[:, 0], fac[:, 0], fac[:, 1], ALU.mult).then_inc(S["fac_done"], 1)
                else:
                    dve.tensor_scalar(fac[:, 0], fac[:, 0], LORA_SCALE, None, ALU.mult).then_inc(S["fac_done"], 1)
                dve.wait_ge(S["fac_done"], 1)
                dve.tensor_tensor(b_raw[:], b_raw[:], fac[:, 0].unsqueeze(1).unsqueeze(3).broadcast_to([P, NT, E, RANK]),
                                  ALU.mult).then_inc(S["b_scaled"], 1)
                dve.wait_ge(S["root"], 1)
                dve.reciprocal(st[:, 0, :], st[:, 2, :]).then_inc(S["rstd_done"], 1)
                dve.wait_ge(S["bias_loaded"], 16)
                dve.tensor_scalar(gbias[:], gbias[:], gate, None, ALU.mult).then_inc(S["bias_done"], 1)
                for j in range(NT):
                    dve.wait_ge(S["w_head"], j + 1)
                    dve.tensor_tensor(wt[1][:, j], work_ps[j % 2][:].rearrange("p a n -> p (a n)"), f32(wt[0][:, j]),
                                      ALU.subtract).then_inc(S["w_tail"], 1)

            @block.scalar
            def _(act):
                act.wait_ge(S["var_eps"], 1)
                act.activation(st[:, 2, :], st[:, 1, :], ACT.Sqrt).then_inc(S["root"], 1)
                for k in range(KT):
                    act.wait_ge(S["b_turned"], k + 1)
                    act.activation(b_turn[:, k], (turn_ps if k == 0 else work_ps[0])[:].rearrange("p a n -> p (a n)"),
                                   ACT.Copy).then_inc(S["b_copied"], 1)
                for j in range(NT):
                    act.wait_ge(S["w_mm"], j + 1)
                    act.activation(wt[0][:, j], work_ps[j % 2][:].rearrange("p a n -> p (a n)"),
                                   ACT.Copy).then_inc(S["w_head"], 1)

            @block.tensor
            def _(pe):
                pe.wait_ge(S["b_scaled"], 1)
                for k in range(KT):
                    for t in range(NT):
                        mm = pe.transpose((turn_ps if k == 0 else work_ps[0])[:, t // 4, (t % 4) * P:(t % 4 + 1) * P],
                                          b_raw[:, t].rearrange("p e r -> p (e r)")[:, k * P:(k + 1) * P], ident[:])
                    mm.then_inc(S["b_turned"], 1)
                pe.wait_ge(S["b_copied"], KT)
                pe.wait_ge(S["w_loaded"], 16)
                for j in range(NT):
                    cols = slice(j * P, (j + 1) * P)
                    if j >= 2:
                        pe.wait_ge(S["w_tail"], j - 1)
                    for n in range(2):
                        for k in range(KT):
                            pe.matmul(work_ps[j % 2][:, n], a_raw[:, k, cols], b_turn[:, k, n * 512:n * 512 + 512],
                                      start=k == 0, stop=False, skip_group_check=True)
                        for i in range(4):
                            mm = pe.matmul(work_ps[j % 2][:, n, i * P:(i + 1) * P], w_raw[:, 4 * n + i, cols], ident[:],
                                           start=False, stop=True, skip_group_check=True)
                    mm.then_inc(S["w_mm"], 1)

        xn, xt = sb("xn", [P, N]), [two(f"xt{i}", [P, NT, P]) for i in range(2)]
        names = "xn_done x_biased turned xt_head xt_tail mm x_new row_stats row_aggr row_kept pair_clear stored"
        S = {n: sem(n) for n in names.split()}
        block = c.enter_context(nc.Block())

        @block.tensor
        def _(pe):
            def turn(b):
                wait(pe, S["xn_done"], b + 1)
                wait(pe, S["xt_tail"], b)
                for i in range(NT):
                    mm = pe.transpose(turn_ps[:, i // 4, (i % 4) * P:(i % 4 + 1) * P], xn[:, i * P:(i + 1) * P], ident[:])
                mm.then_inc(S["turned"], 1)

            def body(b, par, first, last):
                if not last:
                    turn(b + 1)
                wait(pe, S["xt_tail"], b + 1)
                wait(pe, S["x_new"], b - 1)
                for j in range(NT):
                    for n in range(2):
                        mm = three_pass(pe, work_ps[par][:, n], pair(xt[par], slice(None), j),
                                        pair(wt, slice(None), j, slice(n * 512, n * 512 + 512)),
                                        first=j == 0, last=j == NT - 1)
                mm.then_inc(S["mm"], 1)
            turn(0)
            paired(pe, body, NB)

        @block.scalar
        def _(act):
            def body(b, par, first, last):
                wait(act, S["turned"], b + 1)
                wait(act, S["mm"], b - 1)
                act.activation(xt[par][0][:].rearrange("p t n -> p (t n)"), turn_ps[:].rearrange("p a n -> p (a n)"),
                               ACT.Copy).then_inc(S["xt_head"], 1)
            paired(act, body, NB)

        @block.vector
        def _(dve):
            def norm_x(b):
                wait(dve, S["turned"], b)
                dve.tensor_scalar(xn[:], X[:, b, :], mv[:, b, 0:1], st[:, 0, bass.ds(b, 1)],
                                  ALU.subtract, ALU.mult).then_inc(S["xn_done"], 1)
                wait(dve, S["xn_done"], b + 1)
                dve.tensor_tensor(X[:, b, :], X[:, b, :], gbias[:], ALU.add).then_inc(S["x_biased"], 1)

            def tail(b, par):
                wait(dve, S["xt_head"], b + 1)
                dve.tensor_tensor(xt[par][1][:].rearrange("p t n -> p (t n)"), turn_ps[:].rearrange("p a n -> p (a n)"),
                                  f32(xt[par][0][:]).rearrange("p t n -> p (t n)"), ALU.subtract).then_inc(S["xt_tail"], 1)

            def body(b, par, first, last):
                if not last:
                    norm_x(b + 1)
                    tail(b + 1, 1 - par)
                wait(dve, S["mm"], b + 1)
                wait(dve, S["x_biased"], b + 1)
                dve.scalar_tensor_tensor(X[:, b, :], work_ps[par][:].rearrange("p a n -> p (a n)"), gate, X[:, b, :],
                                         ALU.mult, ALU.add).then_inc(S["x_new"], 1)
                if layer == 0:
                    updated_stats(dve, env, b, S, mv_next)
            norm_x(0)
            tail(0, 0)
            paired(dve, body, NB)

        @block.sync
        def _(sp):
            if layer == 1:
                def body(b, par, first, last):
                    wait(sp, S["x_new"], b + 1)
                    sp.dma_start(env["out"][b], X[:, b, :]).then_inc(S["stored"], 16)
                paired(sp, body, NB)
                sp.wait_ge(S["stored"], 16 * NB)


def xattn1(nc, ctx, env):
    X, ident, tg = env["X"], env["ident"], env["tg"]
    work_ps, turn_ps, acc_ps = env["work_ps"], env["turn_ps"], env["acc_ps"]
    mv, mv_next, cmv = env["mv"], env["mv2"], env["cmv"]
    NB, N = X.shape[1], X.shape[2]
    NT = N // P
    VW = 2 * P + 2
    gate = tg[:, 5:6]
    with ExitStack() as c:
        sb = lambda n, s, d=F32: c.enter_context(nc.sbuf_tensor("x_" + n, s, d))
        two = lambda n, s: (sb(n + "_h", s, F32R), sb(n + "_l", s, F32R))
        sem = lambda n: c.enter_context(nc.semaphore("x_" + n))
        wts = two("wts", [P, 3, P])
        bq_bk, bs_row = sb("bq_bk", [P, 2]), sb("bs_row", [P, P])
        sc = sb("sc", [P, 8, NB])
        v = [two(f"v{i}", [P, NT, VW]) for i in range(2)]

        with ExitStack() as w:
            raw = w.enter_context(nc.sbuf_tensor("xw_raw", [P, 3, P], F32))
            edge = w.enter_context(nc.sbuf_tensor("xw_edge", [P, 2, NT, 2], F32))
            names = "loaded turned head tail edge_set edge_done chain root"
            S = {n: w.enter_context(nc.semaphore("xw_" + n)) for n in names.split()}
            block = w.enter_context(nc.Block())

            @block.sync
            def _(sp):
                for n, name in enumerate(("Wq", "Wk", "Ws")):
                    sp.dma_start(raw[:, n], env["L1_xattn_" + name]).then_inc(S["loaded"], 16)
                for n, name in enumerate(("bq", "bk")):
                    sp.dma_start(bq_bk[:, n:n + 1], env["L1_xattn_" + name].unsqueeze(1)).then_inc(S["loaded"], 16)
                sp.dma_start(bs_row[:], env["L1_xattn_bs_"].unsqueeze(0).broadcast_to([P, P])).then_inc(S["loaded"], 16)
                sp.wait_ge(S["loaded"], 96)

            @block.tensor
            def _(pe):
                pe.wait_ge(S["loaded"], 96)
                for n in range(3):
                    mm = pe.transpose(turn_ps[:, 0, n * P:(n + 1) * P], raw[:, n], ident[:])
                mm.then_inc(S["turned"], 1)

            @block.scalar
            def _(act):
                act.wait_ge(S["turned"], 1)
                act.activation(wts[0][:].rearrange("p k n -> p (k n)"), turn_ps[:, 0, 0:3 * P], ACT.Copy).then_inc(
                    S["head"], 1)
                act.wait_ge(S["chain"], 2)
                act.activation(sc[:, 4:6, :], sc[:, 2:4, :], ACT.Sqrt).then_inc(S["root"], 1)
                act.wait_ge(S["chain"], 6)
                act.activation(sc[:, 4, :], sc[:, 7, :], ACT.Sqrt).then_inc(S["root"], 1)

            @block.gpsimd
            def _(pool):
                pool.memset(edge[:, 0, :, 0:1], 1.0).then_inc(S["edge_set"], 1)
                pool.memset(edge[:, 0, :, 1:2], 0.0).then_inc(S["edge_set"], 1)
                pool.memset(edge[:, 1], 0.0).then_inc(S["edge_set"], 1)
                pool.wait_ge(S["edge_set"], 3)
                for i in range(2):
                    for k in range(2):
                        pool.tensor_copy(v[i][k][:, :, 2 * P:VW], edge[:, k]).then_inc(S["edge_done"], 1)

            @block.vector
            def _(dve):
                dve.wait_ge(S["head"], 1)
                dve.tensor_tensor(wts[1][:].rearrange("p k n -> p (k n)"), turn_ps[:, 0, 0:3 * P],
                                  f32(wts[0][:]).rearrange("p k n -> p (k n)"), ALU.subtract).then_inc(S["tail"], 1)
                step = [0]

                def link(ins):
                    step[0] += 1
                    ins.then_inc(S["chain"], 1)
                    dve.wait_ge(S["chain"], step[0])
                link(dve.tensor_scalar(sc[:, 2, :], mv[:, :, 1], LN_EPS, None, ALU.add))
                link(dve.tensor_scalar(sc[:, 3, :], cmv[:, :, 1], LN_EPS, None, ALU.add))
                dve.wait_ge(S["root"], 1)
                link(dve.reciprocal(sc[:, 0:2, :], sc[:, 4:6, :]))
                link(dve.tensor_tensor(sc[:, 6, :], sc[:, 0, :], sc[:, 0, :], ALU.mult))
                link(dve.tensor_tensor(sc[:, 6, :], sc[:, 6, :], mv[:, :, 1], ALU.mult))
                link(dve.tensor_scalar(sc[:, 7, :], sc[:, 6, :], LN_EPS, None, ALU.add))
                dve.wait_ge(S["root"], 2)
                link(dve.reciprocal(sc[:, 5, :], sc[:, 4, :]))
                link(dve.tensor_tensor(sc[:, 0, :], sc[:, 0, :], sc[:, 5, :], ALU.mult))

        cx, xn = sb("cx", [P, N]), sb("xn", [P, N])
        xq, ch, kn = two("xq", [P, N]), two("c", [P, N]), two("kn", [P, N])
        kn_f = [sb(f"kn_f{i}", [P, N]) for i in range(2)]
        qp, kp = two("qp", [P, N]), two("kp", [P, N])
        sp32, sq32 = sb("sp32", [P, NT, P]), sb("sq32", [P, NT, P])
        p, pt = sb("p", [P, 2, N]), [two(f"pt{i}", [P, NT, P]) for i in range(2)]
        smax, rcp = sb("smax", [P, NT]), sb("rcp", [P, NT])
        mean_sq = sb("mean_sq", [P, 2, NT, P])
        std, u = sb("std", [P, NT * P]), sb("u", [P, N])
        names = ("ctx_loaded c_head c_tail xn_done xq_head xq_tail knf_done kn_head kn_tail q_mm q_head q_tail "
                 "k_mm k_head k_tail sp_mm sp_done sq_done v_head v_tail s_mm s_max p_exp p_turned pt_head pt_tail "
                 "pv_mm pv_rec pv_out mean2 var floor root mean_turned std_turned x_mean u_done x_new row_stats row_aggr row_kept pair_clear")
        S = {n: sem(n) for n in names.split()}
        block = c.enter_context(nc.Block())
        flat = lambda ap: ap.rearrange("p a n -> p (a n)")

        @block.sync
        def _(sp):
            def body(b, par, first, last):
                wait(sp, S["c_tail"], b)
                wait(sp, S["knf_done"], b)
                sp.dma_start(cx[:], env["ctx_dram"][b]).then_inc(S["ctx_loaded"], 16)
            paired(sp, body, NB)

        @block.gpsimd
        def _(pool):
            def tail_of(b, t, src, name):
                wait(pool, S[name + "_head"], b + 1)
                pool.tensor_tensor(t[1][:], src, f32(t[0][:]), ALU.subtract).then_inc(S[name + "_tail"], 1)

            def variance(b):
                wait(pool, S["pv_out"], 8 * b + 8)
                wait(pool, S["std_turned"], b)
                pool.tensor_tensor(std[:], flat(mean_sq[:, 0]), flat(mean_sq[:, 0]), ALU.mult).then_inc(S["mean2"], 1)
                wait(pool, S["mean2"], b + 1)
                pool.tensor_tensor(std[:], flat(mean_sq[:, 1]), std[:], ALU.subtract).then_inc(S["var"], 1)

            def values(b, par):
                wait(pool, S["sp_done"], b + 1)
                wait(pool, S["v_tail"], 2 * b)
                pool.tensor_tensor(sq32[:], sp32[:], sp32[:], ALU.mult).then_inc(S["sq_done"], 1)
                for k, src in enumerate((sp32, sq32)):
                    wait(pool, S["v_head"], 2 * b + k + 1)
                    cols = slice(k * P, (k + 1) * P)
                    pool.tensor_tensor(v[par][1][:, :, cols], src[:], f32(v[par][0][:, :, cols]),
                                       ALU.subtract).then_inc(S["v_tail"], 1)

            def prep(b, par):
                tail_of(b, ch, cx[:], "c")
                tail_of(b, xq, xn[:], "xq")
                values(b, par)
                tail_of(b, kn, kn_f[par][:], "kn")

            def body(b, par, first, last):
                if not first:
                    variance(b - 1)
                if not last:
                    prep(b + 1, 1 - par)
            prep(0, 0)
            paired(pool, body, NB)
            variance(NB - 1)

        @block.tensor
        def _(pe):
            ALL = slice(None)

            def turn(out, src):
                for i in range(NT):
                    mm = pe.transpose(out[:, i // 4, (i % 4) * P:(i % 4 + 1) * P], src(i), ident[:])
                return mm

            def project(n, slot, src, done):
                for h in range(2):
                    mm = three_pass(pe, slot[:, h], pair(wts, ALL, n), pair(src, ALL, slice(512 * h, 512 * h + 512)))
                mm.then_inc(done, 1)

            def project_values(b):
                wait(pe, S["c_tail"], b + 1)
                for i in range(NT):
                    mm = three_pass(pe, turn_ps[:, i // 4, (i % 4) * P:(i % 4 + 1) * P],
                                    pair(ch, ALL, slice(i * P, (i + 1) * P)), pair(wts, ALL, 2))
                mm.then_inc(S["sp_mm"], 1)

            def scores(t):
                for h in range(2):
                    mm = three_pass(pe, work_ps[t % 2][:, h], pair(qp, ALL, slice(t * P, (t + 1) * P)),
                                    pair(kp, ALL, slice(512 * h, 512 * h + 512)))
                mm.then_inc(S["s_mm"], 1)

            def turn_scores(b, t):
                wait(pe, S["p_exp"], 8 * b + t + 1)
                turn(turn_ps, lambda i: p[:, t % 2, i * P:(i + 1) * P]).then_inc(S["p_turned"], 1)

            def weigh(b, t, par):
                wait(pe, S["pt_tail"], 8 * b + t + 1)
                wait(pe, S["pv_out"], 8 * b + t - 1)
                for i in range(NT):
                    mm = three_pass(pe, acc_ps[:, t % 2, 0:VW], pair(pt[t % 2], ALL, i), pair(v[par], ALL, i),
                                    first=i == 0, last=i == NT - 1)
                mm.then_inc(S["pv_mm"], 1)

            def turn_mean(b):
                wait(pe, S["pv_out"], 8 * b + 8)
                turn(turn_ps, lambda i: mean_sq[:, 0, i, :]).then_inc(S["mean_turned"], 1)

            def turn_std(b):
                wait(pe, S["root"], b + 1)
                turn(turn_ps, lambda i: std[:, i * P:(i + 1) * P]).then_inc(S["std_turned"], 1)

            def body(b, par, first, last):
                wait(pe, S["q_tail"], b + 1)
                wait(pe, S["k_tail"], b + 1)
                scores(0)
                scores(1)
                wait(pe, S["pt_tail"], 8 * b)
                if not first:
                    turn_mean(b - 1)
                    wait(pe, S["x_mean"], b)
                turn_scores(b, 0)
                for t in range(NT):
                    if t + 2 < NT:
                        wait(pe, S["p_exp"], 8 * b + t + 1)
                        scores(t + 2)
                    if t == 6 and not last:
                        wait(pe, S["p_exp"], 8 * b + 7)
                        wait(pe, S["xq_tail"], b + 2)
                        project(0, work_ps[0], xq, S["q_mm"])
                    if t == 7 and not last:
                        wait(pe, S["p_exp"], 8 * b + 8)
                        wait(pe, S["kn_tail"], b + 2)
                        project(1, work_ps[1], kn, S["k_mm"])
                    if t + 1 < NT:
                        wait(pe, S["pt_tail"], 8 * b + t + 1)
                        if t == 2 and not last:
                            wait(pe, S["sp_done"], b + 2)
                        if t == 3 and not first:
                            wait(pe, S["u_done"], b)
                        turn_scores(b, t + 1)
                    if t == 0:
                        wait(pe, S["v_tail"], 2 * b + 2)
                    weigh(b, t, par)
                    if t == 1 and not last:
                        wait(pe, S["pt_tail"], 8 * b + 3)
                        project_values(b + 1)
                    if t == 2 and not first:
                        wait(pe, S["pt_tail"], 8 * b + 4)
                        turn_std(b - 1)
            wait(pe, S["xq_tail"], 1)
            project(0, work_ps[0], xq, S["q_mm"])
            project_values(0)
            wait(pe, S["kn_tail"], 1)
            project(1, work_ps[1], kn, S["k_mm"])
            wait(pe, S["sp_done"], 1)
            paired(pe, body, NB)
            wait(pe, S["pt_tail"], 8 * NB)
            turn_mean(NB - 1)
            wait(pe, S["x_mean"], NB)
            turn_std(NB - 1)

        @block.scalar
        def _(act):
            def head(b, t, src, name, ready, last_read):
                wait(act, *ready)
                wait(act, *last_read)
                act.activation(t[0][:], src, ACT.Copy).then_inc(S[name + "_head"], 1)

            def head_c(b):
                head(b, ch, cx[:], "c", (S["ctx_loaded"], 16 * b + 16), (S["sp_mm"], b))

            def head_xq(b):
                head(b, xq, xn[:], "xq", (S["xn_done"], b + 1), (S["q_mm"], b))

            def head_kn(b, par):
                head(b, kn, kn_f[par][:], "kn", (S["knf_done"], b + 1), (S["k_mm"], b))

            def head_v(b, par, k):
                wait(act, S["sp_done" if k == 0 else "sq_done"], b + 1)
                act.activation(v[par][0][:, :, k * P:(k + 1) * P], (sp32, sq32)[k][:], ACT.Copy).then_inc(S["v_head"], 1)

            def head_proj(b, n):
                t, name = ((qp, "q"), (kp, "k"))[n]
                wait(act, S[name + "_mm"], b + 1)
                wait(act, S["s_mm"], 8 * b)
                act.activation(t[0][:], flat(work_ps[n][:]), ACT.Identity, bias=bq_bk[:, n:n + 1]).then_inc(
                    S[name + "_head"], 1)

            def exp(b, t):
                wait(act, S["s_max"], 8 * b + t + 1)
                wait(act, S["p_turned"], 8 * b + t - 1)
                act.activation(p[:, t % 2], flat(work_ps[t % 2][:]), ACT.Exp, bias=smax[:, t:t + 1]).then_inc(
                    S["p_exp"], 1)

            def head_scores(b, t):
                wait(act, S["p_turned"], 8 * b + t + 1)
                wait(act, S["pv_mm"], 8 * b + t - 1)
                act.activation(pt[t % 2][0][:].rearrange("p t n -> p (t n)"), flat(turn_ps[:]), ACT.Copy).then_inc(
                    S["pt_head"], 1)

            def root(b):
                wait(act, S["floor"], b + 1)
                act.activation(std[:], std[:], ACT.Sqrt).then_inc(S["root"], 1)

            def body(b, par, first, last):
                exp(b, 0)
                exp(b, 1)
                head_scores(b, 0)
                for t in range(NT):
                    if t + 2 < NT:
                        exp(b, t + 2)
                    if t + 1 < NT:
                        head_scores(b, t + 1)
                    if not last:
                        if t == 0:
                            head_c(b + 1)
                        if t == 1:
                            head_xq(b + 1)
                        if t == 3:
                            head_v(b + 1, 1 - par, 0)
                        if t == 4:
                            head_v(b + 1, 1 - par, 1)
                        if t == 5:
                            head_kn(b + 1, 1 - par)
                        if t == 6:
                            head_proj(b + 1, 0)
                        if t == 7:
                            head_proj(b + 1, 1)
                    if t == 1 and not first:
                        root(b - 1)
            head_c(0)
            head_xq(0)
            head_proj(0, 0)
            head_v(0, 0, 0)
            head_v(0, 0, 1)
            head_kn(0, 0)
            head_proj(0, 1)
            paired(act, body, NB)
            root(NB - 1)

        @block.vector
        def _(dve):
            def norm_x(b):
                wait(dve, S["xq_tail"], b)
                dve.tensor_scalar(xn[:], X[:, b, :], mv[:, b, 0:1], sc[:, 0, bass.ds(b, 1)],
                                  ALU.subtract, ALU.mult).then_inc(S["xn_done"], 1)

            def norm_ctx(b, par):
                wait(dve, S["ctx_loaded"], 16 * b + 16)
                wait(dve, S["kn_tail"], b - 1)
                dve.tensor_scalar(kn_f[par][:], cx[:], cmv[:, b, 0:1], sc[:, 1, bass.ds(b, 1)],
                                  ALU.subtract, ALU.mult).then_inc(S["knf_done"], 1)

            def tail_proj(b, n):
                t, name = ((qp, "q"), (kp, "k"))[n]
                wait(dve, S[name + "_head"], b + 1)
                dve.scalar_tensor_tensor(t[1][:], flat(work_ps[n][:]), bq_bk[:, n:n + 1], f32(t[0][:]),
                                         ALU.add, ALU.subtract).then_inc(S[name + "_tail"], 1)

            def add_value_bias(b):
                wait(dve, S["sp_mm"], b + 1)
                wait(dve, S["v_tail"], 2 * b)
                dve.tensor_tensor(sp32[:], turn_ps[:].rearrange("p a (t n) -> p (a t) n", n=P),
                                  bs_row[:].unsqueeze(1).broadcast_to([P, NT, P]), ALU.add).then_inc(S["sp_done"], 1)

            def max_scores(b, t):
                wait(dve, S["s_mm"], 8 * b + t + 1)
                wait(dve, S["p_exp"], 8 * b + t - 7)
                dve.tensor_reduce(smax[:, t:t + 1], work_ps[t % 2][:], mybir.AxisListType.XY, ALU.max,
                                  negate=True).then_inc(S["s_max"], 1)

            def tail_scores(b, t):
                wait(dve, S["pt_head"], 8 * b + t + 1)
                dve.tensor_tensor(pt[t % 2][1][:].rearrange("p t n -> p (t n)"), flat(turn_ps[:]),
                                  f32(pt[t % 2][0][:]).rearrange("p t n -> p (t n)"), ALU.subtract).then_inc(
                    S["pt_tail"], 1)

            def divide(b, t):
                wait(dve, S["pv_mm"], 8 * b + t + 1)
                dve.reciprocal(rcp[:, t:t + 1], acc_ps[:, t % 2, 2 * P:2 * P + 1]).then_inc(S["pv_rec"], 1)
                wait(dve, S["pv_rec"], 8 * b + t + 1)
                wait(dve, S["mean_turned"], b)
                wait(dve, S["var"], b)
                dve.tensor_scalar(mean_sq[:, :, t, :], acc_ps[:, t % 2, 0:2 * P].rearrange("p (k n) -> p k n", k=2),
                                  rcp[:, t:t + 1], None, ALU.mult).then_inc(S["pv_out"], 1)

            def add_mean(b):
                wait(dve, S["mean_turned"], b + 1)
                wait(dve, S["xn_done"], b + 1)
                dve.scalar_tensor_tensor(X[:, b, :], flat(turn_ps[:]), gate, X[:, b, :], ALU.mult, ALU.add).then_inc(
                    S["x_mean"], 1)

            def floor(b):
                wait(dve, S["var"], b + 1)
                dve.tensor_scalar(std[:], std[:], 0.0, None, ALU.max).then_inc(S["floor"], 1)

            def add_std(b, par):
                wait(dve, S["std_turned"], b + 1)
                dve.tensor_tensor(u[:], flat(turn_ps[:]), kn_f[par][:], ALU.mult).then_inc(S["u_done"], 1)
                wait(dve, S["u_done"], b + 1)
                wait(dve, S["x_mean"], b + 1)
                dve.scalar_tensor_tensor(X[:, b, :], u[:], gate, X[:, b, :], ALU.mult, ALU.add).then_inc(S["x_new"], 1)
                updated_stats(dve, env, b, S, mv_next)

            def body(b, par, first, last):
                max_scores(b, 0)
                max_scores(b, 1)
                if not first:
                    add_mean(b - 1)
                tail_scores(b, 0)
                for t in range(NT):
                    if t + 2 < NT:
                        max_scores(b, t + 2)
                    if t + 1 < NT:
                        tail_scores(b, t + 1)
                    if not last and t == 0:
                        norm_x(b + 1)
                    if not first and t == 1:
                        floor(b - 1)
                    if not last and t == 6:
                        tail_proj(b + 1, 0)
                    if not last and t == 7:
                        tail_proj(b + 1, 1)
                    divide(b, t)
                    if not last and t == 1:
                        add_value_bias(b + 1)
                    if not first and t == 2:
                        add_std(b - 1, 1 - par)
                    if not last and t == 3:
                        norm_ctx(b + 1, 1 - par)
            norm_x(0)
            norm_ctx(0, 0)
            tail_proj(0, 0)
            add_value_bias(0)
            tail_proj(0, 1)
            paired(dve, body, NB)
            add_mean(NB - 1)
            floor(NB - 1)
            add_std(NB - 1, 1)


def flamingo_gated_kernel(nc, out, **dram):
    NB, ROWS, N = dram["x"].shape
    assert ROWS == P and N == 1024
    with ExitStack() as ctx:
        sb = lambda n, s: ctx.enter_context(nc.sbuf_tensor(n, s, F32))
        env = dict(dram)
        env.update(x_dram=dram["x"], ctx_dram=dram["ctx_4096"], out=out)
        env["X"] = sb("X", [P, NB, N])
        env["ident"] = sb("ident", [P, P])
        env["tg"] = sb("tg", [P, 8])
        env["st"] = sb("st", [P, 3, NB])
        env["stats"] = sb("stats", [P, NB, 12])
        env["pair"] = sb("pair", [P, 4])
        env["mv"], env["mv2"], env["cmv"] = (sb(n, [P, NB, 2]) for n in ("mv", "mv2", "cmv"))
        env["work_ps"] = [ctx.enter_context(nc.psum_tensor(f"work{i}", [P, 2, 512], F32)) for i in range(2)]
        env["turn_ps"] = ctx.enter_context(nc.psum_tensor("turn", [P, 2, 512], F32))
        env["acc_ps"] = ctx.enter_context(nc.psum_tensor("acc", [P, 2, 512], F32))
        prepare(nc, ctx, env)
        env["first_sems"] = []
        xattn0(nc, ctx, env)
        nc.all_engine_barrier()
        nc.clear_and_free_semaphores(env["first_sems"])
        nc.all_engine_barrier()
        ffn(nc, ctx, env, 0)
        xattn1(nc, ctx, env)
        ffn(nc, ctx, env, 1)


_INS = ['x', 'ctx_4096', 'g_xattn', 'g_ffn', 'L0_xattn_Wq', 'L0_xattn_Wk', 'L0_xattn_Wv', 'L0_xattn_Wo',
        'L0_xattn_bo', 'L0_xattn_g', 'L0_ffn_W', 'L0_ffn_bias', 'L0_ffn_A', 'L0_ffn_Bf', 'L0_ffn_coeffs',
        'L0_ffn_scales', 'L1_xattn_Wq', 'L1_xattn_bq', 'L1_xattn_Wk', 'L1_xattn_bk', 'L1_xattn_Ws',
        'L1_xattn_bs_', 'L1_ffn_lora_A', 'L1_ffn_lora_B', 'L1_ffn_W', 'L1_ffn_bias', 'L1_ffn_lora_weights']
_OUT = (16, 128, 1024)


def kernel(**inputs):
    import numpy as _np
    import concourse.bacc as _bacc
    from concourse import mybir as _mybir
    from concourse.bass_utils import run_bass_kernel_spmd as _run

    nc = _bacc.Bacc("TRN2", target_bir_lowering=False, num_devices=1)
    arrays, dram = {}, {}
    for name in _INS:
        a = _np.ascontiguousarray(inputs[name])
        arrays[f"in_{name}"] = a
        dram[name] = nc.dram_tensor(f"in_{name}", a.shape, _mybir.dt.from_np(a.dtype), kind="ExternalInput").ap()
    out = nc.dram_tensor("out_0", _OUT, _mybir.dt.float32, kind="ExternalOutput").ap()
    flamingo_gated_kernel(nc, out, **dram)
    r = _run(nc, [arrays], core_ids=[0])
    return r.results[0]["out_0"]
```

```python
from contextlib import ExitStack

import concourse.bass as bass
from concourse import mybir

P = 128
ACT = mybir.ActivationFunctionType
ALU = mybir.AluOpType
F32 = mybir.dt.float32
F32R = mybir.dt.float32r
AX_X = mybir.AxisListType.X
LN_EPS = 1e-5
HEADS, DIM_HEAD = 8, 64


def wait(eng, sem, value):
    if not (isinstance(value, int) and value <= 0):
        eng.wait_ge(sem, value)


def three_pass(eng, out, lhs, rhs, first=True, last=True):
    (lh, ll), (rh, rl) = lhs, rhs
    eng.matmul(out, lh, rh, start=first, stop=False)
    eng.matmul(out, lh, rl, start=False, stop=False)
    return eng.matmul(out, ll, rh, start=False, stop=last)


def pair(t, *idx):
    return (t[0][idx], t[1][idx])


def f32(ap):
    return ap.bitcast(F32)


def prepare(nc, ctx, env):
    x, ctx_in, g_xattn, g_ffn = env["x_dram"], env["ctx_dram"], env["g_xattn"], env["g_ffn"]
    NB, N = x.shape[0], x.shape[2]
    X, ident, tg, st, stats = env["X"], env["ident"], env["tg"], env["st"], env["stats"]
    with ExitStack() as c:
        sem = lambda n: c.enter_context(nc.semaphore(n))
        x_loaded = [sem(f"p_x_loaded{i}") for i in range(NB)]
        g_loaded, ident_zero, ident_ready = sem("p_g_loaded"), sem("p_ident_zero"), sem("p_ident_ready")
        gates_done, stats_done, aggr_done = sem("p_gates_done"), sem("p_stats_done"), sem("p_aggr_done")
        var_eps, sqrt_done, chain = sem("p_var_eps"), sem("p_sqrt_done"), sem("p_chain")
        block = c.enter_context(nc.Block())

        @block.sync
        def _(sp):
            sp.dma_start(tg[:, 0:2], g_xattn.unsqueeze(0).broadcast_to([P, 2])).then_inc(g_loaded, 16)
            sp.dma_start(tg[:, 2:4], g_ffn.unsqueeze(0).broadcast_to([P, 2])).then_inc(g_loaded, 16)
            for b in range(NB):
                sp.dma_start(X[:, b, :], x[b]).then_inc(x_loaded[b], 16)

        @block.gpsimd
        def _(pool):
            pool.memset(ident[:], 0.0).then_inc(ident_zero, 1)
            pool.wait_ge(ident_zero, 1)
            pool.affine_select(out=ident[:], in_=ident[:], compare_op=ALU.not_equal, fill=1.0, base=0,
                               pattern=[[-1, P]], channel_multiplier=1).then_inc(ident_ready, 1)

        @block.scalar
        def _(act):
            act.wait_ge(g_loaded, 32)
            act.activation(tg[:, 4:8], tg[:, 0:4], ACT.Tanh).then_inc(gates_done, 1)
            act.wait_ge(var_eps, 1)
            act.activation(st[:, 2, :], st[:, 1, :], ACT.Sqrt).then_inc(sqrt_done, 1)

        @block.vector
        def _(dve):
            for b in range(NB):
                dve.wait_ge(x_loaded[b], 16)
                row_stats(dve, X[:, b, :], stats[:, b, :], env["mv"][:, b, :], stats_done, 2 * b, aggr_done)
            dve.wait_ge(aggr_done, NB)
            scales(dve, env, env["mv"], var_eps, sqrt_done, chain)


def row_stats(dve, row, six, mv, stats_done, before, aggr_done):
    for h in range(2):
        dve.bn_stats(six[:, 6 * h:6 * h + 6], row[:, 512 * h:512 * h + 512]).then_inc(stats_done, 1)
    dve.wait_ge(stats_done, before + 2)
    dve.bn_aggr(mv, six).then_inc(aggr_done, 1)


def updated_stats(dve, env, b, S, mv):
    six, two = env["stats"][:, 0, :], env["pair"][:, 0:2]
    wait(dve, S["x_new"], b + 1)
    dve.memset(env["pair"][:, 2:3], 0.0).then_inc(S["pair_clear"], 1)
    for h in range(2):
        dve.bn_stats(six[:, 6 * h:6 * h + 6], env["X"][:, b, 512 * h:512 * h + 512]).then_inc(S["row_stats"], 1)
    wait(dve, S["row_stats"], 2 * b + 2)
    dve.memset(env["pair"][:, 3:4], 0.0).then_inc(S["pair_clear"], 1)
    dve.bn_aggr(two, six).then_inc(S["row_aggr"], 1)
    wait(dve, S["row_aggr"], b + 1)
    dve.tensor_copy(mv[:, b, :], two).then_inc(S["row_kept"], 1)


def scales(dve, env, mv, var_eps, sqrt_done, chain, at=0):
    st = env["st"]
    dve.tensor_scalar(st[:, 1, :], mv[:, :, 1], LN_EPS, None, ALU.add).then_inc(var_eps, 1)
    dve.wait_ge(sqrt_done, at + 1)
    dve.reciprocal(st[:, 0, :], st[:, 2, :]).then_inc(chain, 1)


def xattn0(nc, ctx, env):
    X, ident, st, mv, tg = env["X"], env["ident"], env["st"], env["mv"], env["tg"]
    work_ps, turn_ps, acc_ps = env["work_ps"], env["turn_ps"], env["acc_ps"]
    NB, N = X.shape[1], X.shape[2]
    NT = N // P
    HID = HEADS * DIM_HEAD
    HT = HID // P
    SCALE = DIM_HEAD ** -0.5
    with ExitStack() as c:
        sb = lambda n, s, d=F32: c.enter_context(nc.sbuf_tensor("a_" + n, s, d))
        two = lambda n, s: (sb(n + "_h", s, F32R), sb(n + "_l", s, F32R))
        sem = lambda n: env["first_sems"].append(nc.alloc_semaphore("a_" + n)) or env["first_sems"][-1]
        wq, wk, bvo = two("wq", [P, HID]), two("wk", [P, HID]), sb("bvo", [P, HEADS * P])
        bo_row, gate_g = sb("bo_row", [P, P]), sb("gate_g", [P, 2])

        with ExitStack() as w:
            wsb = lambda n, s, d=F32: w.enter_context(nc.sbuf_tensor("aw_" + n, s, d))
            wsem = lambda n: sem("w_" + n)
            q_raw, k_raw = wsb("q_raw", [P, HT, P]), wsb("k_raw", [P, HT, P])
            v_raw, o_raw, o_turn = wsb("v_raw", [P, HT, P]), wsb("o_raw", [P, HID]), wsb("o_turn", [P, HT, P])
            loaded, turned, head_done = wsem("loaded"), wsem("turned"), wsem("head_done")
            tail_done, o_copied, b_done, g_scaled = wsem("tail_done"), wsem("o_copied"), wsem("b_done"), wsem("g_scaled")
            by_parity = lambda t: t.rearrange("p (j i o) -> p i j o", i=2, o=P)
            b_rows = work_ps[1][:].rearrange("p i (j o) -> p i j o", o=P)
            block = w.enter_context(nc.Block())

            @block.sync
            def _(sp):
                for dst, src in ((q_raw, env["L0_xattn_Wq"]), (k_raw, env["L0_xattn_Wk"]), (v_raw, env["L0_xattn_Wv"])):
                    sp.dma_start(dst[:], src.rearrange("(j p) c -> p j c", p=P)).then_inc(loaded, 16)
                sp.dma_start(o_raw[:], env["L0_xattn_Wo"]).then_inc(loaded, 16)
                sp.dma_start(bo_row[:], env["L0_xattn_bo"].unsqueeze(0).broadcast_to([P, P])).then_inc(loaded, 16)
                sp.dma_start(gate_g[:, 0:1], env["L0_xattn_g"].rearrange("a p b -> p (a b)")).then_inc(loaded, 16)

            @block.tensor
            def _(pe):
                pe.wait_ge(loaded, 96)
                for n, (raw, out) in enumerate(((q_raw, work_ps[0][:, 0]), (k_raw, work_ps[0][:, 1]))):
                    for j in range(HT):
                        mm = pe.transpose(out[:, j * P:(j + 1) * P], raw[:, j, :], ident[:])
                    mm.then_inc(turned, 1)
                for j in range(HT):
                    mm = pe.transpose(turn_ps[:, 0, j * P:(j + 1) * P], o_raw[:, j * P:(j + 1) * P], ident[:])
                mm.then_inc(turned, 1)
                pe.wait_ge(o_copied, 1)
                for h in range(HEADS):
                    lo = DIM_HEAD * (h % 2)
                    rows = slice(lo, lo + DIM_HEAD)
                    mm = pe.matmul(work_ps[1][:, h % 2, (h // 2) * P:(h // 2 + 1) * P], v_raw[rows, h // 2, :],
                                   o_turn[rows, h // 2, :], start=True, stop=True)
                mm.then_inc(b_done, 1)

            @block.scalar
            def _(act):
                for n, w_ in enumerate((wq, wk)):
                    act.wait_ge(turned, n + 1)
                    act.activation(w_[0][:], work_ps[0][:, n], ACT.Copy).then_inc(head_done, 1)
                act.wait_ge(b_done, 1)
                act.activation(by_parity(bvo[:]), b_rows, ACT.Copy).then_inc(head_done, 1)

            @block.vector
            def _(dve):
                dve.wait_ge(turned, 3)
                dve.tensor_copy(o_turn[:], turn_ps[:, 0].rearrange("p (j o) -> p j o", o=P)).then_inc(o_copied, 1)
                for n, w_ in enumerate((wq, wk)):
                    dve.wait_ge(head_done, n + 1)
                    dve.tensor_tensor(w_[1][:], work_ps[0][:, n], f32(w_[0][:]), ALU.subtract).then_inc(tail_done, 1)
                dve.scalar_tensor_tensor(gate_g[:, 1:2], gate_g[:, 0:1], float(P) ** 0.5, tg[:, 4:5],
                                         ALU.mult, ALU.mult).then_inc(g_scaled, 1)

        cx, xn = sb("cx", [P, N]), sb("xn", [P, N])
        ch, xh = two("c", [P, N]), two("x", [P, N])
        ct = sb("ct", [P, NT, P])
        ke, qs = sb("ke", [P, 2, N]), sb("qs", [P, 2, 2, HID])
        kt, qt = sb("kt", [P, NT, HID]), sb("qt", [P, 4, 2, HT, P])
        gt, mt = sb("gt", [P, HID]), sb("mt", [P, HT, P])
        kmax, ksum, krec = sb("kmax", [P, HT]), sb("ksum", [P, HT]), sb("krec", [P, HT])
        qmax, qsum, qrec = (sb(n, [P, 4, 2, HEADS]) for n in ("qmax", "qsum", "qrec"))
        ot, osq, ot2 = sb("ot", [P, NT, P]), sb("osq", [P, NT, P]), sb("ot2", [P, NT, P])
        ss, nrm, rn = sb("ss", [P, NT]), sb("nrm", [P, NT]), sb("rn", [P, NT])
        c6, c2 = sb("c6", [P, 12]), sb("c2", [P, 2])
        cmv = env["cmv"]
        names = ("ctx_loaded ctx_stats ctx_aggr ctx_kept c_head c_tail xn_done x_head x_tail ctx_turned ct_copied "
                 "k_mm k_max k_exp k_turned kt_copied k_rec g_mm g_copied m_mm m_diag q_mm q_max q_sub q_exp q_sum "
                 "q_rec q_norm q_turned qt_copied out_mm o_bias o_sq o_ss o_root o_floor o_rec o_scaled o_turned "
                 "warmed x_new row_stats row_aggr row_kept pair_clear")
        S = {n: sem(n) for n in names.split()}
        block = c.enter_context(nc.Block())
        flat = lambda ap: ap.rearrange("p a n -> p (a n)")

        def skewed(eng, body, tail=None):
            body(0, False, False, False)
            body(1, True, False, False)
            with eng.Fori(2, NB - 1) as b:
                body(b, True, True, False)
            body(NB - 1, True, True, True)
            if tail:
                tail(NB)

        @block.sync
        def _(sp):
            def body(b, prev, prev2, last):
                wait(sp, S["ctx_stats"], 2 * b)
                wait(sp, S["ctx_turned"], b)
                wait(sp, S["c_tail"], b)
                sp.dma_start(cx[:], env["ctx_dram"][b]).then_inc(S["ctx_loaded"], 16)
            skewed(sp, body)

        @block.gpsimd
        def _(pool):
            def tail_of(b, t, src, name):
                wait(pool, S[name + "_head"], b + 1)
                pool.tensor_tensor(t[1][:], src, f32(t[0][:]), ALU.subtract).then_inc(S[name + "_tail"], 1)

            def divide_queries(b, u):
                wait(pool, S["q_rec"], 4 * b + u + 1)
                q = qs[:, u % 2].rearrange("p t (h d) -> p (t h) d", d=DIM_HEAD)
                r = qrec[:, u].rearrange("p t h -> p (t h)").unsqueeze(2).broadcast_to([P, 2 * HEADS, DIM_HEAD])
                pool.tensor_tensor(q, q, r, ALU.mult).then_inc(S["q_norm"], 1)

            def square(b):
                wait(pool, S["o_bias"], b + 1)
                wait(pool, S["o_ss"], b)
                pool.tensor_tensor(osq[:], ot[:], ot[:], ALU.mult).then_inc(S["o_sq"], 1)

            def scale_rows(b):
                wait(pool, S["o_rec"], b + 1)
                wait(pool, S["o_turned"], b)
                pool.tensor_tensor(ot2[:], ot[:], rn[:].unsqueeze(2).broadcast_to([P, NT, P]),
                                   ALU.mult).then_inc(S["o_scaled"], 1)

            def body(b, prev, prev2, last):
                if prev2:
                    scale_rows(b - 2)
                for u in range(4):
                    divide_queries(b, u)
                if not last:
                    tail_of(b + 1, ch, cx[:], "c")
                if prev:
                    square(b - 1)
                if not last:
                    tail_of(b + 1, xh, xn[:], "x")

            def tail(b):
                scale_rows(b - 2)
                square(b - 1)
                scale_rows(b - 1)
            tail_of(0, ch, cx[:], "c")
            tail_of(0, xh, xn[:], "x")
            skewed(pool, body, tail)

        @block.tensor
        def _(pe):
            def turn(out, src):
                for i in range(8):
                    mm = pe.transpose(out[:, i // 4, (i % 4) * P:(i % 4 + 1) * P], src(i), ident[:])
                return mm

            def keys(b, j):
                wait(pe, S["k_exp"], 4 * b + j)
                for n in range(2):
                    mm = three_pass(pe, work_ps[0][:, n], pair(wk, slice(None), slice(j * P, (j + 1) * P)),
                                    pair(ch, slice(None), slice(n * 512, n * 512 + 512)))
                mm.then_inc(S["k_mm"], 1)

            def turn_keys(b, j):
                wait(pe, S["k_exp"], 4 * b + j + 1)
                turn(turn_ps, lambda i: ke[:, j % 2, i * P:(i + 1) * P]).then_inc(S["k_turned"], 1)

            def queries(b, u):
                wait(pe, S["q_sub"], 4 * b + u)
                for n in range(2):
                    t = 2 * u + n
                    mm = three_pass(pe, work_ps[1][:, n], pair(xh, slice(None), slice(t * P, (t + 1) * P)),
                                    pair(wq, slice(None), slice(None)))
                mm.then_inc(S["q_mm"], 1)

            def turn_queries(b, u):
                wait(pe, S["q_norm"], 4 * b + u + 1)
                turn(turn_ps, lambda i: qs[:, u % 2, i // 4, (i % 4) * P:(i % 4 + 1) * P]).then_inc(S["q_turned"], 1)

            def out_rows(b, t):
                for j in range(HT):
                    mm = pe.matmul(acc_ps[:, t // 4, (t % 4) * P:(t % 4 + 1) * P], qt[:, t // 2, t % 2, j, :],
                                   mt[:, j, :], start=j == 0, stop=j == HT - 1)
                if t % 2:
                    mm.then_inc(S["out_mm"], 1)

            def turn_out(b):
                wait(pe, S["o_scaled"], b + 1)
                turn(turn_ps, lambda i: ot2[:, i, :]).then_inc(S["o_turned"], 1)

            def body(b, prev, prev2, last):
                for i in range(4):
                    if i == 0:
                        wait(pe, S["qt_copied"], 4 * b)
                        wait(pe, S["ctx_loaded"], 16 * b + 16)
                        turn(turn_ps, lambda i: cx[:, i * P:(i + 1) * P]).then_inc(S["ctx_turned"], 1)
                        wait(pe, S["x_tail"], b + 1)
                        queries(b, 0)
                        wait(pe, S["c_tail"], b + 1)
                        wait(pe, S["m_diag"], 2 * b)
                    keys(b, i)
                    if i == 1 and prev2:
                        wait(pe, S["kt_copied"], 4 * b + 1)
                        turn_out(b - 2)
                    if i >= 1:
                        queries(b, i)
                    if prev:
                        if i == 0:
                            wait(pe, S["g_copied"], b)
                        out_rows(b - 1, 2 * i)
                    if i == 0:
                        wait(pe, S["ct_copied"], b + 1)
                    if i == 1:
                        wait(pe, S["kt_copied"], 4 * b + 1)
                        wait(pe, S["x_new"], b - 1)
                    if i >= 2:
                        wait(pe, S["qt_copied"], 4 * b + i - 1)
                    turn_keys(b, i)
                    if prev:
                        out_rows(b - 1, 2 * i + 1)
                    if i >= 1:
                        wait(pe, S["kt_copied"], 4 * b + i + 1)
                        turn_queries(b, i - 1)
                wait(pe, S["kt_copied"], 4 * b + 4)
                wait(pe, S["o_bias"], b)
                for t in range(NT):
                    mm = pe.matmul(acc_ps[:, 0], ct[:, t, :], kt[:, t, :], start=t == 0, stop=t == NT - 1)
                mm.then_inc(S["g_mm"], 1)
                wait(pe, S["qt_copied"], 4 * b + 3)
                turn_queries(b, 3)
                wait(pe, S["g_copied"], b + 1)
                wait(pe, S["k_exp"], 4 * b + 4)
                for j in range(HT):
                    mm = pe.matmul(work_ps[0][:, j // 2, (j % 2) * 256:(j % 2 + 1) * 256], gt[:, j * P:(j + 1) * P],
                                   bvo[:, j * 256:(j + 1) * 256], start=True, stop=True)
                mm.then_inc(S["m_mm"], 1)

            def tail(b):
                wait(pe, S["m_diag"], 2 * b)
                wait(pe, S["qt_copied"], 4 * b)
                turn_out(b - 2)
                for t in range(NT):
                    out_rows(b - 1, t)
                wait(pe, S["x_new"], b - 1)
                turn_out(b - 1)
            skewed(pe, body, tail)

        @block.scalar
        def _(act):
            def head_of(b, t, src, name, ready, read):
                wait(act, *ready)
                wait(act, *read)
                act.activation(t[0][:], src, ACT.Copy).then_inc(S[name + "_head"], 1)

            def heads(b):
                head_of(b, ch, cx[:], "c", (S["ctx_loaded"], 16 * b + 16), (S["k_mm"], 4 * b))
                head_of(b, xh, xn[:], "x", (S["xn_done"], b + 1), (S["q_mm"], 4 * b))

            def exp_keys(b, j):
                wait(act, S["k_max"], 4 * b + j + 1)
                wait(act, S["k_turned"], 4 * b + j - 1)
                act.activation(ke[:, j % 2, :], flat(work_ps[0][:]), ACT.Exp,
                               bias=kmax[:, j:j + 1], accum_out=ksum[:, j:j + 1]).then_inc(S["k_exp"], 1)

            def copy_keys(b, j):
                wait(act, S["k_turned"], 4 * b + j + 1)
                wait(act, S["g_mm"], b)
                act.activation(kt[:, :, j * P:(j + 1) * P], turn_ps[:].rearrange("p a (t o) -> p (a t) o", o=P),
                               ACT.Copy).then_inc(S["kt_copied"], 1)

            def exp_queries(b, u):
                wait(act, S["q_sub"], 4 * b + u + 1)
                q = flat(qs[:, u % 2])
                act.activation(q, q, ACT.Exp).then_inc(S["q_exp"], 1)

            def copy_queries(b, u):
                wait(act, S["q_turned"], 4 * b + u + 1)
                wait(act, S["out_mm"], 4 * b + u - 3)
                act.activation(qt[:, u].rearrange("p t j n -> p (t j n)"), flat(turn_ps[:]),
                               ACT.Copy).then_inc(S["qt_copied"], 1)

            def root(b):
                wait(act, S["o_ss"], b + 1)
                act.activation(nrm[:], ss[:], ACT.Sqrt).then_inc(S["o_root"], 1)
                wait(act, S["warmed"], b)
                act.activation(env["warm"][:], ident[:, 0:1], ACT.Exp).then_inc(S["warmed"], 1)

            def body(b, prev, prev2, last):
                wait(act, S["ctx_turned"], b + 1)
                wait(act, S["g_mm"], b)
                act.activation(ct[:].rearrange("p t c -> p (t c)"), flat(turn_ps[:]),
                               ACT.Copy).then_inc(S["ct_copied"], 1)
                for i in range(4):
                    exp_keys(b, i)
                    copy_keys(b, i)
                    exp_queries(b, i)
                    if i >= 1:
                        copy_queries(b, i - 1)
                if not last:
                    heads(b + 1)
                wait(act, S["g_mm"], b + 1)
                act.activation(gt[:], acc_ps[:, 0], ACT.Copy).then_inc(S["g_copied"], 1)
                copy_queries(b, 3)
                if prev:
                    root(b - 1)
            heads(0)
            skewed(act, body, lambda b: root(b - 1))

        @block.vector
        def _(dve):
            def norm_x(b):
                wait(dve, S["x_tail"], b)
                dve.tensor_scalar(xn[:], X[:, b, :], mv[:, b, 0:1], st[:, 0, bass.ds(b, 1)],
                                  ALU.subtract, ALU.mult).then_inc(S["xn_done"], 1)

            def max_keys(b, j):
                wait(dve, S["k_mm"], 4 * b + j + 1)
                wait(dve, S["k_exp"], 4 * b + j - 3)
                dve.tensor_reduce(kmax[:, j:j + 1], work_ps[0][:], mybir.AxisListType.XY, ALU.max,
                                  negate=True).then_inc(S["k_max"], 1)

            def max_queries(b, u):
                wait(dve, S["q_mm"], 4 * b + u + 1)
                dve.tensor_reduce(qmax[:, u], work_ps[1][:].rearrange("p t (h d) -> p (t h) d", d=DIM_HEAD),
                                  AX_X, ALU.max).then_inc(S["q_max"], 1)

            def shift_queries(b, u):
                q = work_ps[1][:].rearrange("p t (h d) -> p (t h) d", d=DIM_HEAD)
                wait(dve, S["q_max"], 4 * b + u + 1)
                wait(dve, S["q_turned"], 4 * b + u - 1)
                dve.tensor_tensor(qs[:, u % 2].rearrange("p t (h d) -> p (t h) d", d=DIM_HEAD), q,
                                  qmax[:, u].rearrange("p t h -> p (t h)").unsqueeze(2)
                                  .broadcast_to([P, 2 * HEADS, DIM_HEAD]), ALU.subtract).then_inc(S["q_sub"], 1)

            def sum_queries(b, u):
                wait(dve, S["q_exp"], 4 * b + u + 1)
                wait(dve, S["q_norm"], 4 * b + u - 3)
                dve.tensor_reduce(qsum[:, u], qs[:, u % 2].rearrange("p t (h d) -> p (t h) d", d=DIM_HEAD), AX_X,
                                  ALU.add).then_inc(S["q_sum"], 1)
                wait(dve, S["q_sum"], 4 * b + u + 1)
                dve.reciprocal(qrec[:, u], qsum[:, u]).then_inc(S["q_rec"], 1)

            def add_bias(b):
                wait(dve, S["out_mm"], 4 * b + 4)
                wait(dve, S["o_scaled"], b)
                dve.tensor_tensor(ot[:], acc_ps[:].rearrange("p a (t o) -> p (a t) o", o=P),
                                  bo_row[:].unsqueeze(1).broadcast_to([P, NT, P]), ALU.add).then_inc(S["o_bias"], 1)

            def row_lengths(b):
                wait(dve, S["o_sq"], b + 1)
                wait(dve, S["o_root"], b)
                dve.tensor_reduce(ss[:], osq[:], AX_X, ALU.add).then_inc(S["o_ss"], 1)

            def row_scales(b):
                wait(dve, S["o_root"], b + 1)
                dve.tensor_scalar(nrm[:], nrm[:], 1e-12, None, ALU.max).then_inc(S["o_floor"], 1)
                wait(dve, S["o_floor"], b + 1)
                wait(dve, S["o_scaled"], b)
                dve.reciprocal(rn[:], nrm[:]).then_inc(S["o_rec"], 1)

            def update(b):
                wait(dve, S["o_turned"], b + 1)
                wait(dve, S["xn_done"], b + 1)
                at = X[:, b, :]
                dve.scalar_tensor_tensor(at, flat(turn_ps[:]), gate_g[:, 1:2], at,
                                         ALU.mult, ALU.add).then_inc(S["x_new"], 1)

            def body(b, prev, prev2, last):
                max_queries(b, 0)
                max_keys(b, 0)
                shift_queries(b, 0)
                wait(dve, S["ctx_loaded"], 16 * b + 16)
                for h in range(2):
                    dve.bn_stats(c6[:, 6 * h:6 * h + 6], cx[:, 512 * h:512 * h + 512]).then_inc(S["ctx_stats"], 1)
                sum_queries(b, 0)
                max_keys(b, 1)
                if prev2:
                    update(b - 2)
                max_queries(b, 1)
                wait(dve, S["ctx_stats"], 2 * b + 2)
                shift_queries(b, 1)
                dve.bn_aggr(c2[:], c6[:]).then_inc(S["ctx_aggr"], 1)
                sum_queries(b, 1)
                wait(dve, S["ctx_aggr"], b + 1)
                dve.tensor_copy(cmv[:, b, :], c2[:]).then_inc(S["ctx_kept"], 1)
                max_keys(b, 2)
                max_queries(b, 2)
                shift_queries(b, 2)
                if prev2:
                    updated_stats(dve, env, b - 2, S, env["mv2"])
                sum_queries(b, 2)
                max_keys(b, 3)
                max_queries(b, 3)
                shift_queries(b, 3)
                if not last:
                    norm_x(b + 1)
                if prev:
                    add_bias(b - 1)
                sum_queries(b, 3)
                wait(dve, S["k_exp"], 4 * b + 4)
                dve.reciprocal(krec[:], ksum[:]).then_inc(S["k_rec"], 1)
                if prev:
                    row_lengths(b - 1)
                wait(dve, S["m_mm"], b + 1)
                wait(dve, S["k_rec"], b + 1)
                wait(dve, S["out_mm"], 4 * b)
                mps = work_ps[0][:].rearrange("p a (j e) -> p (a j) e", e=256)
                for i in range(2):
                    rows = slice(64 * i, 64 * i + 64)
                    dve.scalar_tensor_tensor(mt[rows], mps[rows, :, i * P:(i + 1) * P], SCALE,
                                             krec[rows].unsqueeze(2).broadcast_to([64, HT, P]),
                                             ALU.mult, ALU.mult).then_inc(S["m_diag"], 1)
                if prev:
                    row_scales(b - 1)

            def tail(b):
                update(b - 2)
                updated_stats(dve, env, b - 2, S, env["mv2"])
                add_bias(b - 1)
                row_lengths(b - 1)
                row_scales(b - 1)
                update(b - 1)
                updated_stats(dve, env, b - 1, S, env["mv2"])
            norm_x(0)
            skewed(dve, body, tail)


def paired(eng, body, count, outside=1):
    body(0, 0, True, 3 if outside > 1 else False)
    with eng.Fori(0, (count - 1 - outside) // 2) as i:
        body(2 * i + 1, 1, False, 3 if outside > 1 else False)
        body(2 * i + 2, 0, False, 3 if outside > 1 else False)
    for b in range(count - outside, count):
        body(b, b % 2, False, count - 1 - b if outside > 1 else True)


def ffn(nc, ctx, env, layer):
    X, ident, tg, work_ps, turn_ps = env["X"], env["ident"], env["tg"], env["work_ps"], env["turn_ps"]
    mv, mv_next = env["mv2"], env["mv"]
    NB, N = X.shape[1], X.shape[2]
    NT = N // P
    gate = tg[:, 6 + layer:7 + layer]
    if layer == 0:
        W, bias, A, B = (env["L0_ffn_" + n] for n in ("W", "bias", "A", "Bf"))
        factors = [env["L0_ffn_coeffs"], env["L0_ffn_scales"]]
    else:
        W, bias, A, B = (env["L1_ffn_" + n] for n in ("W", "bias", "lora_A", "lora_B"))
        factors = [env["L1_ffn_lora_weights"]]
    E, RANK = A.shape[0], A.shape[1]
    LORA_SCALE = 32 / RANK
    KT = E * RANK // P
    st = env["st"]
    with ExitStack() as c:
        sb = lambda n, s, d=F32: c.enter_context(nc.sbuf_tensor(f"f{layer}_" + n, s, d))
        two = lambda n, s: (sb(n + "_h", s, F32R), sb(n + "_l", s, F32R))
        sem = lambda n: c.enter_context(nc.semaphore(f"f{layer}_" + n))
        wt = two("wt", [P, NT, N])
        gbias = sb("gbias", [P, N])

        with ExitStack() as w:
            wsb = lambda n, s, d=F32: w.enter_context(nc.sbuf_tensor(f"fw{layer}_" + n, s, d))
            w_raw, a_raw, b_raw = wsb("w_raw", [P, NT, N]), wsb("a_raw", [P, KT, N]), wsb("b_raw", [P, NT, E, RANK])
            b_turn, fac = wsb("b_turn", [P, KT, N]), wsb("fac", [P, 2, E])
            names = ("w_loaded lora_loaded bias_loaded fac_done b_scaled b_turned b_copied w_mm w_head w_tail "
                     "bias_done var_eps root rstd_done")
            S = {n: w.enter_context(nc.semaphore(f"fw{layer}_" + n)) for n in names.split()}
            block = w.enter_context(nc.Block())

            @block.sync
            def _(sp):
                for n, f in enumerate(factors):
                    sp.dma_start(fac[:, n], f.unsqueeze(0).broadcast_to([P, E])).then_inc(S["lora_loaded"], 16)
                for t in range(NT):
                    sp.dma_start(b_raw[:, t], B[:, t * P:(t + 1) * P, :].rearrange("e p r -> p e r")).then_inc(
                        S["lora_loaded"], 16)
                sp.dma_start(a_raw[:], A.rearrange("e r d -> (e r) d").rearrange("(k p) d -> p k d", p=P)).then_inc(
                    S["lora_loaded"], 16)
                sp.dma_start(w_raw[:], W.rearrange("(t p) d -> p t d", p=P)).then_inc(S["w_loaded"], 16)
                sp.dma_start(gbias[:], bias.unsqueeze(0).broadcast_to([P, N])).then_inc(S["bias_loaded"], 16)

            @block.vector
            def _(dve):
                dve.tensor_scalar(st[:, 1, :], mv[:, :, 1], LN_EPS, None, ALU.add).then_inc(S["var_eps"], 1)
                dve.wait_ge(S["lora_loaded"], 16 * (len(factors) + NT + 1))
                if layer == 0:
                    dve.tensor_tensor(fac[:, 0], fac[:, 0], fac[:, 1], ALU.mult).then_inc(S["fac_done"], 1)
                else:
                    dve.tensor_scalar(fac[:, 0], fac[:, 0], LORA_SCALE, None, ALU.mult).then_inc(S["fac_done"], 1)
                dve.wait_ge(S["fac_done"], 1)
                dve.tensor_tensor(b_raw[:], b_raw[:], fac[:, 0].unsqueeze(1).unsqueeze(3).broadcast_to([P, NT, E, RANK]),
                                  ALU.mult).then_inc(S["b_scaled"], 1)
                dve.wait_ge(S["root"], 1)
                dve.reciprocal(st[:, 0, :], st[:, 2, :]).then_inc(S["rstd_done"], 1)
                dve.wait_ge(S["bias_loaded"], 16)
                dve.tensor_scalar(gbias[:], gbias[:], gate, None, ALU.mult).then_inc(S["bias_done"], 1)
                for j in range(NT):
                    dve.wait_ge(S["w_head"], j + 1)
                    dve.tensor_tensor(wt[1][:, j], work_ps[j % 2][:].rearrange("p a n -> p (a n)"), f32(wt[0][:, j]),
                                      ALU.subtract).then_inc(S["w_tail"], 1)

            @block.scalar
            def _(act):
                act.wait_ge(S["var_eps"], 1)
                act.activation(st[:, 2, :], st[:, 1, :], ACT.Sqrt).then_inc(S["root"], 1)
                for k in range(KT):
                    act.wait_ge(S["b_turned"], k + 1)
                    act.activation(b_turn[:, k], (turn_ps if k == 0 else work_ps[0])[:].rearrange("p a n -> p (a n)"),
                                   ACT.Copy).then_inc(S["b_copied"], 1)
                for j in range(NT):
                    act.wait_ge(S["w_mm"], j + 1)
                    act.activation(wt[0][:, j], work_ps[j % 2][:].rearrange("p a n -> p (a n)"),
                                   ACT.Copy).then_inc(S["w_head"], 1)

            @block.tensor
            def _(pe):
                pe.wait_ge(S["b_scaled"], 1)
                for k in range(KT):
                    for t in range(NT):
                        mm = pe.transpose((turn_ps if k == 0 else work_ps[0])[:, t // 4, (t % 4) * P:(t % 4 + 1) * P],
                                          b_raw[:, t].rearrange("p e r -> p (e r)")[:, k * P:(k + 1) * P], ident[:])
                    mm.then_inc(S["b_turned"], 1)
                pe.wait_ge(S["b_copied"], KT)
                pe.wait_ge(S["w_loaded"], 16)
                for j in range(NT):
                    cols = slice(j * P, (j + 1) * P)
                    if j >= 2:
                        pe.wait_ge(S["w_tail"], j - 1)
                    for n in range(2):
                        for k in range(KT):
                            pe.matmul(work_ps[j % 2][:, n], a_raw[:, k, cols], b_turn[:, k, n * 512:n * 512 + 512],
                                      start=k == 0, stop=False, skip_group_check=True)
                        for i in range(4):
                            mm = pe.matmul(work_ps[j % 2][:, n, i * P:(i + 1) * P], w_raw[:, 4 * n + i, cols], ident[:],
                                           start=False, stop=True, skip_group_check=True)
                    mm.then_inc(S["w_mm"], 1)

        xn, xt = sb("xn", [P, N]), [two(f"xt{i}", [P, NT, P]) for i in range(2)]
        names = "xn_done x_biased turned xt_head xt_tail mm x_new row_stats row_aggr row_kept pair_clear stored"
        S = {n: sem(n) for n in names.split()}
        block = c.enter_context(nc.Block())

        @block.tensor
        def _(pe):
            def turn(b):
                wait(pe, S["xn_done"], b + 1)
                wait(pe, S["xt_tail"], b)
                for i in range(NT):
                    mm = pe.transpose(turn_ps[:, i // 4, (i % 4) * P:(i % 4 + 1) * P], xn[:, i * P:(i + 1) * P], ident[:])
                mm.then_inc(S["turned"], 1)

            def body(b, par, first, last):
                if not last:
                    turn(b + 1)
                wait(pe, S["xt_tail"], b + 1)
                wait(pe, S["x_new"], b - 1)
                for j in range(NT):
                    for n in range(2):
                        mm = three_pass(pe, work_ps[par][:, n], pair(xt[par], slice(None), j),
                                        pair(wt, slice(None), j, slice(n * 512, n * 512 + 512)),
                                        first=j == 0, last=j == NT - 1)
                mm.then_inc(S["mm"], 1)
            turn(0)
            paired(pe, body, NB)

        @block.scalar
        def _(act):
            def body(b, par, first, last):
                wait(act, S["turned"], b + 1)
                wait(act, S["mm"], b - 1)
                act.activation(xt[par][0][:].rearrange("p t n -> p (t n)"), turn_ps[:].rearrange("p a n -> p (a n)"),
                               ACT.Copy).then_inc(S["xt_head"], 1)
            paired(act, body, NB)

        @block.vector
        def _(dve):
            def norm_x(b):
                wait(dve, S["turned"], b)
                dve.tensor_scalar(xn[:], X[:, b, :], mv[:, b, 0:1], st[:, 0, bass.ds(b, 1)],
                                  ALU.subtract, ALU.mult).then_inc(S["xn_done"], 1)
                wait(dve, S["xn_done"], b + 1)
                dve.tensor_tensor(X[:, b, :], X[:, b, :], gbias[:], ALU.add).then_inc(S["x_biased"], 1)

            def tail(b, par):
                wait(dve, S["xt_head"], b + 1)
                dve.tensor_tensor(xt[par][1][:].rearrange("p t n -> p (t n)"), turn_ps[:].rearrange("p a n -> p (a n)"),
                                  f32(xt[par][0][:]).rearrange("p t n -> p (t n)"), ALU.subtract).then_inc(S["xt_tail"], 1)

            def body(b, par, first, left):
                if left >= 1:
                    tail(b + 1, 1 - par)
                if left >= 2:
                    norm_x(b + 2)
                wait(dve, S["mm"], b + 1)
                wait(dve, S["x_biased"], b + 1)
                dve.scalar_tensor_tensor(X[:, b, :], work_ps[par][:].rearrange("p a n -> p (a n)"), gate, X[:, b, :],
                                         ALU.mult, ALU.add).then_inc(S["x_new"], 1)
                if layer == 0:
                    updated_stats(dve, env, b, S, mv_next)
            norm_x(0)
            tail(0, 0)
            norm_x(1)
            paired(dve, body, NB, outside=3)

        @block.sync
        def _(sp):
            if layer == 1:
                def body(b, par, first, last):
                    wait(sp, S["x_new"], b + 1)
                    sp.dma_start(env["out"][b], X[:, b, :]).then_inc(S["stored"], 16)
                paired(sp, body, NB)
                sp.wait_ge(S["stored"], 16 * NB)


def xattn1(nc, ctx, env):
    X, ident, tg = env["X"], env["ident"], env["tg"]
    work_ps, turn_ps, acc_ps = env["work_ps"], env["turn_ps"], env["acc_ps"]
    mv, mv_next, cmv = env["mv"], env["mv2"], env["cmv"]
    NB, N = X.shape[1], X.shape[2]
    NT = N // P
    VW = 2 * P + 2
    gate = tg[:, 5:6]
    with ExitStack() as c:
        sb = lambda n, s, d=F32: c.enter_context(nc.sbuf_tensor("x_" + n, s, d))
        two = lambda n, s: (sb(n + "_h", s, F32R), sb(n + "_l", s, F32R))
        sem = lambda n: c.enter_context(nc.semaphore("x_" + n))
        wts = two("wts", [P, 3, P])
        bq_bk, bs_row = sb("bq_bk", [P, 2]), sb("bs_row", [P, P])
        sc = sb("sc", [P, 8, NB])
        v = [two(f"v{i}", [P, NT, VW]) for i in range(2)]

        with ExitStack() as w:
            raw = w.enter_context(nc.sbuf_tensor("xw_raw", [P, 3, P], F32))
            edge = w.enter_context(nc.sbuf_tensor("xw_edge", [P, 2, NT, 2], F32))
            names = "loaded turned head tail edge_set edge_done chain root"
            S = {n: w.enter_context(nc.semaphore("xw_" + n)) for n in names.split()}
            block = w.enter_context(nc.Block())

            @block.sync
            def _(sp):
                for n, name in enumerate(("Wq", "Wk", "Ws")):
                    sp.dma_start(raw[:, n], env["L1_xattn_" + name]).then_inc(S["loaded"], 16)
                for n, name in enumerate(("bq", "bk")):
                    sp.dma_start(bq_bk[:, n:n + 1], env["L1_xattn_" + name].unsqueeze(1)).then_inc(S["loaded"], 16)
                sp.dma_start(bs_row[:], env["L1_xattn_bs_"].unsqueeze(0).broadcast_to([P, P])).then_inc(S["loaded"], 16)
                sp.wait_ge(S["loaded"], 96)

            @block.tensor
            def _(pe):
                pe.wait_ge(S["loaded"], 96)
                for n in range(3):
                    mm = pe.transpose(turn_ps[:, 0, n * P:(n + 1) * P], raw[:, n], ident[:])
                mm.then_inc(S["turned"], 1)

            @block.scalar
            def _(act):
                act.wait_ge(S["turned"], 1)
                act.activation(wts[0][:].rearrange("p k n -> p (k n)"), turn_ps[:, 0, 0:3 * P], ACT.Copy).then_inc(
                    S["head"], 1)
                act.wait_ge(S["chain"], 2)
                act.activation(sc[:, 4:6, :], sc[:, 2:4, :], ACT.Sqrt).then_inc(S["root"], 1)
                act.wait_ge(S["chain"], 6)
                act.activation(sc[:, 4, :], sc[:, 7, :], ACT.Sqrt).then_inc(S["root"], 1)

            @block.gpsimd
            def _(pool):
                pool.memset(edge[:, 0, :, 0:1], 1.0).then_inc(S["edge_set"], 1)
                pool.memset(edge[:, 0, :, 1:2], 0.0).then_inc(S["edge_set"], 1)
                pool.memset(edge[:, 1], 0.0).then_inc(S["edge_set"], 1)
                pool.wait_ge(S["edge_set"], 3)
                for i in range(2):
                    for k in range(2):
                        pool.tensor_copy(v[i][k][:, :, 2 * P:VW], edge[:, k]).then_inc(S["edge_done"], 1)

            @block.vector
            def _(dve):
                dve.wait_ge(S["head"], 1)
                dve.tensor_tensor(wts[1][:].rearrange("p k n -> p (k n)"), turn_ps[:, 0, 0:3 * P],
                                  f32(wts[0][:]).rearrange("p k n -> p (k n)"), ALU.subtract).then_inc(S["tail"], 1)
                step = [0]

                def link(ins):
                    step[0] += 1
                    ins.then_inc(S["chain"], 1)
                    dve.wait_ge(S["chain"], step[0])
                link(dve.tensor_scalar(sc[:, 2, :], mv[:, :, 1], LN_EPS, None, ALU.add))
                link(dve.tensor_scalar(sc[:, 3, :], cmv[:, :, 1], LN_EPS, None, ALU.add))
                dve.wait_ge(S["root"], 1)
                link(dve.reciprocal(sc[:, 0:2, :], sc[:, 4:6, :]))
                link(dve.tensor_tensor(sc[:, 6, :], sc[:, 0, :], sc[:, 0, :], ALU.mult))
                link(dve.tensor_tensor(sc[:, 6, :], sc[:, 6, :], mv[:, :, 1], ALU.mult))
                link(dve.tensor_scalar(sc[:, 7, :], sc[:, 6, :], LN_EPS, None, ALU.add))
                dve.wait_ge(S["root"], 2)
                link(dve.reciprocal(sc[:, 5, :], sc[:, 4, :]))
                link(dve.tensor_tensor(sc[:, 0, :], sc[:, 0, :], sc[:, 5, :], ALU.mult))

        cx, xn = sb("cx", [P, N]), sb("xn", [P, N])
        xq, ch, kn = two("xq", [P, N]), two("c", [P, N]), two("kn", [P, N])
        kn_f = [sb(f"kn_f{i}", [P, N]) for i in range(2)]
        qp, kp = two("qp", [P, N]), two("kp", [P, N])
        sp32, sq32 = sb("sp32", [P, NT, P]), sb("sq32", [P, NT, P])
        p, pt = sb("p", [P, 2, N]), [two(f"pt{i}", [P, NT, P]) for i in range(2)]
        smax, rcp = sb("smax", [P, NT]), sb("rcp", [P, NT])
        mean_sq = sb("mean_sq", [P, 2, NT, P])
        std, u = sb("std", [P, NT * P]), sb("u", [P, N])
        names = ("ctx_loaded c_head c_tail xn_done xq_head xq_tail knf_done kn_head kn_tail q_mm q_head q_tail "
                 "k_mm k_head k_tail sp_mm sp_done sq_done v_head v_tail s_mm s_max p_exp p_turned pt_head pt_tail "
                 "pv_mm pv_rec pv_out mean2 var floor root mean_turned std_turned x_mean u_done warmed x_new row_stats row_aggr row_kept pair_clear")
        S = {n: sem(n) for n in names.split()}
        block = c.enter_context(nc.Block())
        flat = lambda ap: ap.rearrange("p a n -> p (a n)")

        @block.sync
        def _(sp):
            def body(b, par, first, last):
                wait(sp, S["c_tail"], b)
                wait(sp, S["knf_done"], b)
                sp.dma_start(cx[:], env["ctx_dram"][b]).then_inc(S["ctx_loaded"], 16)
            paired(sp, body, NB)

        @block.gpsimd
        def _(pool):
            def tail_of(b, t, src, name):
                wait(pool, S[name + "_head"], b + 1)
                pool.tensor_tensor(t[1][:], src, f32(t[0][:]), ALU.subtract).then_inc(S[name + "_tail"], 1)

            def variance(b):
                wait(pool, S["pv_out"], 8 * b + 8)
                wait(pool, S["std_turned"], b)
                pool.tensor_tensor(std[:], flat(mean_sq[:, 0]), flat(mean_sq[:, 0]), ALU.mult).then_inc(S["mean2"], 1)
                wait(pool, S["mean2"], b + 1)
                pool.tensor_tensor(std[:], flat(mean_sq[:, 1]), std[:], ALU.subtract).then_inc(S["var"], 1)

            def values(b, par):
                wait(pool, S["sp_done"], b + 1)
                wait(pool, S["v_tail"], 2 * b)
                pool.tensor_tensor(sq32[:], sp32[:], sp32[:], ALU.mult).then_inc(S["sq_done"], 1)
                for k, src in enumerate((sp32, sq32)):
                    wait(pool, S["v_head"], 2 * b + k + 1)
                    cols = slice(k * P, (k + 1) * P)
                    pool.tensor_tensor(v[par][1][:, :, cols], src[:], f32(v[par][0][:, :, cols]),
                                       ALU.subtract).then_inc(S["v_tail"], 1)

            def prep(b, par):
                tail_of(b, ch, cx[:], "c")
                tail_of(b, xq, xn[:], "xq")
                values(b, par)
                tail_of(b, kn, kn_f[par][:], "kn")

            def body(b, par, first, last):
                if not first:
                    variance(b - 1)
                if not last:
                    prep(b + 1, 1 - par)
            prep(0, 0)
            paired(pool, body, NB)
            variance(NB - 1)

        @block.tensor
        def _(pe):
            ALL = slice(None)

            def turn(out, src):
                for i in range(NT):
                    mm = pe.transpose(out[:, i // 4, (i % 4) * P:(i % 4 + 1) * P], src(i), ident[:])
                return mm

            def project(n, slot, src, done):
                for h in range(2):
                    mm = three_pass(pe, slot[:, h], pair(wts, ALL, n), pair(src, ALL, slice(512 * h, 512 * h + 512)))
                mm.then_inc(done, 1)

            def project_values(b):
                wait(pe, S["c_tail"], b + 1)
                for i in range(NT):
                    mm = three_pass(pe, turn_ps[:, i // 4, (i % 4) * P:(i % 4 + 1) * P],
                                    pair(ch, ALL, slice(i * P, (i + 1) * P)), pair(wts, ALL, 2))
                mm.then_inc(S["sp_mm"], 1)

            def scores(t):
                for h in range(2):
                    mm = three_pass(pe, work_ps[t % 2][:, h], pair(qp, ALL, slice(t * P, (t + 1) * P)),
                                    pair(kp, ALL, slice(512 * h, 512 * h + 512)))
                mm.then_inc(S["s_mm"], 1)

            def turn_scores(b, t):
                wait(pe, S["p_exp"], 8 * b + t + 1)
                turn(turn_ps, lambda i: p[:, t % 2, i * P:(i + 1) * P]).then_inc(S["p_turned"], 1)

            def weigh(b, t, par):
                wait(pe, S["pt_tail"], 8 * b + t + 1)
                wait(pe, S["pv_out"], 8 * b + t - 1)
                for i in range(NT):
                    mm = three_pass(pe, acc_ps[:, t % 2, 0:VW], pair(pt[t % 2], ALL, i), pair(v[par], ALL, i),
                                    first=i == 0, last=i == NT - 1)
                mm.then_inc(S["pv_mm"], 1)

            def turn_mean(b):
                wait(pe, S["pv_out"], 8 * b + 8)
                turn(turn_ps, lambda i: mean_sq[:, 0, i, :]).then_inc(S["mean_turned"], 1)

            def turn_std(b):
                wait(pe, S["root"], b + 1)
                turn(turn_ps, lambda i: std[:, i * P:(i + 1) * P]).then_inc(S["std_turned"], 1)

            def body(b, par, first, last):
                wait(pe, S["q_tail"], b + 1)
                wait(pe, S["k_tail"], b + 1)
                scores(0)
                scores(1)
                wait(pe, S["pt_tail"], 8 * b)
                if not first:
                    turn_mean(b - 1)
                    wait(pe, S["x_mean"], b)
                turn_scores(b, 0)
                for t in range(NT):
                    if t + 2 < NT:
                        wait(pe, S["p_exp"], 8 * b + t + 1)
                        scores(t + 2)
                    if t == 6 and not last:
                        wait(pe, S["p_exp"], 8 * b + 7)
                        wait(pe, S["xq_tail"], b + 2)
                        project(0, work_ps[0], xq, S["q_mm"])
                    if t == 7 and not last:
                        wait(pe, S["p_exp"], 8 * b + 8)
                        wait(pe, S["kn_tail"], b + 2)
                        project(1, work_ps[1], kn, S["k_mm"])
                    if t + 1 < NT:
                        wait(pe, S["pt_tail"], 8 * b + t + 1)
                        if t == 2 and not last:
                            wait(pe, S["sp_done"], b + 2)
                        if t == 3 and not first:
                            wait(pe, S["u_done"], b)
                        turn_scores(b, t + 1)
                    if t == 0:
                        wait(pe, S["v_tail"], 2 * b + 2)
                    weigh(b, t, par)
                    if t == 1 and not last:
                        wait(pe, S["pt_tail"], 8 * b + 3)
                        project_values(b + 1)
                    if t == 2 and not first:
                        wait(pe, S["pt_tail"], 8 * b + 4)
                        turn_std(b - 1)
            wait(pe, S["xq_tail"], 1)
            project(0, work_ps[0], xq, S["q_mm"])
            project_values(0)
            wait(pe, S["kn_tail"], 1)
            project(1, work_ps[1], kn, S["k_mm"])
            wait(pe, S["sp_done"], 1)
            paired(pe, body, NB)
            wait(pe, S["pt_tail"], 8 * NB)
            turn_mean(NB - 1)
            wait(pe, S["x_mean"], NB)
            turn_std(NB - 1)

        @block.scalar
        def _(act):
            def head(b, t, src, name, ready, last_read):
                wait(act, *ready)
                wait(act, *last_read)
                act.activation(t[0][:], src, ACT.Copy).then_inc(S[name + "_head"], 1)

            def head_c(b):
                head(b, ch, cx[:], "c", (S["ctx_loaded"], 16 * b + 16), (S["sp_mm"], b))

            def head_xq(b):
                head(b, xq, xn[:], "xq", (S["xn_done"], b + 1), (S["q_mm"], b))

            def head_kn(b, par):
                head(b, kn, kn_f[par][:], "kn", (S["knf_done"], b + 1), (S["k_mm"], b))

            def head_v(b, par, k):
                wait(act, S["sp_done" if k == 0 else "sq_done"], b + 1)
                act.activation(v[par][0][:, :, k * P:(k + 1) * P], (sp32, sq32)[k][:], ACT.Copy).then_inc(S["v_head"], 1)

            def head_proj(b, n):
                t, name = ((qp, "q"), (kp, "k"))[n]
                wait(act, S[name + "_mm"], b + 1)
                wait(act, S["s_mm"], 8 * b)
                act.activation(t[0][:], flat(work_ps[n][:]), ACT.Identity, bias=bq_bk[:, n:n + 1]).then_inc(
                    S[name + "_head"], 1)

            def exp(b, t):
                wait(act, S["s_max"], 8 * b + t + 1)
                wait(act, S["p_turned"], 8 * b + t - 1)
                act.activation(p[:, t % 2], flat(work_ps[t % 2][:]), ACT.Exp, bias=smax[:, t:t + 1]).then_inc(
                    S["p_exp"], 1)

            def head_scores(b, t):
                wait(act, S["p_turned"], 8 * b + t + 1)
                wait(act, S["pv_mm"], 8 * b + t - 1)
                act.activation(pt[t % 2][0][:].rearrange("p t n -> p (t n)"), flat(turn_ps[:]), ACT.Copy).then_inc(
                    S["pt_head"], 1)

            def root(b):
                wait(act, S["floor"], b + 1)
                act.activation(std[:], std[:], ACT.Sqrt).then_inc(S["root"], 1)
                wait(act, S["warmed"], b)
                act.activation(env["warm"][:], ident[:, 0:1], ACT.Exp).then_inc(S["warmed"], 1)

            def body(b, par, first, last):
                exp(b, 0)
                exp(b, 1)
                head_scores(b, 0)
                for t in range(NT):
                    if t + 1 < NT:
                        head_scores(b, t + 1)
                    if t + 2 < NT:
                        exp(b, t + 2)
                    if not last:
                        if t == 0:
                            head_c(b + 1)
                        if t == 1:
                            head_xq(b + 1)
                        if t == 3:
                            head_v(b + 1, 1 - par, 0)
                        if t == 4:
                            head_v(b + 1, 1 - par, 1)
                        if t == 5:
                            head_kn(b + 1, 1 - par)
                        if t == 6:
                            head_proj(b + 1, 0)
                        if t == 7:
                            head_proj(b + 1, 1)
                    if t == 1 and not first:
                        root(b - 1)
            head_c(0)
            head_xq(0)
            head_proj(0, 0)
            head_v(0, 0, 0)
            head_v(0, 0, 1)
            head_kn(0, 0)
            head_proj(0, 1)
            paired(act, body, NB)
            root(NB - 1)

        @block.vector
        def _(dve):
            def norm_x(b):
                wait(dve, S["xq_tail"], b)
                dve.tensor_scalar(xn[:], X[:, b, :], mv[:, b, 0:1], sc[:, 0, bass.ds(b, 1)],
                                  ALU.subtract, ALU.mult).then_inc(S["xn_done"], 1)

            def norm_ctx(b, par):
                wait(dve, S["ctx_loaded"], 16 * b + 16)
                wait(dve, S["kn_tail"], b - 1)
                dve.tensor_scalar(kn_f[par][:], cx[:], cmv[:, b, 0:1], sc[:, 1, bass.ds(b, 1)],
                                  ALU.subtract, ALU.mult).then_inc(S["knf_done"], 1)

            def tail_proj(b, n):
                t, name = ((qp, "q"), (kp, "k"))[n]
                wait(dve, S[name + "_head"], b + 1)
                dve.scalar_tensor_tensor(t[1][:], flat(work_ps[n][:]), bq_bk[:, n:n + 1], f32(t[0][:]),
                                         ALU.add, ALU.subtract).then_inc(S[name + "_tail"], 1)

            def add_value_bias(b):
                wait(dve, S["sp_mm"], b + 1)
                wait(dve, S["v_tail"], 2 * b)
                dve.tensor_tensor(sp32[:], turn_ps[:].rearrange("p a (t n) -> p (a t) n", n=P),
                                  bs_row[:].unsqueeze(1).broadcast_to([P, NT, P]), ALU.add).then_inc(S["sp_done"], 1)

            def max_scores(b, t):
                wait(dve, S["s_mm"], 8 * b + t + 1)
                wait(dve, S["p_exp"], 8 * b + t - 7)
                dve.tensor_reduce(smax[:, t:t + 1], work_ps[t % 2][:], mybir.AxisListType.XY, ALU.max,
                                  negate=True).then_inc(S["s_max"], 1)

            def tail_scores(b, t):
                wait(dve, S["pt_head"], 8 * b + t + 1)
                dve.tensor_tensor(pt[t % 2][1][:].rearrange("p t n -> p (t n)"), flat(turn_ps[:]),
                                  f32(pt[t % 2][0][:]).rearrange("p t n -> p (t n)"), ALU.subtract).then_inc(
                    S["pt_tail"], 1)

            def divide(b, t):
                wait(dve, S["pv_mm"], 8 * b + t + 1)
                dve.reciprocal(rcp[:, t:t + 1], acc_ps[:, t % 2, 2 * P:2 * P + 1]).then_inc(S["pv_rec"], 1)
                wait(dve, S["pv_rec"], 8 * b + t + 1)
                wait(dve, S["mean_turned"], b)
                wait(dve, S["var"], b)
                dve.tensor_scalar(mean_sq[:, :, t, :], acc_ps[:, t % 2, 0:2 * P].rearrange("p (k n) -> p k n", k=2),
                                  rcp[:, t:t + 1], None, ALU.mult).then_inc(S["pv_out"], 1)

            def add_mean(b):
                wait(dve, S["mean_turned"], b + 1)
                wait(dve, S["xn_done"], b + 1)
                dve.scalar_tensor_tensor(X[:, b, :], flat(turn_ps[:]), gate, X[:, b, :], ALU.mult, ALU.add).then_inc(
                    S["x_mean"], 1)

            def floor(b):
                wait(dve, S["var"], b + 1)
                dve.tensor_scalar(std[:], std[:], 0.0, None, ALU.max).then_inc(S["floor"], 1)

            def add_std(b, par):
                wait(dve, S["std_turned"], b + 1)
                dve.tensor_tensor(u[:], flat(turn_ps[:]), kn_f[par][:], ALU.mult).then_inc(S["u_done"], 1)
                wait(dve, S["u_done"], b + 1)
                wait(dve, S["x_mean"], b + 1)
                dve.scalar_tensor_tensor(X[:, b, :], u[:], gate, X[:, b, :], ALU.mult, ALU.add).then_inc(S["x_new"], 1)
                updated_stats(dve, env, b, S, mv_next)

            def body(b, par, first, last):
                max_scores(b, 0)
                max_scores(b, 1)
                if not first:
                    add_mean(b - 1)
                tail_scores(b, 0)
                for t in range(NT):
                    if t + 2 < NT:
                        max_scores(b, t + 2)
                    if t + 1 < NT:
                        tail_scores(b, t + 1)
                    if not last and t == 0:
                        norm_x(b + 1)
                    if not first and t == 1:
                        floor(b - 1)
                    if not last and t == 6:
                        tail_proj(b + 1, 0)
                    if not last and t == 7:
                        tail_proj(b + 1, 1)
                    divide(b, t)
                    if not last and t == 1:
                        add_value_bias(b + 1)
                    if not first and t == 2:
                        add_std(b - 1, 1 - par)
                    if not last and t == 3:
                        norm_ctx(b + 1, 1 - par)
            norm_x(0)
            norm_ctx(0, 0)
            tail_proj(0, 0)
            add_value_bias(0)
            tail_proj(0, 1)
            paired(dve, body, NB)
            add_mean(NB - 1)
            floor(NB - 1)
            add_std(NB - 1, 1)


def flamingo_gated_kernel(nc, out, **dram):
    NB, ROWS, N = dram["x"].shape
    assert ROWS == P and N == 1024
    with ExitStack() as ctx:
        sb = lambda n, s: ctx.enter_context(nc.sbuf_tensor(n, s, F32))
        env = dict(dram)
        env.update(x_dram=dram["x"], ctx_dram=dram["ctx_4096"], out=out)
        env["X"] = sb("X", [P, NB, N])
        env["ident"] = sb("ident", [P, P])
        env["tg"] = sb("tg", [P, 8])
        env["st"] = sb("st", [P, 3, NB])
        env["stats"] = sb("stats", [P, NB, 12])
        env["warm"] = sb("warm", [P, 1])
        env["pair"] = sb("pair", [P, 4])
        env["mv"], env["mv2"], env["cmv"] = (sb(n, [P, NB, 2]) for n in ("mv", "mv2", "cmv"))
        env["work_ps"] = [ctx.enter_context(nc.psum_tensor(f"work{i}", [P, 2, 512], F32)) for i in range(2)]
        env["turn_ps"] = ctx.enter_context(nc.psum_tensor("turn", [P, 2, 512], F32))
        env["acc_ps"] = ctx.enter_context(nc.psum_tensor("acc", [P, 2, 512], F32))
        prepare(nc, ctx, env)
        env["first_sems"] = []
        xattn0(nc, ctx, env)
        nc.all_engine_barrier()
        nc.clear_and_free_semaphores(env["first_sems"])
        nc.all_engine_barrier()
        ffn(nc, ctx, env, 0)
        xattn1(nc, ctx, env)
        ffn(nc, ctx, env, 1)


_INS = ['x', 'ctx_4096', 'g_xattn', 'g_ffn', 'L0_xattn_Wq', 'L0_xattn_Wk', 'L0_xattn_Wv', 'L0_xattn_Wo',
        'L0_xattn_bo', 'L0_xattn_g', 'L0_ffn_W', 'L0_ffn_bias', 'L0_ffn_A', 'L0_ffn_Bf', 'L0_ffn_coeffs',
        'L0_ffn_scales', 'L1_xattn_Wq', 'L1_xattn_bq', 'L1_xattn_Wk', 'L1_xattn_bk', 'L1_xattn_Ws',
        'L1_xattn_bs_', 'L1_ffn_lora_A', 'L1_ffn_lora_B', 'L1_ffn_W', 'L1_ffn_bias', 'L1_ffn_lora_weights']
_OUT = (16, 128, 1024)


def kernel(**inputs):
    import numpy as _np
    import concourse.bacc as _bacc
    from concourse import mybir as _mybir
    from concourse.bass_utils import run_bass_kernel_spmd as _run

    nc = _bacc.Bacc("TRN2", target_bir_lowering=False, num_devices=1)
    arrays, dram = {}, {}
    for name in _INS:
        a = _np.ascontiguousarray(inputs[name])
        arrays[f"in_{name}"] = a
        dram[name] = nc.dram_tensor(f"in_{name}", a.shape, _mybir.dt.from_np(a.dtype), kind="ExternalInput").ap()
    out = nc.dram_tensor("out_0", _OUT, _mybir.dt.float32, kind="ExternalOutput").ap()
    flamingo_gated_kernel(nc, out, **dram)
    r = _run(nc, [arrays], core_ids=[0])
    return r.results[0]["out_0"]
```

```python
from contextlib import ExitStack

import concourse.bass as bass
from concourse import mybir

P = 128
ACT = mybir.ActivationFunctionType
ALU = mybir.AluOpType
F32 = mybir.dt.float32
F32R = mybir.dt.float32r
AX_X = mybir.AxisListType.X
LN_EPS = 1e-5
HEADS, DIM_HEAD = 8, 64


def wait(eng, sem, value):
    if not (isinstance(value, int) and value <= 0):
        eng.wait_ge(sem, value)


def three_pass(eng, out, lhs, rhs, first=True, last=True):
    (lh, ll), (rh, rl) = lhs, rhs
    eng.matmul(out, lh, rh, start=first, stop=False)
    eng.matmul(out, lh, rl, start=False, stop=False)
    return eng.matmul(out, ll, rh, start=False, stop=last)


def pair(t, *idx):
    return (t[0][idx], t[1][idx])


def over(nc, name, shape, dtype, offset):
    return nc.alloc_sbuf_tensor_at(name, shape, dtype, offset=offset)


def f32(ap):
    return ap.bitcast(F32)


def updated_stats(dve, env, b, S, mv):
    six, two = env["stats"][:], env["pair"][:, 0:2]
    wait(dve, S["x_new"], b + 1)
    dve.memset(env["pair"][:, 2:3], 0.0).then_inc(S["pair_clear"], 1)
    for h in range(2):
        dve.bn_stats(six[:, 6 * h:6 * h + 6], env["X"][:, b, 512 * h:512 * h + 512]).then_inc(S["row_stats"], 1)
    wait(dve, S["row_stats"], 2 * b + 2)
    dve.memset(env["pair"][:, 3:4], 0.0).then_inc(S["pair_clear"], 1)
    dve.bn_aggr(two, six).then_inc(S["row_aggr"], 1)
    wait(dve, S["row_aggr"], b + 1)
    dve.tensor_copy(mv[:, b, :], two).then_inc(S["row_kept"], 1)


def xattn0(nc, ctx, env):
    X, ident, tg = env["X"], env["ident"], env["tg"]
    work_ps, turn_ps, acc_ps = env["work_ps"], env["turn_ps"], env["acc_ps"]
    NB, N = X.shape[1], X.shape[2]
    NT = N // P
    HID = HEADS * DIM_HEAD
    HT = HID // P
    SCALE = DIM_HEAD ** -0.5
    with ExitStack() as c:
        sb = lambda n, s, d=F32: c.enter_context(nc.sbuf_tensor("a_" + n, s, d))
        two = lambda n, s: (sb(n + "_h", s, F32R), sb(n + "_l", s, F32R))
        sem = lambda n: env["first_sems"].append(nc.alloc_semaphore("a_" + n)) or env["first_sems"][-1]
        kt_at = -(-nc.sbuf_base // 32) * 32
        kt = sb("kt", [P, NT, HID])
        wq, wk, bvo = two("wq", [P, HID]), two("wk", [P, HID]), sb("bvo", [P, HEADS * P])
        bo_row, gate_g = sb("bo_row", [P, P]), sb("gate_g", [P, 2])
        cx, xn, *halves = env["stage"]
        ch, xh = halves[0:2], halves[2:4]
        names = ("ctx_loaded ctx_stats ctx_aggr ctx_kept c_head c_tail xn_done x_head x_tail ctx_turned ct_copied "
                 "k_mm k_max k_exp k_turned kt_copied k_rec g_mm g_copied m_mm m_diag q_mm q_max q_sub q_exp q_sum "
                 "q_rec q_norm q_turned qt_copied out_mm o_bias o_sq o_ss o_root o_floor o_rec o_scaled o_turned "
                 "warmed x_new row_stats row_aggr row_kept pair_clear "
                 "in_clear in_stats in_aggr in_var in_root in_scale")
        S = {n: sem(n) for n in names.split()}
        x_loaded = [sem(f"x_loaded{b}") for b in range(NB)]

        in_six, in_st = sb("in_six", [P, 12]), sb("in_st", [P, 6])

        def row_variances(dve, b):
            if isinstance(b, int):
                dve.wait_ge(x_loaded[b], 16)
            for h in range(2):
                dve.bn_stats(in_six[:, 6 * h:6 * h + 6], X[:, b, 512 * h:512 * h + 512]).then_inc(S["in_stats"], 1)
            wait(dve, S["in_stats"], 2 * b + 2)
            wait(dve, S["xn_done"], b)
            dve.memset(in_st[:, 5:6], 0.0).then_inc(S["in_clear"], 1)
            dve.bn_aggr(in_st[:, 0:2], in_six[:]).then_inc(S["in_aggr"], 1)
            wait(dve, S["in_aggr"], b + 1)
            dve.tensor_scalar(in_st[:, 2:3], in_st[:, 1:2], LN_EPS, None, ALU.add).then_inc(S["in_var"], 1)

        def row_roots(act, b):
            wait(act, S["in_var"], b + 1)
            act.activation(in_st[:, 3:4], in_st[:, 2:3], ACT.Sqrt).then_inc(S["in_root"], 1)

        def row_rescales(dve, b):
            wait(dve, S["in_root"], b + 1)
            dve.reciprocal(in_st[:, 4:5], in_st[:, 3:4]).then_inc(S["in_scale"], 1)

        def norm_x(dve, b):
            wait(dve, S["in_scale"], b + 1)
            wait(dve, S["x_tail"], b)
            dve.tensor_scalar(xn[:], X[:, b, :], in_st[:, 0:1], in_st[:, 4:5],
                              ALU.subtract, ALU.mult).then_inc(S["xn_done"], 1)

        with ExitStack() as w:
            wsb = lambda n, s, d=F32: w.enter_context(nc.sbuf_tensor("aw_" + n, s, d))
            wsem = lambda n: sem("w_" + n)
            q_raw, k_raw = wsb("q_raw", [P, HT, P]), wsb("k_raw", [P, HT, P])
            v_raw, o_raw, o_turn = wsb("v_raw", [P, HT, P]), wsb("o_raw", [P, HID]), wsb("o_turn", [P, HT, P])
            q_loaded, k_loaded, v_loaded, o_loaded = (wsem(n + "_loaded") for n in "qkvo")
            g_loaded, bias_loaded, ident_zero, ident_ready = (wsem(n) for n in (
                "g_loaded", "bias_loaded", "ident_zero", "ident_ready"))
            turned, head_done, tail_done = wsem("turned"), wsem("head_done"), wsem("tail_done")
            o_copied, b_done, gates_done, g_scaled = (wsem(n) for n in ("o_copied", "b_done", "gates_done", "g_scaled"))
            by_parity = lambda t: t.rearrange("p (j i o) -> p i j o", i=2, o=P)
            b_rows = work_ps[1][:].rearrange("p i (j o) -> p i j o", o=P)
            block = w.enter_context(nc.Block())

            @block.sync
            def _(sp):
                for dst, src, done in ((q_raw, "Wq", q_loaded), (k_raw, "Wk", k_loaded)):
                    sp.dma_start(dst[:], env["L0_xattn_" + src].rearrange("(j p) c -> p j c", p=P)).then_inc(done, 16)
                sp.dma_start(X[:, 0, :], env["x_dram"][0]).then_inc(x_loaded[0], 16)
                sp.dma_start(o_raw[:], env["L0_xattn_Wo"]).then_inc(o_loaded, 16)
                sp.dma_start(v_raw[:], env["L0_xattn_Wv"].rearrange("(j p) c -> p j c", p=P)).then_inc(v_loaded, 16)
                sp.dma_start(X[:, 1, :], env["x_dram"][1]).then_inc(x_loaded[1], 16)
                sp.dma_start(cx[:], env["ctx_dram"][0]).then_inc(S["ctx_loaded"], 16)
                sp.dma_start(tg[:, 0:2], env["g_xattn"].unsqueeze(0).broadcast_to([P, 2])).then_inc(g_loaded, 16)
                sp.dma_start(tg[:, 2:4], env["g_ffn"].unsqueeze(0).broadcast_to([P, 2])).then_inc(g_loaded, 16)
                sp.dma_start(bo_row[:], env["L0_xattn_bo"].unsqueeze(0).broadcast_to([P, P])).then_inc(bias_loaded, 16)
                sp.dma_start(gate_g[:, 0:1], env["L0_xattn_g"].rearrange("a p b -> p (a b)")).then_inc(bias_loaded, 16)
                for b in range(2, NB):
                    sp.dma_start(X[:, b, :], env["x_dram"][b]).then_inc(x_loaded[b], 16)

            @block.gpsimd
            def _(pool):
                pool.memset(ident[:], 0.0).then_inc(ident_zero, 1)
                pool.wait_ge(ident_zero, 1)
                pool.affine_select(out=ident[:], in_=ident[:], compare_op=ALU.not_equal, fill=1.0, base=0,
                                   pattern=[[-1, P]], channel_multiplier=1).then_inc(ident_ready, 1)

            @block.tensor
            def _(pe):
                pe.wait_ge(ident_ready, 1)
                for raw, out, loaded in ((q_raw, work_ps[0][:, 0], q_loaded), (k_raw, work_ps[0][:, 1], k_loaded)):
                    pe.wait_ge(loaded, 16)
                    for j in range(HT):
                        mm = pe.transpose(out[:, j * P:(j + 1) * P], raw[:, j, :], ident[:])
                    mm.then_inc(turned, 1)
                pe.wait_ge(o_loaded, 16)
                for j in range(HT):
                    mm = pe.transpose(turn_ps[:, 0, j * P:(j + 1) * P], o_raw[:, j * P:(j + 1) * P], ident[:])
                mm.then_inc(turned, 1)
                pe.wait_ge(v_loaded, 16)
                pe.wait_ge(o_copied, 1)
                for h in range(HEADS):
                    lo = DIM_HEAD * (h % 2)
                    rows = slice(lo, lo + DIM_HEAD)
                    mm = pe.matmul(work_ps[1][:, h % 2, (h // 2) * P:(h // 2 + 1) * P], v_raw[rows, h // 2, :],
                                   o_turn[rows, h // 2, :], start=True, stop=True)
                mm.then_inc(b_done, 1)

            @block.scalar
            def _(act):
                for n, w_ in enumerate((wq, wk)):
                    act.wait_ge(turned, n + 1)
                    act.activation(w_[0][:], work_ps[0][:, n], ACT.Copy).then_inc(head_done, 1)
                row_roots(act, 0)
                act.wait_ge(b_done, 1)
                act.activation(by_parity(bvo[:]), b_rows, ACT.Copy).then_inc(head_done, 1)
                row_roots(act, 1)
                act.wait_ge(g_loaded, 32)
                act.activation(tg[:, 4:8], tg[:, 0:4], ACT.Tanh).then_inc(gates_done, 1)
                act.activation(env["warm"][:], ident[:, 0:1], ACT.Exp).then_inc(S["warmed"], 1)

            @block.vector
            def _(dve):
                for n, w_ in enumerate((wq, wk)):
                    dve.wait_ge(head_done, n + 1)
                    dve.tensor_tensor(w_[1][:], work_ps[0][:, n], f32(w_[0][:]), ALU.subtract).then_inc(tail_done, 1)
                row_variances(dve, 0)
                dve.wait_ge(turned, 3)
                dve.tensor_copy(o_turn[:], turn_ps[:, 0].rearrange("p (j o) -> p j o", o=P)).then_inc(o_copied, 1)
                row_rescales(dve, 0)
                norm_x(dve, 0)
                row_variances(dve, 1)
                row_rescales(dve, 1)
                dve.wait_ge(gates_done, 1)
                dve.wait_ge(bias_loaded, 32)
                dve.scalar_tensor_tensor(gate_g[:, 1:2], gate_g[:, 0:1], float(P) ** 0.5, tg[:, 4:5],
                                         ALU.mult, ALU.mult).then_inc(g_scaled, 1)

        ct = sb("ct", [P, NT, P])
        qs, ke = sb("qs", [P, 2, 2, HID]), sb("ke", [P, 2, N])
        lora = env["lora"] = lora_prep(nc, env, 0, kt_at, nc.sbuf_base - 8 * N)
        lora_slots = (work_ps[0], work_ps[1])
        qt = sb("qt", [P, 4, 2, HT, P])
        gt, mt = sb("gt", [P, HID]), sb("mt", [P, HT, P])
        kmax, ksum, krec = sb("kmax", [P, HT]), sb("ksum", [P, HT]), sb("krec", [P, HT])
        qmax, qsum, qrec = (sb(n, [P, 4, 2, HEADS]) for n in ("qmax", "qsum", "qrec"))
        ot, osq, ot2 = sb("ot", [P, NT, P]), sb("osq", [P, NT, P]), sb("ot2", [P, NT, P])
        ss, nrm, rn = sb("ss", [P, NT]), sb("nrm", [P, NT]), sb("rn", [P, NT])
        c6, c2 = sb("c6", [P, 12]), sb("c2", [P, 2])
        cmv = env["cmv"]
        block = c.enter_context(nc.Block())
        flat = lambda ap: ap.rearrange("p a n -> p (a n)")

        def skewed(eng, body, tail=None):
            body(0, False, False, True, False)
            body(1, True, False, True, False)
            with eng.Fori(2, NB - 2) as b:
                body(b, True, True, True, False)
            body(NB - 2, True, True, False, False)
            body(NB - 1, True, True, False, True)
            if tail:
                tail(NB)

        @block.sync
        def _(sp):
            def body(b, prev, prev2, ahead, last):
                if prev:
                    wait(sp, S["ctx_stats"], 2 * b)
                    wait(sp, S["ctx_turned"], b)
                    wait(sp, S["c_tail"], b)
                    sp.dma_start(cx[:], env["ctx_dram"][b]).then_inc(S["ctx_loaded"], 16)
            load_lora(sp, env, 0)
            done = env["x_small_loaded"]
            for n, name in enumerate(("Wq", "Wk", "Ws")):
                sp.dma_start(env["x_raw"][:, n], env["L1_xattn_" + name]).then_inc(done, 16)
            for n, name in enumerate(("bq", "bk")):
                sp.dma_start(env["bq_bk"][:, n:n + 1], env["L1_xattn_" + name].unsqueeze(1)).then_inc(done, 16)
            sp.dma_start(env["bs_row"][:], env["L1_xattn_bs_"].unsqueeze(0).broadcast_to([P, P])).then_inc(done, 16)
            skewed(sp, body)
            sp.wait_ge(S["ctx_stats"], 2 * NB)
            sp.wait_ge(S["ctx_turned"], NB)
            sp.wait_ge(S["c_tail"], NB)
            sp.wait_ge(S["x_tail"], NB)
            sp.wait_ge(S["k_mm"], 4 * NB)
            sp.wait_ge(S["q_mm"], 4 * NB)
            load_w(sp, env, 0)

        @block.gpsimd
        def _(pool):
            def tail_of(b, t, src, name):
                wait(pool, S[name + "_head"], b + 1)
                pool.tensor_tensor(t[1][:], src, f32(t[0][:]), ALU.subtract).then_inc(S[name + "_tail"], 1)

            def divide_queries(b, u):
                wait(pool, S["q_rec"], 4 * b + u + 1)
                q = qs[:, u % 2].rearrange("p t (h d) -> p (t h) d", d=DIM_HEAD)
                r = qrec[:, u].rearrange("p t h -> p (t h)").unsqueeze(2).broadcast_to([P, 2 * HEADS, DIM_HEAD])
                pool.tensor_tensor(q, q, r, ALU.mult).then_inc(S["q_norm"], 1)

            def scale_rows(b):
                wait(pool, S["o_rec"], b + 1)
                pool.tensor_tensor(ot2[:], ot[:], rn[:].unsqueeze(2).broadcast_to([P, NT, P]),
                                   ALU.mult).then_inc(S["o_scaled"], 1)

            def body(b, prev, prev2, ahead, last):
                if prev2:
                    scale_rows(b - 2)
                for u in range(3):
                    divide_queries(b, u)
                if not last:
                    tail_of(b + 1, xh, xn[:], "x")
                divide_queries(b, 3)
                if not last:
                    tail_of(b + 1, ch, cx[:], "c")

            def tail(b):
                scale_rows(b - 2)
                pool.wait_ge(S["k_turned"], 4 * NB)
                lora_scale_b(pool, env, lora)
                lora_tail_a(pool, lora)
            tail_of(0, xh, xn[:], "x")
            tail_of(0, ch, cx[:], "c")
            skewed(pool, body, tail)

        @block.tensor
        def _(pe):
            def turn(out, src):
                for i in range(8):
                    mm = pe.transpose(out[:, i // 4, (i % 4) * P:(i % 4 + 1) * P], src(i), ident[:])
                return mm

            def keys(b, j):
                wait(pe, S["k_exp"], 4 * b + j)
                for n in range(2):
                    mm = three_pass(pe, work_ps[0][:, n], pair(wk, slice(None), slice(j * P, (j + 1) * P)),
                                    pair(ch, slice(None), slice(n * 512, n * 512 + 512)))
                mm.then_inc(S["k_mm"], 1)

            def turn_keys(b, j):
                wait(pe, S["k_exp"], 4 * b + j + 1)
                turn(turn_ps, lambda i: ke[:, j % 2, i * P:(i + 1) * P]).then_inc(S["k_turned"], 1)

            def queries(b, u):
                wait(pe, S["q_sub"], 4 * b + u)
                for n in range(2):
                    t = 2 * u + n
                    mm = three_pass(pe, work_ps[1][:, n], pair(xh, slice(None), slice(t * P, (t + 1) * P)),
                                    pair(wq, slice(None), slice(None)))
                mm.then_inc(S["q_mm"], 1)

            def turn_queries(b, u):
                wait(pe, S["q_norm"], 4 * b + u + 1)
                turn(turn_ps, lambda i: qs[:, u % 2, i // 4, (i % 4) * P:(i % 4 + 1) * P]).then_inc(S["q_turned"], 1)

            def out_rows(b, t):
                for j in range(HT):
                    mm = pe.matmul(acc_ps[:, t // 4, (t % 4) * P:(t % 4 + 1) * P], qt[:, t // 2, t % 2, j, :],
                                   mt[:, j, :], start=j == 0, stop=j == HT - 1)
                if t % 2:
                    mm.then_inc(S["out_mm"], 1)

            def turn_out(b):
                wait(pe, S["o_scaled"], b + 1)
                turn(turn_ps, lambda i: ot2[:, i, :]).then_inc(S["o_turned"], 1)

            def contexts(b, columns, done):
                for t in range(NT):
                    mm = pe.matmul(acc_ps[:, 0, columns], ct[:, t, :], kt[:, t, columns], start=t == 0,
                                   stop=t == NT - 1)
                if done:
                    mm.then_inc(S["g_mm"], 1)

            def body(b, prev, prev2, ahead, last):
                wait(pe, S["qt_copied"], 4 * b)
                wait(pe, S["ctx_loaded"], 16 * b + 16)
                turn(turn_ps, lambda i: cx[:, i * P:(i + 1) * P]).then_inc(S["ctx_turned"], 1)
                for i in range(4):
                    if i == 0:
                        wait(pe, S["x_tail"], b + 1)
                    queries(b, i)
                    if i == 0:
                        wait(pe, S["c_tail"], b + 1)
                        wait(pe, S["m_diag"], 2 * b)
                    keys(b, i)
                    if i >= 1:
                        if i == 1:
                            wait(pe, S["ct_copied"], b + 1)
                            wait(pe, S["x_new"], b - 1)
                        else:
                            wait(pe, S["qt_copied"], 4 * b + i - 1)
                        turn_keys(b, i - 1)
                    if prev:
                        if i == 0:
                            wait(pe, S["g_copied"], b)
                        if i == 2:
                            wait(pe, S["o_bias"], 2 * (b - 1))
                        out_rows(b - 1, 2 * i)
                    if i == 0 and prev2:
                        wait(pe, S["ct_copied"], b + 1)
                        turn_out(b - 2)
                    if prev and i < 3:
                        out_rows(b - 1, 2 * i + 1)
                    if i >= 1:
                        wait(pe, S["kt_copied"], 4 * b + i)
                        turn_queries(b, i - 1)
                if prev:
                    out_rows(b - 1, 7)
                wait(pe, S["qt_copied"], 4 * b + 3)
                turn_keys(b, 3)
                wait(pe, S["o_bias"], 2 * b - 1)
                contexts(b, slice(0, 3 * P), False)
                wait(pe, S["kt_copied"], 4 * b + 4)
                contexts(b, slice(3 * P, 4 * P), True)
                turn_queries(b, 3)
                wait(pe, S["g_copied"], b + 1)
                wait(pe, S["k_exp"], 4 * b + 4)
                for j in range(HT):
                    mm = pe.matmul(work_ps[0][:, j // 2, (j % 2) * 256:(j % 2 + 1) * 256], gt[:, j * P:(j + 1) * P],
                                   bvo[:, j * 256:(j + 1) * 256], start=True, stop=True)
                mm.then_inc(S["m_mm"], 1)

            def tail(b):
                wait(pe, S["m_diag"], 2 * b)
                wait(pe, S["qt_copied"], 4 * b)
                wait(pe, S["g_copied"], b)
                for t in range(NT):
                    out_rows(b - 1, t)
                    if t == 3:
                        turn_out(b - 2)
                pe.wait_ge(S["q_sub"], 4 * NB)
                lora_turn_b(pe, lora, lora_slots, ident)
                wait(pe, S["x_new"], b - 1)
                turn_out(b - 1)
                pe.wait_ge(lora["S"]["a_tail"], 1)
                pe.wait_ge(lora["S"]["b_tail"], lora["KT"])
                for j in range(2):
                    lora_products(pe, env, lora, j)
            skewed(pe, body, tail)

        @block.scalar
        def _(act):
            def head_of(b, t, src, name, ready, read):
                wait(act, *ready)
                wait(act, *read)
                act.activation(t[0][:], src, ACT.Copy).then_inc(S[name + "_head"], 1)

            def heads(b):
                head_of(b, xh, xn[:], "x", (S["xn_done"], b + 1), (S["q_mm"], 4 * b))
                head_of(b, ch, cx[:], "c", (S["ctx_loaded"], 16 * b + 16), (S["k_mm"], 4 * b))

            def exp_keys(b, j):
                wait(act, S["k_max"], 4 * b + j + 1)
                wait(act, S["k_turned"], 4 * b + j - 1)
                act.activation(ke[:, j % 2, :], flat(work_ps[0][:]), ACT.Exp,
                               bias=kmax[:, j:j + 1], accum_out=ksum[:, j:j + 1]).then_inc(S["k_exp"], 1)

            def copy_keys(b, j):
                wait(act, S["k_turned"], 4 * b + j + 1)
                wait(act, S["g_mm"], b)
                act.activation(kt[:, :, j * P:(j + 1) * P], turn_ps[:].rearrange("p a (t o) -> p (a t) o", o=P),
                               ACT.Copy).then_inc(S["kt_copied"], 1)

            def exp_queries(b, u):
                wait(act, S["q_sub"], 4 * b + u + 1)
                q = flat(qs[:, u % 2])
                act.activation(q, q, ACT.Exp).then_inc(S["q_exp"], 1)

            def copy_queries(b, u):
                wait(act, S["q_turned"], 4 * b + u + 1)
                wait(act, S["out_mm"], 4 * b + u - 3)
                act.activation(qt[:, u].rearrange("p t j n -> p (t j n)"), flat(turn_ps[:]),
                               ACT.Copy).then_inc(S["qt_copied"], 1)

            def root(b, ahead):
                wait(act, S["o_ss"], b + 1)
                act.activation(nrm[:], ss[:], ACT.Sqrt).then_inc(S["o_root"], 1)
                if ahead:
                    row_roots(act, b + 3)
                wait(act, S["warmed"], b + 2)
                act.activation(env["warm"][:], ident[:, 0:1], ACT.Exp).then_inc(S["warmed"], 1)

            def body(b, prev, prev2, ahead, last):
                wait(act, S["ctx_turned"], b + 1)
                wait(act, S["g_mm"], b)
                act.activation(ct[:].rearrange("p t c -> p (t c)"), flat(turn_ps[:]),
                               ACT.Copy).then_inc(S["ct_copied"], 1)
                for i in range(4):
                    if i >= 1:
                        copy_keys(b, i - 1)
                    exp_keys(b, i)
                    if i < 3:
                        exp_queries(b, i)
                    if i >= 1:
                        copy_queries(b, i - 1)
                    if i == 3:
                        exp_queries(b, i)
                if not last:
                    heads(b + 1)
                copy_keys(b, 3)
                wait(act, S["g_mm"], b + 1)
                act.activation(gt[:], acc_ps[:, 0], ACT.Copy).then_inc(S["g_copied"], 1)
                copy_queries(b, 3)
                if prev:
                    root(b - 1, ahead)
                else:
                    row_roots(act, 2)
                    act.wait_ge(S["warmed"], 1)
                    act.activation(env["warm"][:], ident[:, 0:1], ACT.Exp).then_inc(S["warmed"], 1)
            def tail(b):
                act.wait_ge(S["g_mm"], NB)
                lora_head_a(act, lora)
                root(b - 1, False)
                lora_head_b(act, lora, lora_slots)
            heads(0)
            skewed(act, body, tail)

        @block.vector
        def _(dve):
            def max_keys(b, j):
                wait(dve, S["k_mm"], 4 * b + j + 1)
                wait(dve, S["k_exp"], 4 * b + j - 3)
                dve.tensor_reduce(kmax[:, j:j + 1], work_ps[0][:], mybir.AxisListType.XY, ALU.max,
                                  negate=True).then_inc(S["k_max"], 1)

            def max_queries(b, u):
                wait(dve, S["q_mm"], 4 * b + u + 1)
                dve.tensor_reduce(qmax[:, u], work_ps[1][:].rearrange("p t (h d) -> p (t h) d", d=DIM_HEAD),
                                  AX_X, ALU.max).then_inc(S["q_max"], 1)

            def shift_queries(b, u):
                q = work_ps[1][:].rearrange("p t (h d) -> p (t h) d", d=DIM_HEAD)
                wait(dve, S["q_max"], 4 * b + u + 1)
                wait(dve, S["q_turned"], 4 * b + u - 1)
                dve.tensor_tensor(qs[:, u % 2].rearrange("p t (h d) -> p (t h) d", d=DIM_HEAD), q,
                                  qmax[:, u].rearrange("p t h -> p (t h)").unsqueeze(2)
                                  .broadcast_to([P, 2 * HEADS, DIM_HEAD]), ALU.subtract).then_inc(S["q_sub"], 1)

            def sum_queries(b, u):
                wait(dve, S["q_exp"], 4 * b + u + 1)
                wait(dve, S["q_norm"], 4 * b + u - 3)
                dve.tensor_reduce(qsum[:, u], qs[:, u % 2].rearrange("p t (h d) -> p (t h) d", d=DIM_HEAD), AX_X,
                                  ALU.add).then_inc(S["q_sum"], 1)
                wait(dve, S["q_sum"], 4 * b + u + 1)
                dve.reciprocal(qrec[:, u], qsum[:, u]).then_inc(S["q_rec"], 1)

            def add_bias(b, half):
                wait(dve, S["out_mm"], 4 * b + 2 * half + 2)
                wait(dve, S["o_scaled"], b)
                dve.tensor_tensor(ot[:, 4 * half:4 * half + 4], acc_ps[:, half].rearrange("p (t o) -> p t o", o=P),
                                  bo_row[:].unsqueeze(1).broadcast_to([P, NT // 2, P]), ALU.add).then_inc(
                    S["o_bias"], 1)

            def square(b):
                wait(dve, S["o_bias"], 2 * b + 2)
                wait(dve, S["o_ss"], b)
                dve.tensor_tensor(osq[:], ot[:], ot[:], ALU.mult).then_inc(S["o_sq"], 1)

            def row_lengths(b):
                wait(dve, S["o_sq"], b + 1)
                wait(dve, S["o_root"], b)
                dve.tensor_reduce(ss[:], osq[:], AX_X, ALU.add).then_inc(S["o_ss"], 1)

            def row_scales(b):
                wait(dve, S["o_root"], b + 1)
                dve.tensor_scalar(nrm[:], nrm[:], 1e-12, None, ALU.max).then_inc(S["o_floor"], 1)
                wait(dve, S["o_floor"], b + 1)
                wait(dve, S["o_scaled"], b)
                dve.reciprocal(rn[:], nrm[:]).then_inc(S["o_rec"], 1)

            def update(b):
                wait(dve, S["o_turned"], b + 1)
                wait(dve, S["xn_done"], b + 1)
                at = X[:, b, :]
                dve.scalar_tensor_tensor(at, flat(turn_ps[:]), gate_g[:, 1:2], at,
                                         ALU.mult, ALU.add).then_inc(S["x_new"], 1)

            def body(b, prev, prev2, ahead, last):
                for i in range(4):
                    max_queries(b, i)
                    if i == 2:
                        wait(dve, S["ctx_loaded"], 16 * b + 16)
                    if i == 3:
                        wait(dve, S["ctx_stats"], 2 * b + 2)
                    max_keys(b, i)
                    shift_queries(b, i)
                    if i == 0 and prev2:
                        update(b - 2)
                    if i == 1 and not last:
                        norm_x(dve, b + 1)
                    if i == 2:
                        for h in range(2):
                            dve.bn_stats(c6[:, 6 * h:6 * h + 6], cx[:, 512 * h:512 * h + 512]).then_inc(
                                S["ctx_stats"], 1)
                    if i == 3:
                        dve.bn_aggr(c2[:], c6[:]).then_inc(S["ctx_aggr"], 1)
                        if prev:
                            add_bias(b - 1, 0)
                    sum_queries(b, i)
                wait(dve, S["ctx_aggr"], b + 1)
                dve.tensor_copy(cmv[:, b, :], c2[:]).then_inc(S["ctx_kept"], 1)
                if prev:
                    add_bias(b - 1, 1)
                if prev2:
                    updated_stats(dve, env, b - 2, S, env["mv2"])
                if prev:
                    square(b - 1)
                if ahead:
                    row_variances(dve, b + 2)
                if not prev2 and prev:
                    for loaded in x_loaded[4:]:
                        dve.wait_ge(loaded, 16)
                wait(dve, S["k_exp"], 4 * b + 4)
                dve.reciprocal(krec[:], ksum[:]).then_inc(S["k_rec"], 1)
                if prev:
                    row_lengths(b - 1)
                wait(dve, S["m_mm"], b + 1)
                wait(dve, S["k_rec"], b + 1)
                wait(dve, S["out_mm"], 4 * b)
                mps = work_ps[0][:].rearrange("p a (j e) -> p (a j) e", e=256)
                for i in range(2):
                    rows = slice(64 * i, 64 * i + 64)
                    dve.scalar_tensor_tensor(mt[rows], mps[rows, :, i * P:(i + 1) * P], SCALE,
                                             krec[rows].unsqueeze(2).broadcast_to([64, HT, P]),
                                             ALU.mult, ALU.mult).then_inc(S["m_diag"], 1)
                if prev:
                    row_scales(b - 1)
                if ahead:
                    row_rescales(dve, b + 2)

            def tail(b):
                for half in range(2):
                    add_bias(b - 1, half)
                    tiles = slice(4 * half, 4 * half + 4)
                    dve.wait_ge(S["o_bias"], 2 * b + half - 1)
                    dve.tensor_tensor(osq[:, tiles], ot[:, tiles], ot[:, tiles], ALU.mult).then_inc(S["o_sq"], 1)
                dve.wait_ge(S["o_sq"], b + 1)
                dve.tensor_reduce(ss[:], osq[:], AX_X, ALU.add).then_inc(S["o_ss"], 1)
                update(b - 2)
                row_scales(b - 1)
                dve.wait_ge(S["o_rec"], b)
                dve.tensor_tensor(ot2[:], ot[:], rn[:].unsqueeze(2).broadcast_to([P, NT, P]), ALU.mult).then_inc(
                    S["o_scaled"], 1)
                lora_tail_b(dve, lora, lora_slots)
                updated_stats(dve, env, b - 2, S, env["mv2"])
                update(b - 1)
                updated_stats(dve, env, b - 1, S, env["mv2"])
            skewed(dve, body, tail)


def paired(eng, body, count, outside=1):
    body(0, 0, True, 3 if outside > 1 else False)
    with eng.Fori(0, (count - 1 - outside) // 2) as i:
        body(2 * i + 1, 1, False, 3 if outside > 1 else False)
        body(2 * i + 2, 0, False, 3 if outside > 1 else False)
    for b in range(count - outside, count):
        body(b, b % 2, False, count - 1 - b if outside > 1 else True)


def lora_inputs(env, layer):
    if layer == 0:
        return env["L0_ffn_A"], env["L0_ffn_Bf"], [env["L0_ffn_coeffs"], env["L0_ffn_scales"]]
    return env["L1_ffn_lora_A"], env["L1_ffn_lora_B"], [env["L1_ffn_lora_weights"]]


def load_lora(sp, env, layer):
    A, B, factors = lora_inputs(env, layer)
    E, R, N = A.shape
    done = env["lora_loaded"][layer]
    for n, f in enumerate(factors):
        sp.dma_start(env["fac"][layer][:, n], f.unsqueeze(0).broadcast_to([P, E])).then_inc(done, 16)
    b_raw = env["lora_b"][:].rearrange("p k n -> p (k n)")[:, 0:E * N * R // P]
    sp.dma_start(b_raw.rearrange("p (e i) -> p e i", e=E), B.rearrange("e (p i) r -> p e (i r)", p=P)).then_inc(
        done, 16)
    sp.dma_start(env["lora_a"][:, 0:E * R // P], A.rearrange("e r d -> (e r) d").rearrange("(k p) d -> p k d", p=P)
                 ).then_inc(done, 16)


def lora_prep(nc, env, layer, free, b_at):
    A, B, factors = lora_inputs(env, layer)
    E, R, N = A.shape
    KT, NT = E * R // P, N // P
    k_n = lambda t: t[:, 0:KT]
    L = {"KT": KT, "NT": NT, "R": R, "E": E, "layer": layer}
    L["bt"] = (k_n(env["lora_b_head"]), over(nc, f"l{layer}_bt_l", [P, KT, N], F32R, free))
    L["at"] = (over(nc, f"l{layer}_at_h", [P, KT, N], F32R, free + 8 * N), k_n(env["lora_a_tail"]))
    L["a_raw"] = k_n(env["lora_a"])
    L["b_raw"] = k_n(env["lora_b"]).rearrange("p k n -> p (k n)").rearrange("p (e i r) -> p e i r", e=E, r=R)
    L["b_scaled"] = over(nc, f"l{layer}_b_scaled", [P, KT, N], F32, b_at)[:].rearrange(
        "p k n -> p (k n)").rearrange("p (i k) -> p i k", i=NT)
    L["loaded"] = (env["lora_loaded"][layer], 16 * (len(factors) + 2))
    names = "fac_done b_scaled b_turned b_head b_tail a_head a_tail products"
    L["S"] = {n: env["lora_sem"](f"l{layer}_{n}") for n in names.split()}
    return L


def lora_scale_b(pool, env, L):
    fac, S = env["fac"][L["layer"]], L["S"]
    pool.wait_ge(*L["loaded"])
    if L["layer"] == 0:
        pool.tensor_tensor(fac[:, 0], fac[:, 0], fac[:, 1], ALU.mult).then_inc(S["fac_done"], 1)
    else:
        pool.tensor_scalar(fac[:, 0], fac[:, 0], 32 / L["R"], None, ALU.mult).then_inc(S["fac_done"], 1)
    pool.wait_ge(S["fac_done"], 1)
    pool.tensor_tensor(L["b_scaled"].rearrange("p i (e r) -> p e i r", r=L["R"]), L["b_raw"],
                       fac[:, 0].unsqueeze(2).unsqueeze(3).broadcast_to([P, L["E"], L["NT"], L["R"]]),
                       ALU.mult).then_inc(S["b_scaled"], 1)


def lora_tail_a(pool, L):
    pool.wait_ge(L["S"]["a_head"], 1)
    pool.tensor_tensor(L["at"][1], L["a_raw"], f32(L["at"][0][:]), ALU.subtract).then_inc(L["S"]["a_tail"], 1)


def lora_head_a(act, L):
    act.wait_ge(*L["loaded"])
    act.activation(L["at"][0][:], L["a_raw"], ACT.Copy).then_inc(L["S"]["a_head"], 1)


def lora_turn_b(pe, L, slots, ident):
    pe.wait_ge(L["S"]["b_scaled"], 1)
    for k in range(L["KT"]):
        for i in range(L["NT"]):
            mm = pe.transpose(slots[k][:, i // 4, (i % 4) * P:(i % 4 + 1) * P],
                              L["b_scaled"][:, i, k * P:(k + 1) * P], ident[:])
        mm.then_inc(L["S"]["b_turned"], 1)


def lora_head_b(act, L, slots):
    for k in range(L["KT"]):
        act.wait_ge(L["S"]["b_turned"], k + 1)
        act.activation(L["bt"][0][:, k].rearrange("k (o i) -> k i o", i=L["NT"]),
                       slots[k][:].rearrange("p a (i o) -> p (a i) o", o=P), ACT.Copy).then_inc(L["S"]["b_head"], 1)


def lora_tail_b(dve, L, slots):
    for k in range(L["KT"]):
        dve.wait_ge(L["S"]["b_head"], k + 1)
        dve.tensor_tensor(L["bt"][1][:, k].rearrange("k (o i) -> k i o", i=L["NT"]),
                          slots[k][:].rearrange("p a (i o) -> p (a i) o", o=P),
                          f32(L["bt"][0][:, k]).rearrange("k (o i) -> k i o", i=L["NT"]),
                          ALU.subtract).then_inc(L["S"]["b_tail"], 1)


def lora_products(pe, env, L, j):
    KT = L["KT"]
    for n in range(2):
        for k in range(KT):
            mm = three_pass(pe, env["work_ps"][j % 2][:, n], pair(L["bt"], slice(None), k, slice(j * P, (j + 1) * P)),
                            pair(L["at"], slice(None), k, slice(n * 512, n * 512 + 512)),
                            first=k == 0, last=k == KT - 1)
    mm.then_inc(L["S"]["products"], 1)


def load_w(sp, env, layer):
    for t in range(env["w_rows"].shape[1]):
        sp.dma_start(env["w_rows"][:, t], env[f"L{layer}_ffn_W"][t * P:(t + 1) * P]).then_inc(
            env["w_loaded"][layer], 16)


def project(pe, env, n, slot, src, done):
    ALL = slice(None)
    for h in range(2):
        mm = three_pass(pe, slot[:, h], pair(env["x_wts"], ALL, n), pair(src, ALL, slice(512 * h, 512 * h + 512)))
    mm.then_inc(done, 1)


def project_values(pe, env, slot, ch, done):
    ALL = slice(None)
    for i in range(8):
        mm = three_pass(pe, slot[:, i // 4, (i % 4) * P:(i % 4 + 1) * P], pair(ch, ALL, slice(i * P, (i + 1) * P)),
                        pair(env["x_wts"], ALL, 2))
    mm.then_inc(done, 1)


def tail_of(eng, S, b, t, src, name):
    wait(eng, S[name + "_head"], b + 1)
    eng.tensor_tensor(t[1][:], src, f32(t[0][:]), ALU.subtract).then_inc(S[name + "_tail"], 1)


def query_variances(dve, out, var):
    return dve.tensor_scalar(out, var, 1 + LN_EPS, LN_EPS * LN_EPS, ALU.mult, ALU.add)


class Ahead:

    def __init__(self, env):
        self.env, self.S = env, env["attention_sems"]
        self.cx, self.xn, *halves = env["stage"]
        self.xq, self.ch, self.kn = halves[0:2], halves[2:4], halves[4:6]
        self.kn_f = env["lora_a"][:, 1]
        self.var, self.root, self.scale = env["st"][:, 1, 0:2], env["st"][:, 2, 0:2], env["st"][:, 1, 2:4]

    def vector(self, dve):
        env, S = self.env, self.S
        mv, cmv = env["mv"], env["cmv"]
        query_variances(dve, self.var[:, 0:1], mv[:, 0, 1:2]).then_inc(S["ahead_var"], 1)
        dve.tensor_scalar(self.var[:, 1:2], cmv[:, 0, 1:2], LN_EPS, None, ALU.add).then_inc(S["ahead_var"], 1)
        dve.wait_ge(S["ahead_root"], 1)
        dve.reciprocal(self.scale, self.root).then_inc(S["ahead_scale"], 1)
        dve.wait_ge(S["ahead_scale"], 1)
        dve.wait_ge(env["ctx_ahead"], 16)
        dve.tensor_scalar(self.xn[:], env["X"][:, 0, :], mv[:, 0, 0:1], self.scale[:, 0:1],
                          ALU.subtract, ALU.mult).then_inc(S["xn_done"], 1)
        dve.tensor_scalar(self.kn_f, self.cx[:], cmv[:, 0, 0:1], self.scale[:, 1:2],
                          ALU.subtract, ALU.mult).then_inc(S["ahead_kn"], 1)
        tail_of(dve, S, 0, self.xq, self.xn[:], "xq")
        tail_of(dve, S, 0, self.kn, self.kn_f, "kn")

    def scalar(self, act):
        S = self.S
        act.wait_ge(S["ahead_var"], 2)
        act.activation(self.root, self.var, ACT.Sqrt).then_inc(S["ahead_root"], 1)
        act.wait_ge(self.env["ctx_ahead"], 16)
        for t, src, name, ready in ((self.ch, self.cx[:], "c", None), (self.xq, self.xn[:], "xq", "xn_done"),
                                    (self.kn, self.kn_f, "kn", "ahead_kn")):
            if ready:
                act.wait_ge(S[ready], 1)
            act.activation(t[0][:], src, ACT.Copy).then_inc(S[name + "_head"], 1)

    def gpsimd(self, pool):
        tail_of(pool, self.S, 0, self.ch, self.cx[:], "c")

    def tensor(self, pe):
        env, S = self.env, self.S
        pe.wait_ge(S["xq_tail"], 1)
        project(pe, env, 0, env["work_ps"][0], self.xq, S["q_mm"])
        pe.wait_ge(S["kn_tail"], 1)
        project(pe, env, 1, env["turn_ps"], self.kn, S["k_mm"])
        pe.wait_ge(S["c_tail"], 1)
        project_values(pe, env, env["acc_ps"], self.ch, S["sp_mm"])


def ffn(nc, ctx, env, layer):
    X, ident, tg, work_ps, turn_ps = env["X"], env["ident"], env["tg"], env["work_ps"], env["turn_ps"]
    mv, mv_next = env["mv2"], env["mv"]
    NB, N = X.shape[1], X.shape[2]
    NT = N // P
    gate = tg[:, 6 + layer:7 + layer]
    A, B, factors = lora_inputs(env, layer)
    bias, acc_ps = env[f"L{layer}_ffn_bias"], env["acc_ps"]
    E, RANK = A.shape[0], A.shape[1]
    KT = E * RANK // P
    st = env["st"]
    with ExitStack() as c:
        sb = lambda n, s, d=F32: c.enter_context(nc.sbuf_tensor(f"f{layer}_" + n, s, d))
        two = lambda n, s: (sb(n + "_h", s, F32R), sb(n + "_l", s, F32R))
        sem = lambda n: c.enter_context(nc.semaphore(f"f{layer}_" + n))
        xt = [two(f"xt{i}", [P, NT, P]) for i in range(2)]
        xn = sb("xn", [P, N])
        wt = two("wt", [P, NT, N])
        gbias = sb("gbias", [P, N])

        lora = env["lora"]
        rows = [env["w_rows"][:, j] for j in range(NT)]
        turned_ps = (turn_ps, acc_ps)
        by_o = lambda ps: ps[:].rearrange("p a (i o) -> p (a i) o", o=P)
        x_wts, x_ps = env["x_wts"], acc_ps[:, 0, 0:3 * P].rearrange("p (k n) -> p k n", n=P)
        names = ("bias_loaded w_sum w_turned "
                 "w_head w_tail bias_done var_eps root rstd_done x_turned x_head x_tail "
                 "xn_done x_biased turned xt_head xt_tail mm x_new row_stats row_aggr row_kept pair_clear stored")
        S = {n: sem(n) for n in names.split()}
        block = c.enter_context(nc.Block())

        @block.sync
        def _(sp):
            sp.dma_start(gbias[:], bias.unsqueeze(0).broadcast_to([P, N])).then_inc(S["bias_loaded"], 16)

            if layer == 1:
                def body(b, par, first, last):
                    wait(sp, S["x_new"], b + 1)
                    sp.dma_start(env["out"][b], X[:, b, :]).then_inc(S["stored"], 16)
                paired(sp, body, NB)
                sp.wait_ge(S["stored"], 16 * NB)
            else:
                sp.wait_ge(S["w_turned"], NT)
                sp.dma_start(env["stage"][0][:], env["ctx_dram"][0]).then_inc(env["ctx_ahead"], 16)

        @block.gpsimd
        def _(pool):
            pool.wait_ge(S["bias_loaded"], 16)
            pool.tensor_tensor(gbias[:], gbias[:], gate.broadcast_to([P, N]), ALU.mult).then_inc(S["bias_done"], 1)
            if layer == 0:
                Ahead(env).gpsimd(pool)

        @block.tensor
        def _(pe):
            def turn_w(j):
                pe.wait_ge(S["w_sum"], j + 1)
                if j >= 2:
                    pe.wait_ge(S["w_tail"], j - 1)
                for i in range(NT):
                    mm = pe.transpose(turned_ps[j % 2][:, i // 4, (i % 4) * P:(i % 4 + 1) * P],
                                      rows[j][:, i * P:(i + 1) * P], ident[:])
                mm.then_inc(S["w_turned"], 1)

            def turn(b, slot=turn_ps):
                wait(pe, S["xn_done"], b + 1)
                wait(pe, S["xt_tail"], b)
                for i in range(NT):
                    mm = pe.transpose(slot[:, i // 4, (i % 4) * P:(i % 4 + 1) * P], xn[:, i * P:(i + 1) * P],
                                      ident[:])
                mm.then_inc(S["turned"], 1)

            if layer == 0:
                pe.wait_ge(env["x_small_loaded"], 96)
                for n in range(3):
                    mm = pe.transpose(x_ps[:, n], env["x_raw"][:, n], ident[:])
                mm.then_inc(S["x_turned"], 1)

            for j in range(1, NT):
                if j >= 2:
                    pe.wait_ge(S["w_sum"], j - 1)
                    lora_products(pe, env, lora, j)
                if layer == 0 and j == 2:
                    pe.wait_ge(S["x_tail"], 1)
                if j == NT - 1:
                    pe.wait_ge(S["w_sum"], NT - 1)
                    turn(0, work_ps[0])
                turn_w(j - 1)
            turn_w(NT - 1)

            def body(b, par, first, last):
                if not last and not first:
                    turn(b + 1)
                wait(pe, S["xt_tail"], b + 1)
                if first:
                    wait(pe, S["w_tail"], NT)
                for j in range(NT):
                    if first and j == NT // 2:
                        turn(1)
                    for n in range(2):
                        mm = three_pass(pe, work_ps[par][:, n], pair(xt[par], slice(None), j),
                                        pair(wt, slice(None), j, slice(n * 512, n * 512 + 512)),
                                        first=j == 0, last=j == NT - 1)
                mm.then_inc(S["mm"], 1)
            paired(pe, body, NB)
            if layer == 0:
                wait(pe, S["x_new"], NB - 1)
                Ahead(env).tensor(pe)

        @block.scalar
        def _(act):
            if layer == 0:
                act.wait_ge(S["x_turned"], 1)
                act.activation(x_wts[0][:], x_ps, ACT.Copy).then_inc(S["x_head"], 1)
            def head(b, par, slot=turn_ps):
                wait(act, S["turned"], b + 1)
                act.activation(xt[par][0][:].rearrange("p t n -> p (t n)"), slot[:].rearrange("p a n -> p (a n)"),
                               ACT.Copy).then_inc(S["xt_head"], 1)

            def body(b, par, first, last):
                if not first:
                    head(b, par)

            for j in range(NT):
                if j == NT - 2:
                    head(0, 0, work_ps[0])
                if j == 1:
                    act.wait_ge(S["var_eps"], 1)
                    act.activation(st[:, 2, :], st[:, 1, :], ACT.Sqrt).then_inc(S["root"], 1)
                act.wait_ge(S["w_turned"], j + 1)
                act.activation(wt[0][:, :, j * P:(j + 1) * P], by_o(turned_ps[j % 2]), ACT.Copy).then_inc(
                    S["w_head"], 1)
            paired(act, body, NB)
            if layer == 0:
                Ahead(env).scalar(act)

        @block.vector
        def _(dve):
            def add_w(j):
                dve.wait_ge(lora["S"]["products"], max(j + 1, 2))
                if j == 0:
                    dve.wait_ge(env["w_loaded"][layer], 16 * NT)
                dve.tensor_tensor(rows[j], work_ps[j % 2][:].rearrange("p a n -> p (a n)"), rows[j],
                                  ALU.add).then_inc(S["w_sum"], 1)

            def tail_w(j):
                cols = slice(j * P, (j + 1) * P)
                dve.wait_ge(S["w_head"], j + 1)
                dve.tensor_tensor(wt[1][:, :, cols], by_o(turned_ps[j % 2]), f32(wt[0][:, :, cols]),
                                  ALU.subtract).then_inc(S["w_tail"], 1)
            def norm_x(b):
                wait(dve, S["turned"], b)
                dve.tensor_scalar(xn[:], X[:, b, :], mv[:, b, 0:1], st[:, 0, bass.ds(b, 1)],
                                  ALU.subtract, ALU.mult).then_inc(S["xn_done"], 1)
                wait(dve, S["xn_done"], b + 1)
                dve.tensor_tensor(X[:, b, :], X[:, b, :], gbias[:], ALU.add).then_inc(S["x_biased"], 1)

            def tail(b, par, slot=turn_ps):
                wait(dve, S["xt_head"], b + 1)
                dve.tensor_tensor(xt[par][1][:].rearrange("p t n -> p (t n)"), slot[:].rearrange("p a n -> p (a n)"),
                                  f32(xt[par][0][:]).rearrange("p t n -> p (t n)"), ALU.subtract).then_inc(
                    S["xt_tail"], 1)

            def body(b, par, first, left):
                if left >= 1:
                    tail(b + 1, 1 - par)
                if left >= 2:
                    norm_x(b + 2)
                if layer == 0 and left == 0:
                    Ahead(env).vector(dve)
                wait(dve, S["mm"], b + 1)
                wait(dve, S["x_biased"], b + 1)
                dve.scalar_tensor_tensor(X[:, b, :], work_ps[par][:].rearrange("p a n -> p (a n)"), gate, X[:, b, :],
                                         ALU.mult, ALU.add).then_inc(S["x_new"], 1)
                if layer == 0:
                    updated_stats(dve, env, b, S, mv_next)
            add_w(0)
            add_w(1)
            if layer == 0:
                dve.wait_ge(S["x_head"], 1)
                dve.tensor_tensor(x_wts[1][:], x_ps, f32(x_wts[0][:]), ALU.subtract).then_inc(S["x_tail"], 1)
            dve.tensor_scalar(st[:, 1, :], mv[:, :, 1], LN_EPS, None, ALU.add).then_inc(S["var_eps"], 1)
            tail_w(0)
            for j in range(2, NT):
                add_w(j)
                if j == NT - 1:
                    tail(0, 0, work_ps[0])
                tail_w(j - 1)
                if j == 2:
                    dve.wait_ge(S["root"], 1)
                    dve.reciprocal(st[:, 0, :], st[:, 2, :]).then_inc(S["rstd_done"], 1)
                if j == 4:
                    dve.wait_ge(S["rstd_done"], 1)
                    dve.wait_ge(S["bias_done"], 1)
                    norm_x(0)
            tail_w(NT - 1)
            norm_x(1)
            paired(dve, body, NB, outside=3)


def xattn1(nc, ctx, env):
    X, ident, tg = env["X"], env["ident"], env["tg"]
    work_ps, turn_ps, acc_ps = env["work_ps"], env["turn_ps"], env["acc_ps"]
    mv, mv_next, cmv = env["mv"], env["mv2"], env["cmv"]
    NB, N = X.shape[1], X.shape[2]
    NT = N // P
    VW = 2 * P + 2
    gate = tg[:, 5:6]
    with ExitStack() as c:
        sb = lambda n, s, d=F32: c.enter_context(nc.sbuf_tensor("x_" + n, s, d))
        two = lambda n, s: (sb(n + "_h", s, F32R), sb(n + "_l", s, F32R))
        wts, bq_bk, bs_row = env["x_wts"], env["bq_bk"], env["bs_row"]
        qp_at = -(-nc.sbuf_base // 32) * 32
        qp, kp = two("qp", [P, N]), two("kp", [P, N])
        v = [two(f"v{i}", [P, NT, VW]) for i in range(2)]
        sc = sb("sc", [P, 6, NB])

        cx, xn, *halves = env["stage"]
        xq, ch, kn = halves[0:2], halves[2:4], halves[4:6]
        kn_f = [sb(f"kn_f{i}", [P, N]) for i in (1, 0)][::-1]
        lora = env["lora"] = lora_prep(nc, env, 1, qp_at, nc.sbuf_base - 4 * N)
        tiles = lambda t, k: t[:, k].rearrange("p (t n) -> p t n", n=P)
        sp32, sq32 = tiles(env["lora_a"], 0), tiles(env["lora_b"], 0)
        p, pt = sb("p", [P, 2, N]), [two(f"pt{i}", [P, NT, P]) for i in range(2)]
        smax, rcp = sb("smax", [P, NT]), sb("rcp", [P, NT])
        mean_sq = sb("mean_sq", [P, 2, NT, P])
        std, u = env["lora_a"][:, 1], env["lora_b"][:, 1]
        edge = u[:, 0:4 * NT].rearrange("p (k t e) -> p k t e", k=2, t=NT)
        S = env["attention_sems"]
        block = c.enter_context(nc.Block())
        flat = lambda ap: ap.rearrange("p a n -> p (a n)")

        def wait_ctx(eng, b):
            if not (isinstance(b, int) and b == 0):
                eng.wait_ge(S["ctx_loaded"], 16 * b)

        @block.sync
        def _(sp):
            def body(b, par, first, last):
                if not first:
                    wait(sp, S["c_tail"], b)
                    wait(sp, S["knf_done"], b)
                    sp.dma_start(cx[:], env["ctx_dram"][b]).then_inc(S["ctx_loaded"], 16)
            paired(sp, body, NB)
            sp.wait_ge(S["v_tail"], 2 * NB)
            load_lora(sp, env, 1)
            sp.wait_ge(S["c_tail"], NB)
            sp.wait_ge(S["knf_done"], NB)
            sp.wait_ge(S["sp_mm"], NB)
            sp.wait_ge(S["q_mm"], NB)
            sp.wait_ge(S["k_mm"], NB)
            load_w(sp, env, 1)

        @block.gpsimd
        def _(pool):
            def variance(b, tiles=NT):
                wait(pool, S["pv_out"], 8 * b + tiles)
                mean, sq = (flat(mean_sq[:, k, 0:tiles]) for k in range(2))
                pool.tensor_tensor(std[:, 0:tiles * P], mean, mean, ALU.mult).then_inc(S["mean2"], 1)
                wait(pool, S["mean2"], b + 1)
                pool.tensor_tensor(std[:, 0:tiles * P], sq, std[:, 0:tiles * P], ALU.subtract).then_inc(S["var"], 1)

            def values(b, par):
                wait(pool, S["sp_done"], b + 1)
                wait(pool, S["v_tail"], 2 * b)
                pool.tensor_tensor(sq32[:], sp32[:], sp32[:], ALU.mult).then_inc(S["sq_done"], 1)
                for k, src in enumerate((sp32, sq32)):
                    wait(pool, S["v_head"], 2 * b + k + 1)
                    cols = slice(k * P, (k + 1) * P)
                    pool.tensor_tensor(v[par][1][:, :, cols], src[:], f32(v[par][0][:, :, cols]),
                                       ALU.subtract).then_inc(S["v_tail"], 1)

            def prep(b, par):
                tail_of(pool, S, b, ch, cx[:], "c")
                tail_of(pool, S, b, xq, xn[:], "xq")
                values(b, par)
                tail_of(pool, S, b, kn, kn_f[par][:], "kn")

            def body(b, par, first, last):
                if not first:
                    variance(b - 1)
                if not last:
                    prep(b + 1, 1 - par)
            pool.memset(edge[:, 0, :, 0:1], 1.0).then_inc(S["edge_set"], 1)
            pool.memset(edge[:, 0, :, 1:2], 0.0).then_inc(S["edge_set"], 1)
            pool.memset(edge[:, 1], 0.0).then_inc(S["edge_set"], 1)
            pool.wait_ge(S["edge_set"], 3)
            for i in range(2):
                for k in range(2):
                    pool.tensor_copy(v[i][k][:, :, 2 * P:VW], edge[:, k]).then_inc(S["edge_done"], 1)
            values(0, 0)
            paired(pool, body, NB)
            pool.wait_ge(S["u_done"], NB - 1)
            lora_scale_b(pool, env, lora)
            variance(NB - 1, 6)
            lora_tail_a(pool, lora)

        @block.tensor
        def _(pe):
            ALL = slice(None)

            def turn(out, src):
                for i in range(NT):
                    mm = pe.transpose(out[:, i // 4, (i % 4) * P:(i % 4 + 1) * P], src(i), ident[:])
                return mm

            def scores(t):
                for h in range(2):
                    mm = three_pass(pe, work_ps[t % 2][:, h], pair(qp, ALL, slice(t * P, (t + 1) * P)),
                                    pair(kp, ALL, slice(512 * h, 512 * h + 512)))
                mm.then_inc(S["s_mm"], 1)

            def turn_scores(b, t):
                wait(pe, S["p_exp"], 8 * b + t + 1)
                turn(turn_ps, lambda i: p[:, t % 2, i * P:(i + 1) * P]).then_inc(S["p_turned"], 1)

            def weigh(b, t, par, tiles=range(NT)):
                if tiles[0] == 0:
                    wait(pe, S["pt_tail"], 8 * b + t + 1)
                    wait(pe, S["pv_out"], 8 * b + t - 1)
                for i in tiles:
                    mm = three_pass(pe, acc_ps[:, t % 2, 0:VW], pair(pt[t % 2], ALL, i), pair(v[par], ALL, i),
                                    first=i == 0, last=i == NT - 1)
                if tiles[-1] == NT - 1:
                    mm.then_inc(S["pv_mm"], 1)

            def turn_mean(b):
                wait(pe, S["pv_out"], 8 * b + 8)
                turn(work_ps[1], lambda i: mean_sq[:, 0, i, :]).then_inc(S["mean_turned"], 1)

            def turn_std(b):
                wait(pe, S["root"], b + 1)
                turn(work_ps[0], lambda i: std[:, i * P:(i + 1) * P]).then_inc(S["std_turned"], 1)

            def open_scores(b):
                wait(pe, S["q_tail"], b + 1)
                wait(pe, S["k_tail"], b + 1)
                scores(0)
                scores(1)

            def body(b, par, first, last):
                for t in range(NT):
                    if t + 2 < NT:
                        wait(pe, S["p_exp"], 8 * b + t + 1)
                        if t == 1 and not first:
                            wait(pe, S["x_mean"], b)
                        if t == 3 and not last:
                            wait(pe, S["sp_done"], b + 2)
                        if t == 4 and not first:
                            wait(pe, S["u_done"], b)
                        scores(t + 2)
                    if t == 2 or t == 3:
                        wait(pe, S["p_exp"], 8 * b + t + 2)
                    if t == 2 and not last:
                        wait(pe, S["c_tail"], b + 2)
                        project_values(pe, env, work_ps[1], ch, S["sp_mm"])
                    if t == 3 and not first:
                        turn_std(b - 1)
                    if t + 1 < NT:
                        wait(pe, S["pt_tail"], 8 * b + t + 1)
                        turn_scores(b, t + 1)
                    if t == 0 and not first:
                        wait(pe, S["p_exp"], 8 * b + 2)
                        turn_mean(b - 1)
                    if t == 5 and not last:
                        wait(pe, S["p_exp"], 8 * b + 7)
                        wait(pe, S["xq_tail"], b + 2)
                        project(pe, env, 0, work_ps[0], xq, S["q_mm"])
                    if t == 6 and not last:
                        wait(pe, S["p_exp"], 8 * b + 8)
                        wait(pe, S["kn_tail"], b + 2)
                        project(pe, env, 1, work_ps[1], kn, S["k_mm"])
                    if t == 0:
                        wait(pe, S["v_tail"], 2 * b + 2)
                        if first:
                            wait(pe, S["edge_done"], 4)
                    if t == 7 and not last:
                        open_scores(b + 1)
                        weigh(b, t, par, range(NT // 2 + 1))
                        wait(pe, S["pt_tail"], 8 * b + 8)
                        turn_scores(b + 1, 0)
                        weigh(b, t, par, range(NT // 2 + 1, NT))
                    else:
                        weigh(b, t, par)
            open_scores(0)
            turn_scores(0, 0)
            paired(pe, body, NB)
            turn_mean(NB - 1)
            pe.wait_ge(S["pt_tail"], 8 * NB)
            lora_turn_b(pe, lora, [turn_ps], ident)
            turn_std(NB - 1)
            pe.wait_ge(lora["S"]["a_tail"], 1)
            pe.wait_ge(lora["S"]["b_tail"], 1)
            pe.wait_ge(S["x_mean"], NB)
            lora_products(pe, env, lora, 1)
            pe.wait_ge(S["u_done"], NB)
            lora_products(pe, env, lora, 0)

        @block.scalar
        def _(act):
            def head(b, t, src, name, last_read):
                wait(act, *last_read)
                act.activation(t[0][:], src, ACT.Copy).then_inc(S[name + "_head"], 1)

            def head_c(b):
                wait_ctx(act, b)
                head(b, ch, cx[:], "c", (S["sp_mm"], b))

            def head_xq(b):
                wait(act, S["xn_done"], b + 1)
                head(b, xq, xn[:], "xq", (S["q_mm"], b))

            def head_kn(b, par):
                wait(act, S["knf_done"], b + 1)
                head(b, kn, kn_f[par][:], "kn", (S["k_mm"], b))

            def head_v(b, par, k):
                wait(act, S["sp_done" if k == 0 else "sq_done"], b + 1)
                act.activation(v[par][0][:, :, k * P:(k + 1) * P], (sp32, sq32)[k][:], ACT.Copy).then_inc(
                    S["v_head"], 1)

            def head_proj(b, n, slot=None):
                t, name = ((qp, "q"), (kp, "k"))[n]
                wait(act, S[name + "_mm"], b + 1)
                wait(act, S["s_mm"], 8 * b)
                act.activation(t[0][:], flat((slot or work_ps[n])[:]), ACT.Identity, bias=bq_bk[:, n:n + 1]).then_inc(
                    S[name + "_head"], 1)

            def exp(b, t):
                wait(act, S["s_max"], 8 * b + t + 1)
                wait(act, S["p_turned"], 8 * b + t - 1)
                act.activation(p[:, t % 2], flat(work_ps[t % 2][:]), ACT.Exp, bias=smax[:, t:t + 1]).then_inc(
                    S["p_exp"], 1)

            def head_scores(b, t):
                wait(act, S["p_turned"], 8 * b + t + 1)
                wait(act, S["pv_mm"], 8 * b + t - 1)
                act.activation(pt[t % 2][0][:].rearrange("p t n -> p (t n)"), flat(turn_ps[:]), ACT.Copy).then_inc(
                    S["pt_head"], 1)

            def root(b):
                wait(act, S["floor"], b + 1)
                act.activation(std[:], std[:], ACT.Sqrt).then_inc(S["root"], 1)
                wait(act, S["warmed"], b + 1)
                act.activation(env["warm"][:], ident[:, 0:1], ACT.Exp).then_inc(S["warmed"], 1)

            def open_scores(b):
                exp(b, 0)
                exp(b, 1)
                head_scores(b, 0)

            def body(b, par, first, last):
                for t in range(NT):
                    if t + 1 < NT:
                        head_scores(b, t + 1)
                    if t + 2 < NT:
                        exp(b, t + 2)
                    if not last:
                        if t == 0:
                            head_c(b + 1)
                        if t == 1:
                            head_xq(b + 1)
                        if t == 3:
                            head_v(b + 1, 1 - par, 0)
                        if t == 4:
                            head_v(b + 1, 1 - par, 1)
                            head_kn(b + 1, 1 - par)
                        if t == 5:
                            head_proj(b + 1, 0)
                        if t == 6:
                            head_proj(b + 1, 1)
                        if t == 7:
                            open_scores(b + 1)
                    if t == 1 and not first:
                        root(b - 1)
            head_proj(0, 0)
            wait(act, S["var_eps"], 2)
            act.activation(sc[:, 4:6, :], sc[:, 2:4, :], ACT.Sqrt).then_inc(S["sc_root"], 1)
            head_proj(0, 1, turn_ps)
            act.activation(env["warm"][:], ident[:, 0:1], ACT.Exp).then_inc(S["warmed"], 1)
            head_v(0, 0, 0)
            exp(0, 0)
            head_v(0, 0, 1)
            exp(0, 1)
            head_scores(0, 0)
            paired(act, body, NB)
            lora_head_a(act, lora)
            lora_head_b(act, lora, [turn_ps])
            root(NB - 1)

        @block.vector
        def _(dve):
            def norm_x(b):
                wait(dve, S["xq_tail"], b)
                dve.tensor_scalar(xn[:], X[:, b, :], mv[:, b, 0:1], sc[:, 0, bass.ds(b, 1)],
                                  ALU.subtract, ALU.mult).then_inc(S["xn_done"], 1)

            def norm_ctx(b, par):
                wait_ctx(dve, b)
                wait(dve, S["kn_tail"], b - 1)
                dve.tensor_scalar(kn_f[par][:], cx[:], cmv[:, b, 0:1], sc[:, 1, bass.ds(b, 1)],
                                  ALU.subtract, ALU.mult).then_inc(S["knf_done"], 1)

            def tail_proj(b, n, slot=None):
                t, name = ((qp, "q"), (kp, "k"))[n]
                wait(dve, S[name + "_head"], b + 1)
                dve.scalar_tensor_tensor(t[1][:], flat((slot or work_ps[n])[:]), bq_bk[:, n:n + 1], f32(t[0][:]),
                                         ALU.add, ALU.subtract).then_inc(S[name + "_tail"], 1)

            def add_value_bias(b, slot):
                wait(dve, S["sp_mm"], b + 1)
                wait(dve, S["v_tail"], 2 * b)
                dve.tensor_tensor(sp32[:], slot[:].rearrange("p a (t n) -> p (a t) n", n=P),
                                  bs_row[:].unsqueeze(1).broadcast_to([P, NT, P]), ALU.add).then_inc(S["sp_done"], 1)

            def max_scores(b, t):
                wait(dve, S["s_mm"], 8 * b + t + 1)
                wait(dve, S["p_exp"], 8 * b + t - 7)
                dve.tensor_reduce(smax[:, t:t + 1], work_ps[t % 2][:], mybir.AxisListType.XY, ALU.max,
                                  negate=True).then_inc(S["s_max"], 1)

            def tail_scores(b, t):
                wait(dve, S["pt_head"], 8 * b + t + 1)
                dve.tensor_tensor(pt[t % 2][1][:].rearrange("p t n -> p (t n)"), flat(turn_ps[:]),
                                  f32(pt[t % 2][0][:]).rearrange("p t n -> p (t n)"), ALU.subtract).then_inc(
                    S["pt_tail"], 1)

            def divide(b, t):
                wait(dve, S["pv_mm"], 8 * b + t + 1)
                dve.reciprocal(rcp[:, t:t + 1], acc_ps[:, t % 2, 2 * P:2 * P + 1]).then_inc(S["pv_rec"], 1)
                wait(dve, S["pv_rec"], 8 * b + t + 1)
                wait(dve, S["mean_turned"], b)
                wait(dve, S["var"], b)
                dve.tensor_scalar(mean_sq[:, :, t, :], acc_ps[:, t % 2, 0:2 * P].rearrange("p (k n) -> p k n", k=2),
                                  rcp[:, t:t + 1], None, ALU.mult).then_inc(S["pv_out"], 1)

            def add_mean(b):
                wait(dve, S["mean_turned"], b + 1)
                wait(dve, S["xn_done"], b + 1)
                dve.scalar_tensor_tensor(X[:, b, :], flat(work_ps[1][:]), gate, X[:, b, :], ALU.mult, ALU.add).then_inc(
                    S["x_mean"], 1)

            def floor(b):
                wait(dve, S["var"], b + 1)
                dve.tensor_scalar(std[:], std[:], 0.0, None, ALU.max).then_inc(S["floor"], 1)

            def modulate(b, par):
                wait(dve, S["std_turned"], b + 1)
                dve.tensor_tensor(u[:], flat(work_ps[0][:]), kn_f[par][:], ALU.mult).then_inc(S["u_done"], 1)

            def add_std(b):
                wait(dve, S["u_done"], b + 1)
                wait(dve, S["x_mean"], b + 1)
                dve.scalar_tensor_tensor(X[:, b, :], u[:], gate, X[:, b, :], ALU.mult, ALU.add).then_inc(S["x_new"], 1)

            def body(b, par, first, last):
                for t in range(NT):
                    if t + 2 < NT:
                        max_scores(b, t + 2)
                    if not first and t == 0:
                        add_mean(b - 1)
                    if not last and t == 2:
                        add_value_bias(b + 1, work_ps[1])
                    if not first and t == 3:
                        modulate(b - 1, 1 - par)
                    if not last and t == 6:
                        tail_proj(b + 1, 1)
                    if t + 1 < NT:
                        tail_scores(b, t + 1)
                    if not last and t == 5:
                        tail_proj(b + 1, 0)
                    if t == 7:
                        if not last:
                            max_scores(b + 1, 0)
                            max_scores(b + 1, 1)
                        if not first:
                            updated_stats(dve, env, b - 1, S, mv_next)
                        if not last:
                            tail_scores(b + 1, 0)
                    divide(b, t)
                    if not last and t == 0:
                        norm_x(b + 1)
                    if not first and t == 1:
                        floor(b - 1)
                    if not last and t == 3:
                        norm_ctx(b + 1, 1 - par)
                    if not first and t == 4:
                        add_std(b - 1)
            query_variances(dve, sc[:, 2, :], mv[:, :, 1]).then_inc(S["var_eps"], 1)
            dve.tensor_scalar(sc[:, 3, :], cmv[:, :, 1], LN_EPS, None, ALU.add).then_inc(S["var_eps"], 1)
            tail_proj(0, 0)
            tail_proj(0, 1, turn_ps)
            add_value_bias(0, acc_ps)
            max_scores(0, 0)
            max_scores(0, 1)
            tail_scores(0, 0)
            dve.wait_ge(S["sc_root"], 1)
            dve.reciprocal(sc[:, 0:2, :], sc[:, 4:6, :]).then_inc(S["sc_done"], 1)
            dve.wait_ge(S["sc_done"], 1)
            norm_ctx(0, 0)
            paired(dve, body, NB)
            dve.wait_ge(S["pv_out"], 8 * NB)
            ends = slice(6, NT)
            mean, sq, v_end = flat(mean_sq[:, 0, ends]), flat(mean_sq[:, 1, ends]), std[:, 6 * P:NT * P]
            dve.tensor_tensor(v_end, mean, mean, ALU.mult).then_inc(S["end_mean2"], 1)
            dve.wait_ge(S["end_mean2"], 1)
            dve.tensor_tensor(v_end, sq, v_end, ALU.subtract).then_inc(S["end_var"], 1)
            dve.wait_ge(S["end_var"], 1)
            floor(NB - 1)
            add_mean(NB - 1)
            lora_tail_b(dve, lora, [turn_ps])
            modulate(NB - 1, 1)
            add_std(NB - 1)
            updated_stats(dve, env, NB - 1, S, mv_next)


def flamingo_gated_kernel(nc, out, **dram):
    NB, ROWS, N = dram["x"].shape
    assert ROWS == P and N == 1024
    with ExitStack() as ctx:
        sb = lambda n, s: ctx.enter_context(nc.sbuf_tensor(n, s, F32))
        env = dict(dram)
        env.update(x_dram=dram["x"], ctx_dram=dram["ctx_4096"], out=out)
        env["X"] = sb("X", [P, NB, N])
        env["ident"] = sb("ident", [P, P])
        env["tg"] = sb("tg", [P, 8])
        env["st"] = sb("st", [P, 3, NB])
        env["stats"] = sb("stats", [P, 12])
        env["warm"] = sb("warm", [P, 1])
        env["pair"] = sb("pair", [P, 4])
        env["mv"], env["mv2"], env["cmv"] = (sb(n, [P, NB, 2]) for n in ("mv", "mv2", "cmv"))
        env["work_ps"] = [ctx.enter_context(nc.psum_tensor(f"work{i}", [P, 2, 512], F32)) for i in range(2)]
        env["turn_ps"] = ctx.enter_context(nc.psum_tensor("turn", [P, 2, 512], F32))
        env["acc_ps"] = ctx.enter_context(nc.psum_tensor("acc", [P, 2, 512], F32))
        env["w_rows"] = sb("w_rows", [P, N // P, N])
        env["stage"] = [over(nc, f"stage{i}", [P, N], F32 if i < 2 else F32R, nc.sbuf_base - 4 * N * (N // P - i))
                        for i in range(8)]
        env["lora_b"], env["lora_a"] = sb("lora_b", [P, 2, N]), sb("lora_a", [P, 2, N])
        env["lora_b_head"] = over(nc, "lora_b_head", [P, 2, N], F32R, nc.sbuf_base - 16 * N)
        env["lora_a_tail"] = over(nc, "lora_a_tail", [P, 2, N], F32R, nc.sbuf_base - 8 * N)
        env["fac"] = [sb(f"fac{i}", [P, 2, dram[f"L{i}_ffn_" + n].shape[0]]) for i, n in enumerate(("A", "lora_A"))]
        env["lora_loaded"] = [ctx.enter_context(nc.semaphore(f"lora_loaded{i}")) for i in range(2)]
        env["lora_sem"] = lambda n: ctx.enter_context(nc.semaphore(n))
        env["w_loaded"] = [ctx.enter_context(nc.semaphore(f"w_loaded{i}")) for i in range(2)]
        env["x_raw"], env["bq_bk"], env["bs_row"] = sb("x_raw", [P, 3, P]), sb("bq_bk", [P, 2]), sb("bs_row", [P, P])
        env["x_wts"] = [ctx.enter_context(nc.sbuf_tensor(f"x_wts_{n}", [P, 3, P], F32R)) for n in "hl"]
        env["x_small_loaded"] = ctx.enter_context(nc.semaphore("x_small_loaded"))
        env["ctx_ahead"] = ctx.enter_context(nc.semaphore("ctx_ahead"))
        env["first_sems"] = []
        xattn0(nc, ctx, env)
        nc.all_engine_barrier()
        nc.clear_and_free_semaphores(env["first_sems"])
        nc.all_engine_barrier()
        names = ("end_mean2 end_var edge_set edge_done ahead_var ahead_root ahead_scale ahead_kn var_eps "
                 "sc_root sc_done ctx_loaded c_head c_tail xn_done xq_head xq_tail knf_done kn_head kn_tail "
                 "q_mm q_head q_tail k_mm k_head k_tail sp_mm sp_done sq_done v_head v_tail s_mm s_max p_exp "
                 "p_turned pt_head pt_tail pv_mm pv_rec pv_out mean2 var floor root mean_turned std_turned "
                 "x_mean u_done warmed x_new row_stats row_aggr row_kept pair_clear")
        env["attention_sems"] = {n: ctx.enter_context(nc.semaphore("x_" + n)) for n in names.split()}
        ffn(nc, ctx, env, 0)
        xattn1(nc, ctx, env)
        ffn(nc, ctx, env, 1)


_INS = ['x', 'ctx_4096', 'g_xattn', 'g_ffn', 'L0_xattn_Wq', 'L0_xattn_Wk', 'L0_xattn_Wv', 'L0_xattn_Wo',
        'L0_xattn_bo', 'L0_xattn_g', 'L0_ffn_W', 'L0_ffn_bias', 'L0_ffn_A', 'L0_ffn_Bf', 'L0_ffn_coeffs',
        'L0_ffn_scales', 'L1_xattn_Wq', 'L1_xattn_bq', 'L1_xattn_Wk', 'L1_xattn_bk', 'L1_xattn_Ws',
        'L1_xattn_bs_', 'L1_ffn_lora_A', 'L1_ffn_lora_B', 'L1_ffn_W', 'L1_ffn_bias', 'L1_ffn_lora_weights']
_OUT = (16, 128, 1024)


def kernel(**inputs):
    import numpy as _np
    import concourse.bacc as _bacc
    from concourse import mybir as _mybir
    from concourse.bass_utils import run_bass_kernel_spmd as _run

    nc = _bacc.Bacc("TRN2", target_bir_lowering=False, num_devices=1)
    arrays, dram = {}, {}
    for name in _INS:
        a = _np.ascontiguousarray(inputs[name])
        arrays[f"in_{name}"] = a
        dram[name] = nc.dram_tensor(f"in_{name}", a.shape, _mybir.dt.from_np(a.dtype), kind="ExternalInput").ap()
    out = nc.dram_tensor("out_0", _OUT, _mybir.dt.float32, kind="ExternalOutput").ap()
    flamingo_gated_kernel(nc, out, **dram)
    r = _run(nc, [arrays], core_ids=[0])
    return r.results[0]["out_0"]
```
